# Optimizing a Trainium2 kernel written in Bass

```python
import numpy as np
import jax
import jax.numpy as jnp

def _softmax(x, axis=-1):
    return jax.nn.softmax(x, axis=axis)
def _gelu(x):
    return jax.nn.gelu(x, approximate=True)
def _silu(x):
    return jax.nn.silu(x)
def _sigmoid(x):
    return jax.nn.sigmoid(x)
def _layernorm(x, axis=-1, eps=1e-5):
    m = jnp.mean(x, axis=axis, keepdims=True)
    v = jnp.var(x, axis=axis, keepdims=True)
    return (x - m) / jnp.sqrt(v + eps)
def _scatter_add(tgt, idx, src, axis=0):
    return tgt.at[idx].add(src)
def _segment_sum(src, seg, n):
    return jax.ops.segment_sum(src, seg, n)

kernel_name = 'mk_conv_preact_d4_conv_nchw128_4a3cc7'

def setup_inputs(seed: int = 0):
    np.random.seed(seed)
    _w = jnp.asarray
    def _rec_inputs():
        import jax
        import jax.numpy as jnp
        _gk = jax.random.key(seed)
        x = -0.0002928 + 1 * jax.random.normal(jax.random.fold_in(_gk, 1), (8, 128, 64, 64), jnp.float32)
        return x
    x = _rec_inputs()
    def _L0_conv_setup():
        import jax, jax.numpy as jnp
        import numpy as np
        B, CIN, H, W = (8, 128, 64, 64)
        GC = 64
        D = 64
        DI = 128
        N = 16
        R = 4
        K = 3

        def _ln(x, g, b, eps=1e-05):
            m = x.mean(-1, keepdims=True)
            v = x.var(-1, keepdims=True)
            return (x - m) * jax.lax.rsqrt(v + eps) * g + b
        key = jax.random.key(seed)
        ks = jax.random.split(key, 12)

        def nrm(k, shape, s=0.02):
            return jax.random.normal(k, shape, jnp.float32) * s
        return {'x': jax.random.normal(ks[0], (B, CIN, H, W), jnp.float32), 'conv_w': nrm(ks[1], (GC, GC, 3, 3), 0.05), 'conv_b': jnp.zeros((GC,), jnp.float32), 'expand_w': nrm(ks[2], (D, 2 * D)), 'concat_w': nrm(ks[3], (2 * D, D)), 'concat_b': jnp.zeros((D,), jnp.float32), 'ln_g': jnp.ones((D,), jnp.float32), 'ln_b': jnp.zeros((D,), jnp.float32), 'in_w': nrm(ks[4], (D, 2 * DI)), 'in_b': jnp.zeros((2 * DI,), jnp.float32), 'conv1d_w': nrm(ks[5], (K, DI), 0.1), 'conv1d_b': jnp.zeros((DI,), jnp.float32), 'xproj_w': nrm(ks[6], (DI, R + 2 * N)), 'dt_w': nrm(ks[7], (R, DI), 0.1), 'dt_b': jnp.full((DI,), -4.0, jnp.float32), 'A_log': jnp.log(jnp.broadcast_to(jnp.arange(1, N + 1, dtype=jnp.float32), (DI, N)) + 0.0), 'D_ssm': jnp.ones((DI,), jnp.float32), 'out_w': nrm(ks[8], (DI, D)), 'out_b': jnp.zeros((D,), jnp.float32)}
    _L0_conv_all = _L0_conv_setup()
    _L0_conv_in = {k: v for k, v in _L0_conv_all.items() if k in ('conv_w', 'conv_b', 'expand_w', 'concat_w', 'concat_b', 'ln_g', 'ln_b', 'in_w', 'in_b', 'conv1d_w', 'conv1d_b', 'xproj_w', 'dt_w', 'dt_b', 'A_log', 'D_ssm', 'out_w', 'out_b', )}
    del _L0_conv_all

    def _L1_conv_setup():
        import jax, jax.numpy as jnp
        import numpy as np
        K = 9
        PAD = K // 2

        def _conv1d(x, w):
            return jax.lax.conv_general_dilated(x, w, window_strides=(1,), padding=((PAD, PAD),), dimension_numbers=('NCH', 'OIH', 'NCH'))

        def _propagate(x, w, axis, reverse):
            xm = jnp.moveaxis(x, axis, 0)
            if reverse:
                xm = xm[::-1]

            def step(prev, cur):
                new = cur + jax.nn.relu(_conv1d(prev, w))
                return (new, new)
            _, outs = jax.lax.scan(step, xm[0], xm[1:])
            res = jnp.concatenate([xm[:1], outs], axis=0)
            if reverse:
                res = res[::-1]
            return jnp.moveaxis(res, 0, axis)
        key = jax.random.key(seed)
        ks = jax.random.split(key, 5)
        B, C, H, W = (16, 128, 72, 200)
        scale = 1.0 / np.sqrt(C * K)
        x = jax.random.normal(ks[0], (B, C, H, W), dtype=jnp.float32)
        w_down = jax.random.normal(ks[1], (C, C, K), dtype=jnp.float32) * scale
        w_up = jax.random.normal(ks[2], (C, C, K), dtype=jnp.float32) * scale
        w_right = jax.random.normal(ks[3], (C, C, K), dtype=jnp.float32) * scale
        w_left = jax.random.normal(ks[4], (C, C, K), dtype=jnp.float32) * scale
        return {'x': x, 'w_down': w_down, 'w_up': w_up, 'w_right': w_right, 'w_left': w_left}
    _L1_conv_all = _L1_conv_setup()
    _L1_conv_in = {k: v for k, v in _L1_conv_all.items() if k in ('w_down', 'w_up', 'w_right', 'w_left', )}
    del _L1_conv_all

    def _L2_conv_setup():
        import jax, jax.numpy as jnp
        import numpy as np
        N, C, H, W, G = (32, 128, 56, 56, 8)

        def _unfold_w3_dil2(x):
            n, c, h, w = x.shape
            xp = jnp.pad(x, ((0, 0), (0, 0), (0, 0), (2, 2)))
            return jnp.stack([xp[..., 0:w], xp[..., 2:w + 2], xp[..., 4:w + 4]], axis=2)
        key = jax.random.key(seed)
        k1, k2, k3, k4 = jax.random.split(key, 4)
        x = jax.random.normal(k1, (N, C, H, W), dtype=jnp.float32)
        w1 = jax.random.normal(k2, (C, C, 5, 1), dtype=jnp.float32) * 0.05
        w3 = jax.random.normal(k3, (C, 1, 3, 1), dtype=jnp.float32) * 0.1
        w4 = jax.random.normal(k4, (C, 3, 1, G), dtype=jnp.float32) * 0.05
        return {'x': x, 'w1': w1, 'w3': w3, 'w4': w4}
    _L2_conv_all = _L2_conv_setup()
    _L2_conv_in = {k: v for k, v in _L2_conv_all.items() if k in ('w1', 'w3', 'w4', )}
    del _L2_conv_all

    def _L3_conv_setup():
        import jax, jax.numpy as jnp
        from jax import lax
        import numpy as np
        CIN, COUT, K, STRIDE, PAD = (128, 128, 3, 1, 1)
        KK = K * K

        def _dcn_forward(x, offset_w, offset_b, dcn_w, dcn_b, gamma, beta):
            B, C, H, W = x.shape
            om = lax.conv_general_dilated(x, offset_w, (STRIDE, STRIDE), ((PAD, PAD), (PAD, PAD)), dimension_numbers=('NCHW', 'OIHW', 'NCHW')) + offset_b[None, :, None, None]
            o1, o2, m = jnp.split(om, 3, axis=1)
            offset = jnp.concatenate([o1, o2], axis=1)
            mask = jax.nn.sigmoid(m)
            Ho, Wo = (om.shape[2], om.shape[3])
            dy = offset[:, 0::2]
            dx = offset[:, 1::2]
            ki, kj = jnp.meshgrid(jnp.arange(K), jnp.arange(K), indexing='ij')
            base_y = (jnp.arange(Ho) * STRIDE - PAD)[None, :, None] + ki.reshape(KK, 1, 1)
            base_x = (jnp.arange(Wo) * STRIDE - PAD)[None, None, :] + kj.reshape(KK, 1, 1)
            py = dy + base_y[None].astype(dy.dtype)
            px = dx + base_x[None].astype(dx.dtype)
            y0f = jnp.floor(py)
            x0f = jnp.floor(px)
            wy1 = py - y0f
            wx1 = px - x0f
            y0 = y0f.astype(jnp.int32)
            x0 = x0f.astype(jnp.int32)
            xf = x.reshape(B, C, H * W)

            def corner(yi, xi, wgt):
                valid = (yi >= 0) & (yi < H) & (xi >= 0) & (xi < W)
                idx = jnp.clip(yi, 0, H - 1) * W + jnp.clip(xi, 0, W - 1)
                g = jax.vmap(lambda xb, ib: xb[:, ib])(xf, idx)
                return g * (wgt * valid)[:, None]
            samp = corner(y0, x0, (1 - wy1) * (1 - wx1)) + corner(y0, x0 + 1, (1 - wy1) * wx1) + corner(y0 + 1, x0, wy1 * (1 - wx1)) + corner(y0 + 1, x0 + 1, wy1 * wx1)
            samp = samp * mask[:, None]
            out = jnp.einsum('bckhw,ock->bohw', samp, dcn_w.reshape(COUT, C, KK))
            out = out + dcn_b[None, :, None, None]
            mu = out.mean(axis=(0, 2, 3), keepdims=True)
            var = out.var(axis=(0, 2, 3), keepdims=True)
            out = (out - mu) * lax.rsqrt(var + 1e-05)
            out = out * gamma[None, :, None, None] + beta[None, :, None, None]
            return jnp.where(out >= 0, out, 0.1 * out)
        key = jax.random.key(seed)
        ks = jax.random.split(key, 5)
        x = jax.random.normal(ks[0], (4, CIN, 96, 96), dtype=jnp.float32)
        offset_w = jax.random.normal(ks[1], (3 * KK, CIN, K, K), dtype=jnp.float32) * 0.01
        offset_b = jnp.zeros((3 * KK,), dtype=jnp.float32)
        fan_in = CIN * KK
        dcn_w = jax.random.normal(ks[2], (COUT, CIN, K, K), dtype=jnp.float32) / np.sqrt(fan_in)
        dcn_b = jax.random.normal(ks[3], (COUT,), dtype=jnp.float32) * 0.01
        gamma = jnp.ones((COUT,), dtype=jnp.float32)
        beta = jnp.zeros((COUT,), dtype=jnp.float32)
        return {'x': x, 'offset_w': offset_w, 'offset_b': offset_b, 'dcn_w': dcn_w, 'dcn_b': dcn_b, 'gamma': gamma, 'beta': beta}
    _L3_conv_all = _L3_conv_setup()
    _L3_conv_in = {k: v for k, v in _L3_conv_all.items() if k in ('offset_w', 'offset_b', 'dcn_w', 'dcn_b', 'gamma', 'beta', )}
    del _L3_conv_all

    return {
        "x": x,
        "L0_conv_conv_w": _L0_conv_in["conv_w"],
        "L0_conv_conv_b": _L0_conv_in["conv_b"],
        "L0_conv_expand_w": _L0_conv_in["expand_w"],
        "L0_conv_concat_w": _L0_conv_in["concat_w"],
        "L0_conv_concat_b": _L0_conv_in["concat_b"],
        "L0_conv_ln_g": _L0_conv_in["ln_g"],
        "L0_conv_ln_b": _L0_conv_in["ln_b"],
        "L0_conv_in_w": _L0_conv_in["in_w"],
        "L0_conv_in_b": _L0_conv_in["in_b"],
        "L0_conv_conv1d_w": _L0_conv_in["conv1d_w"],
        "L0_conv_conv1d_b": _L0_conv_in["conv1d_b"],
        "L0_conv_xproj_w": _L0_conv_in["xproj_w"],
        "L0_conv_dt_w": _L0_conv_in["dt_w"],
        "L0_conv_dt_b": _L0_conv_in["dt_b"],
        "L0_conv_A_log": _L0_conv_in["A_log"],
        "L0_conv_D_ssm": _L0_conv_in["D_ssm"],
        "L0_conv_out_w": _L0_conv_in["out_w"],
        "L0_conv_out_b": _L0_conv_in["out_b"],
        "L1_conv_w_down": _L1_conv_in["w_down"],
        "L1_conv_w_up": _L1_conv_in["w_up"],
        "L1_conv_w_right": _L1_conv_in["w_right"],
        "L1_conv_w_left": _L1_conv_in["w_left"],
        "L2_conv_w1": _L2_conv_in["w1"],
        "L2_conv_w3": _L2_conv_in["w3"],
        "L2_conv_w4": _L2_conv_in["w4"],
        "L3_conv_offset_w": _L3_conv_in["offset_w"],
        "L3_conv_offset_b": _L3_conv_in["offset_b"],
        "L3_conv_dcn_w": _L3_conv_in["dcn_w"],
        "L3_conv_dcn_b": _L3_conv_in["dcn_b"],
        "L3_conv_gamma": _L3_conv_in["gamma"],
        "L3_conv_beta": _L3_conv_in["beta"],
    }

def reference(x, L0_conv_conv_w, L0_conv_conv_b, L0_conv_expand_w, L0_conv_concat_w, L0_conv_concat_b, L0_conv_ln_g, L0_conv_ln_b, L0_conv_in_w, L0_conv_in_b, L0_conv_conv1d_w, L0_conv_conv1d_b, L0_conv_xproj_w, L0_conv_dt_w, L0_conv_dt_b, L0_conv_A_log, L0_conv_D_ssm, L0_conv_out_w, L0_conv_out_b, L1_conv_w_down, L1_conv_w_up, L1_conv_w_right, L1_conv_w_left, L2_conv_w1, L2_conv_w3, L2_conv_w4, L3_conv_offset_w, L3_conv_offset_b, L3_conv_dcn_w, L3_conv_dcn_b, L3_conv_gamma, L3_conv_beta):
    import jax
    import jax.numpy as jnp
    def _L0_conv_ref(x, conv_w, conv_b, expand_w, concat_w, concat_b, ln_g, ln_b, in_w, in_b, conv1d_w, conv1d_b, xproj_w, dt_w, dt_b, A_log, D_ssm, out_w, out_b):
        import jax, jax.numpy as jnp
        import numpy as np
        B, CIN, H, W = (8, 128, 64, 64)
        GC = 64
        D = 64
        DI = 128
        N = 16
        R = 4
        K = 3

        def _ln(x, g, b, eps=1e-05):
            m = x.mean(-1, keepdims=True)
            v = x.var(-1, keepdims=True)
            return (x - m) * jax.lax.rsqrt(v + eps) * g + b
        x_id, x_hw = (x[:, :GC], x[:, GC:])
        t = x_id.transpose(0, 2, 3, 1)
        t = t @ expand_w
        t = t @ concat_w + concat_b
        tn = _ln(t, ln_g, ln_b)
        xz = tn @ in_w + in_b
        xs, z = (xz[..., :DI], xz[..., DI:])
        L = H * W
        xs = xs.reshape(B, L, DI)
        z = z.reshape(B, L, DI)
        xp = jnp.pad(xs, ((0, 0), (K - 1, 0), (0, 0)))
        xc = conv1d_b + sum([xp[:, k:k + L, :] * conv1d_w[k] for k in range(K)])
        xc = jax.nn.silu(xc)
        dbc = xc @ xproj_w
        dt = jax.nn.softplus(dbc[..., :R] @ dt_w + dt_b)
        Bm = dbc[..., R:R + N]
        Cm = dbc[..., R + N:]
        A = -jnp.exp(A_log)
        dA = jnp.exp(dt[..., None] * A)
        dBx = dt[..., None] * Bm[:, :, None, :] * xc[..., None]

        def step(h, inp):
            dA_t, dBx_t, C_t = inp
            h = dA_t * h + dBx_t
            return (h, jnp.einsum('bdn,bn->bd', h, C_t))
        h0 = jnp.zeros((B, DI, N), xc.dtype)
        _, ys = jax.lax.scan(step, h0, (dA.swapaxes(0, 1), dBx.swapaxes(0, 1), Cm.swapaxes(0, 1)))
        y = ys.swapaxes(0, 1) + xc * D_ssm
        y = y * jax.nn.silu(z)
        out = (y @ out_w + out_b).reshape(B, H, W, D)
        x_id_out = (t + out).transpose(0, 3, 1, 2)
        hw = jax.lax.conv_general_dilated(x_hw, conv_w, (1, 1), 'SAME', dimension_numbers=('NCHW', 'OIHW', 'NCHW')) + conv_b[None, :, None, None]
        return jax.nn.relu(jnp.concatenate([x_id_out, hw], axis=1))

    def _L1_conv_ref(x, w_down, w_up, w_right, w_left):
        import jax, jax.numpy as jnp
        import numpy as np
        K = 9
        PAD = K // 2

        def _conv1d(x, w):
            return jax.lax.conv_general_dilated(x, w, window_strides=(1,), padding=((PAD, PAD),), dimension_numbers=('NCH', 'OIH', 'NCH'))

        def _propagate(x, w, axis, reverse):
            xm = jnp.moveaxis(x, axis, 0)
            if reverse:
                xm = xm[::-1]

            def step(prev, cur):
                new = cur + jax.nn.relu(_conv1d(prev, w))
                return (new, new)
            _, outs = jax.lax.scan(step, xm[0], xm[1:])
            res = jnp.concatenate([xm[:1], outs], axis=0)
            if reverse:
                res = res[::-1]
            return jnp.moveaxis(res, 0, axis)
        x = _propagate(x, w_down, 2, False)
        x = _propagate(x, w_up, 2, True)
        x = _propagate(x, w_right, 3, False)
        x = _propagate(x, w_left, 3, True)
        return x

    def _L2_conv_ref(x, w1, w3, w4):
        import jax, jax.numpy as jnp
        import numpy as np
        N, C, H, W, G = (32, 128, 56, 56, 8)

        def _unfold_w3_dil2(x):
            n, c, h, w = x.shape
            xp = jnp.pad(x, ((0, 0), (0, 0), (0, 0), (2, 2)))
            return jnp.stack([xp[..., 0:w], xp[..., 2:w + 2], xp[..., 4:w + 4]], axis=2)
        n, c, h, w = x.shape
        g = w4.shape[-1]
        t1 = jax.lax.conv_general_dilated(x, w1, window_strides=(1, 1), padding=((2, 2), (0, 0)))
        t3 = jax.lax.conv_general_dilated(t1, w3, window_strides=(1, 1), padding=((1, 1), (0, 0)), feature_group_count=c)
        t2 = _unfold_w3_dil2(x)
        t4 = jnp.einsum('nckhw,ckg->nghw', t2, w4[:, :, 0, :])
        t5 = t4[:, None, :, :, :] * t3.reshape(n, c // g, g, h, w)
        return t5.reshape(n, c, h, w)

    def _L3_conv_ref(x, offset_w, offset_b, dcn_w, dcn_b, gamma, beta):
        import jax, jax.numpy as jnp
        from jax import lax
        import numpy as np
        CIN, COUT, K, STRIDE, PAD = (128, 128, 3, 1, 1)
        KK = K * K

        def _dcn_forward(x, offset_w, offset_b, dcn_w, dcn_b, gamma, beta):
            B, C, H, W = x.shape
            om = lax.conv_general_dilated(x, offset_w, (STRIDE, STRIDE), ((PAD, PAD), (PAD, PAD)), dimension_numbers=('NCHW', 'OIHW', 'NCHW')) + offset_b[None, :, None, None]
            o1, o2, m = jnp.split(om, 3, axis=1)
            offset = jnp.concatenate([o1, o2], axis=1)
            mask = jax.nn.sigmoid(m)
            Ho, Wo = (om.shape[2], om.shape[3])
            dy = offset[:, 0::2]
            dx = offset[:, 1::2]
            ki, kj = jnp.meshgrid(jnp.arange(K), jnp.arange(K), indexing='ij')
            base_y = (jnp.arange(Ho) * STRIDE - PAD)[None, :, None] + ki.reshape(KK, 1, 1)
            base_x = (jnp.arange(Wo) * STRIDE - PAD)[None, None, :] + kj.reshape(KK, 1, 1)
            py = dy + base_y[None].astype(dy.dtype)
            px = dx + base_x[None].astype(dx.dtype)
            y0f = jnp.floor(py)
            x0f = jnp.floor(px)
            wy1 = py - y0f
            wx1 = px - x0f
            y0 = y0f.astype(jnp.int32)
            x0 = x0f.astype(jnp.int32)
            xf = x.reshape(B, C, H * W)

            def corner(yi, xi, wgt):
                valid = (yi >= 0) & (yi < H) & (xi >= 0) & (xi < W)
                idx = jnp.clip(yi, 0, H - 1) * W + jnp.clip(xi, 0, W - 1)
                g = jax.vmap(lambda xb, ib: xb[:, ib])(xf, idx)
                return g * (wgt * valid)[:, None]
            samp = corner(y0, x0, (1 - wy1) * (1 - wx1)) + corner(y0, x0 + 1, (1 - wy1) * wx1) + corner(y0 + 1, x0, wy1 * (1 - wx1)) + corner(y0 + 1, x0 + 1, wy1 * wx1)
            samp = samp * mask[:, None]
            out = jnp.einsum('bckhw,ock->bohw', samp, dcn_w.reshape(COUT, C, KK))
            out = out + dcn_b[None, :, None, None]
            mu = out.mean(axis=(0, 2, 3), keepdims=True)
            var = out.var(axis=(0, 2, 3), keepdims=True)
            out = (out - mu) * lax.rsqrt(var + 1e-05)
            out = out * gamma[None, :, None, None] + beta[None, :, None, None]
            return jnp.where(out >= 0, out, 0.1 * out)
        return _dcn_forward(x, offset_w, offset_b, dcn_w, dcn_b, gamma, beta)

    def _gn(v, G=32, eps=1e-5):
        B_, C_, H_, W_ = v.shape
        g = v.reshape(B_, G, C_ // G, H_, W_)
        m = jnp.mean(g, axis=(2, 3, 4), keepdims=True)
        s = jnp.var(g, axis=(2, 3, 4), keepdims=True)
        return ((g - m) / jnp.sqrt(s + eps)).reshape(v.shape)

    def _ln_c(v, eps=1e-6):
        m = jnp.mean(v, axis=1, keepdims=True)
        s = jnp.var(v, axis=1, keepdims=True)
        return (v - m) / jnp.sqrt(s + eps)

    def _ln_t(v, eps=1e-5):
        m = jnp.mean(v, axis=-1, keepdims=True)
        s = jnp.var(v, axis=-1, keepdims=True)
        return (v - m) / jnp.sqrt(s + eps)

    def _to_tokens(v):
        B_, C_, H_, W_ = v.shape
        return v.reshape(B_, C_, H_ * W_).transpose(0, 2, 1)
    def _from_tokens(t, like):
        B_, C_, H_, W_ = like.shape
        return t.transpose(0, 2, 1).reshape(B_, C_, H_, W_)

    x = x + _L0_conv_ref(_gn(x), L0_conv_conv_w, L0_conv_conv_b, L0_conv_expand_w, L0_conv_concat_w, L0_conv_concat_b, L0_conv_ln_g, L0_conv_ln_b, L0_conv_in_w, L0_conv_in_b, L0_conv_conv1d_w, L0_conv_conv1d_b, L0_conv_xproj_w, L0_conv_dt_w, L0_conv_dt_b, L0_conv_A_log, L0_conv_D_ssm, L0_conv_out_w, L0_conv_out_b)
    x = x + _L1_conv_ref(_gn(x), L1_conv_w_down, L1_conv_w_up, L1_conv_w_right, L1_conv_w_left)
    x = x + _L2_conv_ref(_gn(x), L2_conv_w1, L2_conv_w3, L2_conv_w4)
    x = x + _L3_conv_ref(_gn(x), L3_conv_offset_w, L3_conv_offset_b, L3_conv_dcn_w, L3_conv_dcn_b, L3_conv_gamma, L3_conv_beta)
    return x


_drawn_inputs = setup_inputs


def setup_inputs(seed=0):
    import zlib

    import numpy as np

    out = dict(_drawn_inputs(seed))
    spreads = {'L0_conv_conv_b': (0.0, 0.545),
     'L0_conv_concat_b': (0.0, 0.5),
     'L0_conv_ln_g': (1.0, 0.6),
     'L0_conv_ln_b': (0.0, 0.8),
     'L0_conv_in_b': (0.0, 0.8),
     'L0_conv_conv1d_b': (0.0, 0.8),
     'L0_conv_dt_b': (-4.0, 0.6),
     'L0_conv_D_ssm': (1.0, 0.6),
     'L0_conv_out_b': (0.0, 0.725),
     'L3_conv_offset_b': (0.0, 0.682),
     'L3_conv_gamma': (1.0, 0.6),
     'L3_conv_beta': (0.0, 0.8)}
    factors = {'L0_conv_expand_w': 8.0,
     'L0_conv_concat_w': 8.0,
     'L0_conv_in_w': 8.0,
     'L0_conv_conv1d_w': 8.0,
     'L0_conv_xproj_w': 8.0,
     'L0_conv_dt_w': 8.0,
     'L0_conv_A_log': 8.0,
     'L0_conv_out_w': 8.0,
     'L2_conv_w1': 3.718,
     'L2_conv_w3': 3.627,
     'L2_conv_w4': 2.748,
     'L3_conv_dcn_b': 8.0}
    for name, (base, spread) in spreads.items():
        noise = np.random.default_rng([zlib.crc32(name.encode()), seed]).standard_normal(out[name].shape)
        drawn = base * np.exp(spread * noise) if base else spread * noise
        out[name] = jnp.asarray(drawn.astype(out[name].dtype))
    for name, factor in factors.items():
        out[name] = (out[name] * factor).astype(out[name].dtype)
    return out
```

```python
from contextlib import ExitStack

import concourse.bass as bass
import numpy as np
from concourse import mybir

F32 = mybir.dt.float32
F32R = mybir.dt.float32r
U32 = mybir.dt.uint32
ALU = mybir.AluOpType
ACT = mybir.ActivationFunctionType
AX_X = mybir.AxisListType.X

P = 128
B, H, W = 8, 64, 64
HW = H * W
CH = 512
NCH = HW // CH
ROWS = CH // W
HALF = 64
NS = 16
PADH, PADW = 3, 2
HP, WP = H + 2 * PADH, W + 2 * PADW
TAPS = 9
CREDIT = 32


def after(eng, sem, k, lag=0):
    eng.wait_ge(sem, k + (1 + CREDIT - lag))


def apart(eng, passed):
    eng.sem_inc(passed, 1)


def host_constants():
    ident = np.eye(P, dtype=np.float32)
    group_mean = np.kron(np.eye(P // 4), np.full((4, 4), 0.25)).astype(np.float32)
    mean64 = np.zeros((P, P), np.float32)
    mean64[:HALF, :] = 1.0 / HALF
    centre = np.zeros((P, P), np.float32)
    centre[:HALF, :HALF] = np.eye(HALF) - 1.0 / HALF
    pick = np.zeros((P, 32), np.float32)
    for k in range(64):
        pick[k, k % 32] = 1.0
    small = np.concatenate([ident, group_mean, mean64, centre, pick], axis=1)
    p = np.arange(P)
    base = np.zeros((P, 2, NCH, TAPS, 4), np.float32)
    for t in range(HW // P):
        for k in range(TAPS):
            base[:, 0, t // 4, k, t % 4] = 2 * t + p // W + k // 3
            base[:, 1, t // 4, k, t % 4] = p % W + k % 3
    return small, base.reshape(P, -1)


def group_norm_scales(nc, ctx_outer, G):
    with ExitStack() as ctx:
        def sem(name):
            return ctx.enter_context(nc.semaphore(f"{name}_{G.tag}"))
        tag = G.tag
        mv = ctx.enter_context(nc.sbuf_tensor(f"gn_mv{tag}", [P, B, 2], F32))
        moments = ctx.enter_context(nc.sbuf_tensor(f"gn_moments{tag}", [P, 2, B], F32))
        mean = ctx.enter_context(nc.sbuf_tensor(f"gn_mean{tag}", [P, 2, B], F32))
        var = ctx.enter_context(nc.sbuf_tensor(f"gn_var{tag}", [P, B], F32))
        ps = ctx.enter_context(nc.psum_tensor(f"gn_ps{tag}", [P, 2, B], F32))
        s_step, s_ps, s_std = sem("gn_step"), sem("gn_group_moments"), sem("gn_std")
        with nc.Block() as block:
            @block.vector
            def _(dve):
                for b in range(B):
                    nc.vector.bn_aggr(mv[:, b, :], G.stats[:, b, :, :].rearrange("p c s -> p (c s)")).then_inc(s_step, 1)
                dve.wait_ge(s_step, B)
                nc.vector.tensor_copy(moments[:, 0, :], mv[:, :, 0]).then_inc(s_step, 1)
                nc.vector.tensor_tensor(var[:], mv[:, :, 0], mv[:, :, 0], ALU.mult).then_inc(s_step, 1)
                dve.wait_ge(s_step, B + 2)
                nc.vector.tensor_tensor(moments[:, 1, :], mv[:, :, 1], var[:], ALU.add).then_inc(s_step, 1)
                dve.wait_ge(s_ps, 1)
                nc.vector.tensor_copy(mean[:], ps[:]).then_inc(s_step, 1)
                dve.wait_ge(s_step, B + 4)
                nc.vector.tensor_tensor(var[:], mean[:, 0, :], mean[:, 0, :], ALU.mult).then_inc(s_step, 1)
                dve.wait_ge(s_step, B + 5)
                nc.vector.tensor_tensor(mean[:, 1, :], mean[:, 1, :], var[:], ALU.subtract).then_inc(s_step, 1)
                dve.wait_ge(s_std, 1)
                nc.vector.reciprocal(G.rstd[:], mv[:, :, 0]).then_inc(s_step, 1)
                dve.wait_ge(s_step, B + 7)
                nc.vector.scalar_tensor_tensor(G.shift[:], mean[:, 0, :], -1.0, G.rstd[:], ALU.mult, ALU.mult).then_inc(s_step, 1)
                dve.wait_ge(s_step, B + 8)

            @block.tensor
            def _(pe):
                pe.wait_ge(s_step, B + 3)
                nc.tensor.matmul(ps[:].rearrange("p a b -> p (a b)"), G.group_mean, moments[:].rearrange("p a b -> p (a b)"),
                                 start=True, stop=True).then_inc(s_ps, 1)

            @block.scalar
            def _(act):
                act.wait_ge(s_step, B + 6)
                nc.scalar.activation(mv[:, :, 0], mean[:, 1, :], ACT.Sqrt, bias=G.eps5[:, 0:1]).then_inc(s_std, 1)


def load_image_and_statistics(nc, G, x_dram):
    with ExitStack() as ctx:
        s_x = [ctx.enter_context(nc.semaphore(f"x_landed{b}")) for b in range(B)]
        s_c = ctx.enter_context(nc.semaphore("constants_landed"))
        s_st = ctx.enter_context(nc.semaphore("load_stats_done"))
        with nc.Block() as block:
            @block.sync
            def _(sp):
                sp.dma_start(G.small[:], G.d["small"]).then_inc(s_c, 16)
                for b in range(B):
                    sp.dma_start(G.X[:, b, :], x_dram[b]).then_inc(s_x[b], 16)
                sp.wait_ge(s_c, 16)

            @block.vector
            def _(dve):
                nc.vector.memset(G.eps5[:], 1e-5).then_inc(s_st, 1)
                for b in range(B):
                    dve.wait_ge(s_x[b], 16)
                    for c in range(NCH):
                        nc.vector.bn_stats(G.stats[:, b, c, :], G.X[:, b, c * CH:(c + 1) * CH]).then_inc(s_st, 1)
                dve.wait_ge(s_st, 1 + B * NCH)


def layer1(nc, G):
    NI, PAD = 2, TAPS // 2
    with ExitStack() as ctx:
        def sb(name, shape, dt=F32):
            return ctx.enter_context(nc.sbuf_tensor(name, shape, dt))

        def sem(name):
            return ctx.enter_context(nc.semaphore(name))
        S = sb("prop_S", [P, 4, H, W])
        wt = sb("prop_w", [P, 2, TAPS * P])
        cur = sb("prop_cur", [P, 2, 2, NI, W + 2 * PAD])
        ps = [ctx.enter_context(nc.psum_tensor(f"prop_ps{s}", [P, NI, W], F32)) for s in range(2)]
        s_zero, s_norm, s_w = sem("p_borders_zero"), sem("p_S_normed"), [sem("p_w0"), sem("p_w1")]
        s_conv = [sem("p_conv0"), sem("p_conv1")]
        s_line = [sem("p_line0"), sem("p_line1")]
        s_kept = [sem("p_kept0"), sem("p_kept1")]
        s_stat = sem("p_stats")
        XV = G.X[:].rearrange("p b (h w) -> p b h w", h=H)
        names = ["w_down", "w_up", "w_right", "w_left"]

        def line(buf, d, b0, s, idx):
            lo = b0 + NI * s
            if d < 2:
                return buf[:, lo:lo + NI, idx, :]
            return buf[:, lo:lo + NI, :, idx]

        def place(d, t):
            return t if d % 2 == 0 else t * -1 + (H - 1)

        with nc.Block() as block:
            @block.sync
            def _(sp):
                for a in range(2):
                    for d in range(4):
                        D = 4 * a + d
                        if D >= 2:
                            for s in range(2):
                                sp.wait_ge(s_conv[s], (H - 1) * (D - 1))
                        sp.dma_start(wt[:, D % 2, :], G.d[names[d]]).then_inc(s_w[D % 2], 16)

            @block.scalar
            def _(act):
                for a in range(2):
                    if a:
                        for s in range(2):
                            act.wait_ge(s_line[s], H * 4 * a)
                    for k in range(4):
                        b = 4 * a + k
                        act.activation(S[:, k, :, :], XV[:, b, :, :], ACT.Identity, bias=G.shift[:, b:b + 1],
                                       scale=G.rstd[:, b:b + 1]).then_inc(s_norm, 1)
                    act.wait_ge(s_norm, 4 * (a + 1))
                    for d in range(3):
                        m0 = H * (4 * a + d)

                        def keep(t, turn):
                            for s in range(2):
                                act.wait_ge(s_line[s], m0 + t + 1)
                                act.activation(line(S, d, 0, s, place(d, t)), cur[:, s, turn, :, PAD:PAD + W],
                                               ACT.Copy).then_inc(s_kept[s], 1)
                        with act.Fori(0, H // 2) as j:
                            keep(2 * j, 0)
                            keep(2 * j + 1, 1)

            @block.gpsimd
            def _(pool):
                pool.memset(cur[:].rearrange("p a b c d -> p (a b c d)"), 0.0).then_inc(s_zero, 1)
                for a in range(2):
                    d = 3
                    m0 = H * (4 * a + d)

                    def add(t, turn):
                        for s in range(2):
                            pool.wait_ge(s_line[s], m0 + t + 1)
                            xl = line(XV, d, 4 * a, s, place(d, t))
                            pool.tensor_tensor(xl, xl, cur[:, s, turn, :, PAD:PAD + W], ALU.add).then_inc(s_kept[s], 1)
                    for s in range(2):
                        pool.wait_ge(s_kept[s], m0)
                    pool.wait_ge(s_norm, 4 * (a + 1))
                    with pool.Fori(0, H // 2) as j:
                        add(2 * j, 0)
                        add(2 * j + 1, 1)

            @block.tensor
            def _(pe):
                for a in range(2):
                    for d in range(4):
                        D = 4 * a + d
                        m0 = H * D
                        pe.wait_ge(s_w[D % 2], 16 * (D // 2 + 1))

                        def conv(t, turn):
                            for s in range(2):
                                pe.wait_ge(s_line[s], m0 + t)
                                for k in range(TAPS):
                                    mm = pe.matmul(ps[s][:], wt[:, D % 2, k * P:(k + 1) * P],
                                                   cur[:, s, 1 - turn, :, k:k + W], start=(k == 0), stop=(k == TAPS - 1))
                                mm.then_inc(s_conv[s], 1)
                        with pe.Fori(0, H // 2 - 1) as j:
                            conv(2 * j + 1, 1)
                            conv(2 * j + 2, 0)
                        conv(H - 1, 1)

            @block.vector
            def _(dve):
                dve.wait_ge(s_zero, 1)
                for a in range(2):
                    dve.wait_ge(s_norm, 4 * (a + 1))
                    for d in range(4):
                        D = 4 * a + d
                        m0, c0 = H * D, (H - 1) * D

                        def step(t, turn):
                            for s in range(2):
                                dve.wait_ge(s_kept[s], m0 + t - 1)
                                dve.wait_ge(s_conv[s], c0 + t)
                                dve.scalar_tensor_tensor(cur[:, s, turn, :, PAD:PAD + W], ps[s][:], 0.0,
                                                         line(S, d, 0, s, place(d, t)), ALU.max, ALU.add).then_inc(s_line[s], 1)
                        for s in range(2):
                            if D:
                                dve.wait_ge(s_kept[s], m0)
                            dve.tensor_copy(cur[:, s, 0, :, PAD:PAD + W], line(S, d, 0, s, place(d, 0))).then_inc(s_line[s], 1)
                        if D == 0:
                            for s in range(2):
                                dve.wait_ge(s_conv[s], 1)
                                dve.scalar_tensor_tensor(cur[:, s, 1, :, PAD:PAD + W], ps[s][:], 0.0,
                                                         line(S, d, 0, s, place(d, 1)), ALU.max, ALU.add).then_inc(s_line[s], 1)
                        else:
                            step(1, 1)
                        with dve.Fori(0, H // 2 - 1) as j:
                            step(2 * j + 2, 0)
                            step(2 * j + 3, 1)
                    for s in range(2):
                        dve.wait_ge(s_kept[s], H * 4 * (a + 1))
                    for b in range(4 * a, 4 * a + 4):
                        for c in range(NCH):
                            dve.bn_stats(G.stats[:, b, c, :], G.X[:, b, c * CH:(c + 1) * CH]).then_inc(s_stat, 1)
                dve.wait_ge(s_stat, B * NCH)


def layer2(nc, G, x3_dram):
    K1, K3, GT = 5, 3, 3
    K7 = K1 + K3 - 1
    with ExitStack() as ctx:
        def sb(name, shape, dt=F32):
            return ctx.enter_context(nc.sbuf_tensor(name, shape, dt))

        def sem(name):
            return ctx.enter_context(nc.semaphore(name))
        w1 = sb("l2_w1", [P, K1, P])
        w3 = sb("l2_w3", [P, K3, P])
        w7 = sb("l2_w7", [P, K7, P])
        edge = sb("l2_edge", [P, 4, P])
        tmp = sb("l2_tmp", [P, P])
        w4g = sb("l2_w4g", [P, GT, 8])
        w4 = sb("l2_w4", [P, GT, P])
        xn = [sb(f"l2_xn{i}", [P, HP, WP]) for i in range(2)]
        gate = sb("l2_gate", [P, 2, CH])
        prod = sb("l2_prod", [P, 2, CH])
        ps3 = ctx.enter_context(nc.psum_tensor("l2_ps3", [P, 2, CH], F32))
        ps4 = ctx.enter_context(nc.psum_tensor("l2_ps4", [P, 2, CH], F32))
        s_ld, s_w, s_xn = sem("c_weights_landed"), sem("c_weights_made"), sem("c_xn_ready")
        s_t3, s_t4, s_gate, s_prod = sem("c_conv_done"), sem("c_gate_summed"), sem("c_gate_copied"), sem("c_product")
        s_x, s_st, s_out = sem("c_x_updated"), sem("c_stats"), sem("c_x_stored")
        XV = G.X[:].rearrange("p b (h w) -> p b h w", h=H)

        with nc.Block() as block:
            @block.sync
            def _(sp):
                sp.dma_start(w1[:], G.d["l2_w1"]).then_inc(s_ld, 16)
                sp.dma_start(w3[:].rearrange("p a o -> p (a o)"), G.d["l2_w3"].to_broadcast([P, K3 * P])).then_inc(s_ld, 16)
                sp.dma_start(w4g[:], G.d["l2_w4"]).then_inc(s_ld, 16)
                with sp.Fori(0, B) as b:
                    sp.wait_ge(s_x, b * NCH + NCH)
                    sp.dma_start(x3_dram[b], G.X[:, b, :]).then_inc(s_out, 16)
                sp.wait_ge(s_out, 16 * B)

            @block.gpsimd
            def _(pool):
                for i in range(2):
                    pool.memset(xn[i][:].rearrange("p a b -> p (a b)"), 0.0).then_inc(s_w, 1)
                pool.wait_ge(s_ld, 48)
                n = 2

                def done(ins):
                    nonlocal n
                    n += 1
                    ins.then_inc(s_w, 1)
                    pool.wait_ge(s_w, n)
                for j in range(K7):
                    first = True
                    for a in range(K3):
                        if 0 <= j - a < K1:
                            dst = w7[:, j, :] if first else tmp[:]
                            done(pool.tensor_tensor(dst, w1[:, j - a, :], w3[:, a, :], ALU.mult))
                            if not first:
                                done(pool.tensor_tensor(w7[:, j, :], w7[:, j, :], tmp[:], ALU.add))
                            first = False
                for e, (a, b1) in enumerate([(0, 3), (0, 4), (2, 0), (2, 1)]):
                    done(pool.tensor_tensor(tmp[:], w1[:, b1, :], w3[:, a, :], ALU.mult))
                    done(pool.tensor_scalar(edge[:, e, :], tmp[:], -1.0, None, ALU.mult))
                for k in range(GT):
                    done(pool.tensor_copy(w4[:, k, :].rearrange("p (r g) -> p r g", g=8),
                                          w4g[:, k:k + 1, :].to_broadcast([P, P // 8, 8])))
                pool.sem_inc(s_w, 100)
                with pool.Fori(0, B) as b:
                    for c in range(NCH):
                        g = b * NCH + c
                        pool.wait_ge(s_prod, g + 1)
                        xc = G.X[:, b, c * CH:(c + 1) * CH]
                        pool.tensor_tensor(xc, xc, prod[:, c % 2, :], ALU.add).then_inc(s_x, 1)

            @block.scalar
            def _(act):
                act.wait_ge(s_w, 100)

                def norm(b):
                    bb = b % 2
                    act.activation(xn[bb][:, PADH:PADH + H, PADW:PADW + W], XV[:, b, :, :], ACT.Identity,
                                   bias=G.shift[:, b:b + 1], scale=G.rstd[:, b:b + 1]).then_inc(s_xn, 1)
                norm(0)
                for b in range(B):
                    if b + 1 < B:
                        if b:
                            act.wait_ge(s_t3, b * NCH)
                        norm(b + 1)
                    for c in range(NCH):
                        g = b * NCH + c
                        act.wait_ge(s_t4, g + 1)
                        if g >= 2:
                            act.wait_ge(s_prod, g - 1)
                        act.activation(gate[:, c % 2, :], ps4[:, c % 2, :], ACT.Copy).then_inc(s_gate, 1)

            @block.tensor
            def _(pe):
                pe.wait_ge(s_w, 100)
                for b in range(B):
                    pe.wait_ge(s_xn, b + 1)
                    x = xn[b % 2]
                    for c in range(NCH):
                        g = b * NCH + c
                        if g >= 2:
                            pe.wait_ge(s_prod, g - 1)
                        o3 = ps3[:, c % 2, :].rearrange("p (h w) -> p h w", w=W)
                        o4 = ps4[:, c % 2, :].rearrange("p (h w) -> p h w", w=W)
                        r = c * ROWS
                        for k in range(GT):
                            mm = pe.matmul(o4, w4[:, k, :], x[:, PADH + r:PADH + r + ROWS, 2 * k:2 * k + W],
                                           start=(k == 0), stop=(k == GT - 1))
                        mm.then_inc(s_t4, 1)
                        for j in range(K7):
                            if j == K7 - 1 and c == 0:
                                for e, row in ((0, 0), (1, 1)):
                                    pe.matmul(o3[:, 0, :], edge[:, e, :], x[:, PADH + row, PADW:PADW + W],
                                              start=False, stop=False, skip_group_check=True)
                            if j == K7 - 1 and c == NCH - 1:
                                for e, row in ((2, H - 2), (3, H - 1)):
                                    pe.matmul(o3[:, ROWS - 1, :], edge[:, e, :], x[:, PADH + row, PADW:PADW + W],
                                              start=False, stop=False, skip_group_check=True)
                            mm = pe.matmul(o3, w7[:, j, :], x[:, r + j:r + j + ROWS, PADW:PADW + W],
                                           start=(j == 0), stop=(j == K7 - 1), skip_group_check=True)
                        mm.then_inc(s_t3, 1)

            @block.vector
            def _(dve):
                for b in range(B):
                    for c in range(NCH):
                        g = b * NCH + c
                        dve.wait_ge(s_t3, g + 1)
                        dve.wait_ge(s_gate, g + 1)
                        if g >= 2:
                            dve.wait_ge(s_x, g - 1)
                        dve.tensor_tensor(prod[:, c % 2, :], ps3[:, c % 2, :], gate[:, c % 2, :], ALU.mult).then_inc(s_prod, 1)
                        if g >= 1:
                            bb, cc = (g - 1) // NCH, (g - 1) % NCH
                            dve.wait_ge(s_x, g)
                            dve.bn_stats(G.stats[:, bb, cc, :], G.X[:, bb, cc * CH:(cc + 1) * CH]).then_inc(s_st, 1)
                dve.wait_ge(s_x, B * NCH)
                dve.bn_stats(G.stats[:, B - 1, NCH - 1, :], G.X[:, B - 1, (NCH - 1) * CH:]).then_inc(s_st, 1)
                dve.wait_ge(s_st, B * NCH)


def layer0_weights(nc, G, T):
    with ExitStack() as ctx:
        def sb(name, shape, dt=F32):
            return ctx.enter_context(nc.sbuf_tensor(name, shape, dt))
        expand = sb("w_expand", [P, HALF])
        concat = sb("w_concat", [P, HALF])
        folded = sb("w_folded", [P, P])
        in_raw = sb("w_in_raw", [P, 2 * P])
        cols = sb("w_cols", [P, 16])
        xproj = sb("w_xproj", [P, 36])
        xdt = sb("w_xdt", [4, P])
        dtw = sb("w_dtw", [4, P])
        ps = ctx.enter_context(nc.psum_tensor("w_ps", [P, 8, P], F32))
        s_zero, s_ld, s_mm, s_v = [ctx.enter_context(nc.semaphore(f"w0_{n}")) for n in ("zero", "landed", "products", "made")]
        concat_b, ln_g, ln_b, out_b, d_ssm = (cols[:, k:k + 1] for k in range(5))
        c1w = cols[:, 5:8]
        with nc.Block() as block:
            @block.gpsimd
            def _(pool):
                for t in (T.conv, folded, in_raw, cols, T.bc, T.out, T.fin_b, T.dt_b):
                    flat = t[:] if len(t.shape) == 2 else t[:].rearrange("p a b -> p (a b)")
                    pool.memset(flat, 0.0).then_inc(s_zero, 1)
                pool.memset(T.one[:], 1.0).then_inc(s_zero, 1)
                pool.memset(T.zero[:], 0.0).then_inc(s_zero, 1)

            @block.sync
            def _(sp):
                sp.wait_ge(s_zero, 10)
                loads = [(expand[:], "expand_wT"), (concat[:], "concat_w"), (in_raw[0:HALF, :], "in_w"),
                         (concat_b[0:HALF, :], "concat_b"), (ln_g[0:HALF, :], "ln_g"), (ln_b[0:HALF, :], "ln_b"),
                         (out_b[0:HALF, :], "out_b"), (d_ssm, "D_ssm"), (c1w, "conv1d_w"), (T.conv1d_b[:], "conv1d_b"),
                         (xproj[:], "xproj_w"), (xdt[:], "xproj_dtT"), (dtw[:], "dt_w"), (T.dt_b[:], "dt_b"),
                         (T.A[:], "A_log"), (T.out[:, 0:HALF], "out_w"), (T.in_b[:], "in_b"),
                         (T.conv[HALF:P, :, HALF:P], "conv_w"), (T.fin_b[HALF:P, :], "conv_b"),
                         (T.fin_b[0:HALF, :], "concat_b")]
                for dst, name in loads:
                    sp.dma_start(dst, G.d[name]).then_inc(s_ld, 16)
                sp.wait_ge(s_ld, 16 * len(loads))
                sp.sem_inc(s_ld, 1000)

            @block.tensor
            def _(pe):
                pe.wait_ge(s_ld, 1000)
                pe.matmul(ps[0:HALF, 0, 0:HALF], concat[:], expand[:], start=True, stop=True).then_inc(s_mm, 1)
                pe.matmul(ps[0:HALF, 4, 0:HALF], expand[:], concat[:], start=True, stop=True).then_inc(s_mm, 1)
                pe.wait_ge(s_v, 2)
                pe.matmul(ps[:, 0, :], folded[:], G.centre, start=True, stop=True).then_inc(s_mm, 1)
                pe.matmul(ps[:, 4, 0:1], G.centre, concat_b, start=True, stop=True).then_inc(s_mm, 1)
                pe.wait_ge(s_v, 4)
                pe.matmul(ps[:, 0, :], xdt[:], dtw[:], start=True, stop=True).then_inc(s_mm, 1)
                for h in range(2):
                    pe.matmul(ps[:, 4, h:h + 1], in_raw[:, h * P:(h + 1) * P], ln_b, start=True, stop=True).then_inc(s_mm, 1)

            @block.scalar
            def _(act):
                act.wait_ge(s_ld, 1000)
                act.activation(T.A[:], T.A[:], ACT.Exp).then_inc(s_zero, 1)

            @block.vector
            def _(dve):
                dve.wait_ge(s_ld, 1000)
                dve.wait_ge(s_mm, 2)
                dve.tensor_copy(folded[0:HALF, 0:HALF], ps[0:HALF, 0, 0:HALF]).then_inc(s_v, 1)
                dve.tensor_copy(T.conv[0:HALF, TAPS // 2, 0:HALF], ps[0:HALF, 4, 0:HALF]).then_inc(s_v, 1)
                dve.wait_ge(s_mm, 4)
                dve.tensor_copy(T.centred[:], ps[:, 0, :]).then_inc(s_v, 1)
                dve.tensor_copy(T.centred_b[:], ps[:, 4, 0:1]).then_inc(s_v, 1)
                dve.wait_ge(s_mm, 7)
                dve.tensor_copy(T.dt[:], ps[:, 0, :]).then_inc(s_v, 1)
                dve.tensor_tensor(T.in_b[:], T.in_b[:], ps[:, 4, 0:2], ALU.add).then_inc(s_v, 1)
                dve.tensor_scalar(T.inw[:], in_raw[:], ln_g, None, ALU.mult).then_inc(s_v, 1)
                for k in range(3):
                    dve.tensor_scalar(T.conv1d[:, k, :], G.ident, c1w[:, k:k + 1], None, ALU.mult).then_inc(s_v, 1)
                dve.tensor_scalar(T.d_diag[:], G.ident, d_ssm, None, ALU.mult).then_inc(s_v, 1)
                for k in range(2):
                    dve.tensor_copy(T.bc[:, 32 * k:32 * k + 32], xproj[:, 4:36]).then_inc(s_v, 1)
                dve.tensor_copy(T.pick[:], G.pick).then_inc(s_v, 1)
                dve.tensor_tensor(T.fin_b[0:HALF, :], T.fin_b[0:HALF, :], out_b[0:HALF, :], ALU.add).then_inc(s_v, 1)
                dve.wait_ge(s_zero, 11)
                dve.tensor_scalar(T.A[:], T.A[:], -1.0, None, ALU.mult).then_inc(s_v, 1)
                dve.wait_ge(s_v, 16)


def layer0(nc, G):
    NDA = 8
    LEAD = 3
    with ExitStack() as ctx:
        def sb(name, shape, dt=F32):
            return ctx.enter_context(nc.sbuf_tensor(name, shape, dt))

        class T:
            pass
        T.conv = sb("m_conv", [P, TAPS, P])
        T.centred, T.dt, T.bc, T.out, T.d_diag = (sb(f"m_{n}", [P, P]) for n in ("centred", "dt", "bc", "out", "d"))
        T.inw = sb("m_inw", [P, 2 * P])
        T.conv1d = sb("m_conv1d", [P, 3, P])
        T.pick = sb("m_pick", [P, 32], F32R)
        T.A = sb("m_A", [P, NS])
        T.in_b = sb("m_in_b", [P, 2])
        T.centred_b, T.conv1d_b, T.dt_b, T.fin_b, T.one = (sb(f"m_{n}", [P, 1]) for n in ("cb", "c1b", "dtb", "finb", "one"))
        T.zero = sb("m_zero", [P, W + 2])
        layer0_weights(nc, G, T)

        xn = sb("m_xn", [P, 2, ROWS + 2, W + 2])
        xnc = sb("m_xnc", [P, CH])
        tc = sb("m_tc", [P, CH])
        sq = sb("m_sq", [P, CH])
        arg = sb("m_arg", [P, CH])
        ea = sb("m_ea", [P, CH])
        ln = sb("m_ln", [P, CH])
        rest = sb("m_rest", [P, CH])
        fin = sb("m_fin", [P, CH])
        xs = sb("m_xs", [P, 2 + CH])
        xc = sb("m_xc", [P, CH])
        dt = sb("m_dtv", [P, 2, CH])
        dtx = sb("m_dtx", [P, 2, CH])
        sz = sb("m_sz", [P, 2, CH])
        bcs = sb("m_bcs", [P, 2, CH], F32R)
        dA = sb("m_dA", [P, NDA, CH])
        hb = sb("m_hb", [P, 4, CH])
        hc = sb("m_hc", [P, 4, CH])
        hs = sb("m_hs", [P, 2, CH])
        state = sb("m_state", [P, NS])
        pf = [ctx.enter_context(nc.psum_tensor(f"m_pf{i}", [P, CH], F32)) for i in range(2)]
        pB = ctx.enter_context(nc.psum_tensor("m_pB", [P, 2, CH], F32))
        pC = ctx.enter_context(nc.psum_tensor("m_pC", [P, 2, CH], F32))
        pY = ctx.enter_context(nc.psum_tensor("m_pY", [P, CH], F32))
        pO = ctx.enter_context(nc.psum_tensor("m_pO", [P, CH], F32))
        XV = G.X[:].rearrange("p b (h w) -> p b h w", h=H)

        class s:
            pass
        credited = []

        def sem(name):
            q = ctx.enter_context(nc.semaphore("m_" + name))
            credited.append(q)
            return q
        s.p1, s.tc, s.sq, s.var, s.lnv, s.rstd, s.u = (sem(n) for n in ("p1", "tc", "sq", "var", "lnv", "rstd", "u"))
        s.halo, s.xs, s.z, s.xse, s.sz, s.cv, s.xc = (sem(n) for n in ("halo", "xs", "z", "xse", "sz", "cv", "xc"))
        s.dtp, s.bc, s.xb, s.abs, s.e, s.ln, s.bhi, s.blo = (sem(n) for n in ("dtp", "bc", "xb", "abs", "e", "ln", "bhi", "blo"))
        s.r1, s.r2, s.r3, s.dt, s.dtx = (sem(n) for n in ("rest1", "rest2", "rest3", "dt", "dtx"))
        s.dterm, s.y, s.out, s.fin, s.add, s.st = (sem(n) for n in ("dterm", "y", "out", "fin", "add", "stats"))
        s.B, s.C, s.dA, s.U, s.S, s.HC, s.state = (sem(n) for n in ("B", "C", "dA", "U", "S", "HC", "state"))
        s.pair, s.sum = sem("pair"), sem("sum")
        s.norm, s.xn, s.edge = sem("norm"), sem("xn"), sem("edge")
        s.border = sem("border")

        PE_AT = {1: ["scan input"], 2: ["gate input"], 3: ["convolve"], 6: ["centre"], 7: ["project dt"],
                 8: ["project B, C"], 9: ["variance"]}
        ACT_AT = {2: ["scan input"], 4: ["norm"], 5: ["silu"], 6: ["pad"], 7: ["centre"], 8: ["dt argument"],
                  9: ["round B, C"], 10: ["log", "deviation"]}
        POOL_AT = {0: ["halo"], 11: ["softplus"], 13: ["normalise"], 14: ["dt * x"]}
        DVE_AT = {10: ["rest of B, C", "softplus"], 13: ["dt"]}
        TWO_AHEAD = ("norm", "centre", "variance", "deviation", "normalise")
        CONV_AT = {7: 1, 9: 1, 10: 1, 11: 2, 12: 1, 13: 1, 14: 1, 15: 1}
        SUM_AT = {5: 0, 6: 1, 8: 2, 10: 3, 12: 4, 14: 5}
        LATE_SUM_AT = {0: 6, 2: 7}

        def front_pe(g, b, c, par, what):
            pe = nc.tensor
            if what == "centre":
                after(pe, s.norm, g)
                after(pe, s.xc, g, 1)
                pe.matmul(pf[0][:], T.centred[:], xnc[:], start=True, stop=True).then_inc(s.p1, 1)
            if what == "variance":
                after(pe, s.sq, g)
                after(pe, s.xb, g, 1)
                pe.matmul(pf[1][:], G.mean64, sq[:], start=True, stop=True).then_inc(s.var, 1)
            if what == "scan input":
                after(pe, s.u, g)
                after(pe, s.blo, g, 1)
                pe.matmul(pf[0][:], T.inw[:, 0:P], tc[:], start=True, stop=True).then_inc(s.xs, 1)
            if what == "gate input":
                after(pe, s.lnv, g)
                pe.matmul(pf[1][:], T.inw[:, P:2 * P], tc[:], start=True, stop=True).then_inc(s.z, 1)
            if what == "convolve":
                after(pe, s.xse, g)
                for j in range(3):
                    mm = pe.matmul(pf[0][:], T.conv1d[:, j, :], xs[:, j:j + CH], start=(j == 0), stop=(j == 2))
                mm.then_inc(s.cv, 1)
            if what == "project dt":
                after(pe, s.sz, g)
                after(pe, s.xc, g)
                pe.matmul(pf[1][:], T.dt[:], xc[:], start=True, stop=True).then_inc(s.dtp, 1)
            if what == "project B, C":
                after(pe, s.sq, g + 1)
                pe.matmul(pf[0][:], T.bc[:], xc[:], start=True, stop=True).then_inc(s.bc, 1)

        def front_act(g, b, c, par, what):
            act = nc.scalar
            bias, scale = G.shift[:, bass.ds(b, 1)], G.rstd[:, bass.ds(b, 1)]
            if what == "norm":
                after(act, s.p1, g, 1)
                act.activation(xnc[:].rearrange("p (h w) -> p h w", w=W), XV[:, b, bass.ds(c * ROWS, ROWS), :],
                               ACT.Identity, bias=bias, scale=scale).then_inc(s.norm, 1)
            if what == "pad":
                after(act, s.out, g, 2)
                top = isinstance(c, int) and c == 0
                bottom = isinstance(c, int) and c == NCH - 1
                if top or bottom:
                    act.activation(xn[:, par, 0 if top else ROWS + 1, :], T.zero[:], ACT.Copy).then_inc(s.edge, 1)
                first = 0 if top else c * ROWS - 1
                n = ROWS + 2 - top - bottom
                act.activation(xn[:, par, int(top):int(top) + n, 1:1 + W], XV[:, b, bass.ds(first, n), :],
                               ACT.Identity, bias=bias, scale=scale).then_inc(s.xn, 1)
            if what == "centre":
                after(act, s.p1, g)
                after(act, s.z, g, 1)
                after(act, s.u, g, 1)
                act.activation(tc[:], pf[0][:], ACT.Identity, bias=T.centred_b[:, 0:1]).then_inc(s.tc, 1)
                act.activation(sq[:], pf[0][:], ACT.Square, bias=T.centred_b[:, 0:1]).then_inc(s.sq, 1)
            if what == "deviation":
                after(act, s.var, g)
                act.activation(sq[:], pf[1][:], ACT.Ln, bias=G.eps5[:, 0:1]).then_inc(s.lnv, 1)
                after(act, s.lnv, g)
                act.activation(sq[:], sq[:], ACT.Exp, scale=-0.5).then_inc(s.rstd, 1)
            if what == "scan input":
                after(act, s.xs, g)
                after(act, s.halo, g)
                act.activation(xs[:, 2:2 + CH], pf[0][:], ACT.Identity, bias=T.in_b[:, 0:1]).then_inc(s.xse, 1)
            if what == "silu":
                after(act, s.z, g)
                after(act, s.out, g, 2)
                act.activation(sz[:, par, :], pf[1][:], ACT.Silu, bias=T.in_b[:, 1:2]).then_inc(s.sz, 1)
                after(act, s.cv, g)
                after(act, s.dterm, g, 1)
                after(act, s.dtx, g, 1)
                act.activation(xc[:], pf[0][:], ACT.Silu, bias=T.conv1d_b[:, 0:1]).then_inc(s.xc, 1)
            if what == "dt argument":
                after(act, s.dtp, g)
                after(act, s.dt, g, 1)
                act.activation(arg[:], pf[1][:], ACT.Identity, bias=T.dt_b[:, 0:1]).then_inc(s.xb, 1)
                after(act, s.xb, g)
                after(act, s.r3, g, 1)
                act.activation(ea[:], arg[:], ACT.Abs).then_inc(s.abs, 1)
                after(act, s.abs, g)
                act.activation(ea[:], ea[:], ACT.Exp, scale=-1.0).then_inc(s.e, 1)
            if what == "round B, C":
                after(act, s.bc, g)
                after(act, s.C, 16 * g - 16, 1)
                act.activation(bcs[:, par, :], pf[0][:], ACT.Copy).then_inc(s.bhi, 1)
            if what == "log":
                after(act, s.e, g)
                after(act, s.r3, g, 1)
                act.activation(ln[:], ea[:], ACT.Ln, bias=T.one[:, 0:1]).then_inc(s.ln, 1)

        def front_pool(g, b, c, par, what):
            pool = nc.gpsimd
            if what == "normalise":
                after(pool, s.tc, g)
                after(pool, s.rstd, g)
                pool.tensor_tensor(tc[:], tc[:], sq[:], ALU.mult).then_inc(s.u, 1)
            if what == "halo":
                after(pool, s.cv, g, 1)
                after(pool, s.xse, g, 1)
                after(pool, s.halo, g, 1)
                if isinstance(c, int) and c == 0:
                    pool.tensor_tensor(xs[:, 0:2], T.zero[:, 0:2], T.zero[:, 0:2], ALU.add).then_inc(s.halo, 1)
                else:
                    pool.tensor_tensor(xs[:, 0:2], xs[:, CH:CH + 2], T.one[:].to_broadcast([P, 2]), ALU.mult).then_inc(s.halo, 1)
            if what == "softplus":
                after(pool, s.r1, g)
                pool.tensor_tensor(rest[:], ea[:], rest[:], ALU.subtract).then_inc(s.r2, 1)
                after(pool, s.r2, g)
                after(pool, s.ln, g)
                pool.tensor_tensor(rest[:], rest[:], ln[:], ALU.add).then_inc(s.r3, 1)
            if what == "dt * x":
                after(pool, s.dt, g)
                after(pool, s.xc, g)
                after(pool, s.U, 16 * g - 16, 1)
                pool.tensor_tensor(dtx[:, par, :], dt[:, par, :], xc[:], ALU.mult).then_inc(s.dtx, 1)

        def front_dve(g, b, c, par, what):
            dve = nc.vector
            if what == "rest of B, C":
                after(dve, s.bhi, g)
                dve.tensor_tensor(bcs[32:64, par, :], pf[0][32:64, :], bcs[32:64, par, :].bitcast(F32),
                                  ALU.subtract).then_inc(s.blo, 1)
            if what == "softplus":
                after(dve, s.e, g)
                after(dve, s.dt, g, 1)
                dve.tensor_scalar(rest[:], ea[:], 1.0, -1.0, ALU.add, ALU.add).then_inc(s.r1, 1)
            if what == "dt":
                after(dve, s.r3, g)
                after(dve, s.xb, g)
                after(dve, s.dA, 16 * g - 16, 1)
                dve.scalar_tensor_tensor(dt[:, par, :], arg[:], 0.0, rest[:], ALU.max, ALU.add).then_inc(s.dt, 1)

        def program(eng, at, chunk, front, finish, before=lambda: None):
            def parts(n, one_ahead, two_ahead):
                for what in at.get(n, ()):
                    where = two_ahead if what in TWO_AHEAD else one_ahead
                    if where:
                        front(*where, what)

            def image(b, last):
                def place(c):
                    if isinstance(c, int) and c >= NCH:
                        return b * NCH + c, (b + 1) % B, c - NCH
                    return b * NCH + c, b, c

                def one(c, par, last=True):
                    prev = place(c - 1) if last else None
                    if last and isinstance(c, int) and c == 0:
                        prev = (b * NCH - 1, b - 1, NCH - 1)
                    chunk(b * NCH + c, b, c, par, prev,
                          lambda n: parts(n, (*place(c + 1), 1 - par), (*place(c + 2), par)))
                one(0, 0, last)
                with eng.Fori(0, NCH // 2 - 2) as j:
                    one(2 * j + 1, 1)
                    one(2 * j + 2, 0)
                for c in range(NCH - 3, NCH):
                    one(c, c % 2)
            for n in range(NS):
                parts(n, None, (0, 0, 0, 0))
            for n in range(NS):
                parts(n, (0, 0, 0, 0), (1, 0, 1, 1))
            before()
            image(0, False)
            with eng.Fori(1, B) as b:
                image(b, True)
            finish(B * NCH - 1, B - 1, NCH - 1, 1)

        with nc.Block() as block:
            @block.sync
            def _(sp):
                for q in credited:
                    sp.sem_inc(q, CREDIT)

            @block.tensor
            def _(pe):
                def sum_pair(g, k):
                    after(pe, s.pair, 8 * g + k)
                    pe.matmul(pY[:], G.ident, hs[:, k % 2, :], start=False, stop=(k == NS // 2 - 1)).then_inc(s.sum, 1)

                def project_out(g, par):
                    after(pe, s.y, g)
                    pe.matmul(pO[:], T.out[:], sz[:, par, :], start=False, stop=True).then_inc(s.out, 1)

                def chunk(g, b, c, par, prev, parts_ahead):
                    def spread_B(n):
                        after(pe, s.U, NS * g + n, 2)
                        pe.matmul(pB[:, n % 2, :], T.pick[:, n:n + 1].to_broadcast([P, P]), bcs[:, par, :],
                                  start=True, stop=True).then_inc(s.B, 1)

                    def spread_C(n):
                        after(pe, s.HC, NS * g + n, 2)
                        pe.matmul(pC[:, n % 2, :], T.pick[:, NS + n:NS + n + 1].to_broadcast([P, P]), bcs[:, par, :],
                                  start=True, stop=True).then_inc(s.C, 1)
                    after(pe, s.blo, g)
                    spread_B(0)
                    spread_B(1)
                    tap = 0
                    for n in range(NS):
                        if n + 2 < NS:
                            spread_B(n + 2)
                        spread_C(n)
                        if prev and n in LATE_SUM_AT:
                            sum_pair(g - 1, LATE_SUM_AT[n])
                        if n == 4:
                            if prev:
                                project_out(g - 1, 1 - par)
                            after(pe, s.y, g, 1)
                            pe.matmul(pY[:], T.d_diag[:], xc[:], start=True, stop=False).then_inc(s.dterm, 1)
                        if n in SUM_AT:
                            sum_pair(g, SUM_AT[n])
                        for _ in range(CONV_AT.get(n, 0)):
                            if tap == 0:
                                after(pe, s.fin, g, 1)
                                after(pe, s.xn, g)
                            pe.matmul(pO[:].rearrange("p (h w) -> p h w", w=W), T.conv[:, tap, :],
                                      xn[:, par, tap // 3:tap // 3 + ROWS, tap % 3:tap % 3 + W],
                                      start=(tap == 0), stop=False)
                            tap += 1
                        parts_ahead(n)

                def finish(g, b, c, par):
                    for k in LATE_SUM_AT.values():
                        sum_pair(g, k)
                    project_out(g, par)
                program(pe, PE_AT, chunk, front_pe, finish)

            @block.scalar
            def _(act):
                after(act, s.border, 0)

                def result(g, b, c, par):
                    after(act, s.out, g)
                    after(act, s.add, g, 1)
                    act.activation(fin[:], pO[:], ACT.Relu, bias=T.fin_b[:, 0:1]).then_inc(s.fin, 1)

                def decay(g, n, par):
                    m = NS * g + n
                    after(act, s.dt, g)
                    after(act, s.S, m, NDA)
                    act.activation(dA[:, n % NDA, :], dt[:, par, :], ACT.Exp, scale=T.A[:, n:n + 1]).then_inc(s.dA, 1)

                def chunk(g, b, c, par, prev, parts_ahead):
                    for n in range(NS):
                        if n < NS - LEAD:
                            decay(g, n + LEAD, par)
                        else:
                            decay(g + 1, n + LEAD - NS, 1 - par)
                        if prev and n == 5:
                            result(*prev, 1 - par)
                        parts_ahead(n)
                program(act, ACT_AT, chunk, front_act, result, lambda: [decay(0, n, 0) for n in range(LEAD)])

            @block.gpsimd
            def _(pool):
                pool.memset(xn[:].rearrange("p a h w -> p (a h w)"), 0.0).then_inc(s.border, 1)

                def add_pair(g, k):
                    after(pool, s.HC, NS * g + 2 * k + 1)
                    after(pool, s.sum, 8 * g + k, 2)
                    pool.tensor_tensor(hs[:, k % 2, :], hc[:, (2 * k) % 4, :], hc[:, (2 * k + 1) % 4, :],
                                       ALU.add).then_inc(s.pair, 1)

                def result(g, b, c, par):
                    after(pool, s.fin, g)
                    xg = XV[:, b, bass.ds(c * ROWS, ROWS), :]
                    pool.tensor_tensor(xg, xg, fin[:].rearrange("p (h w) -> p h w", w=W), ALU.add).then_inc(s.add, 1)

                def chunk(g, b, c, par, prev, parts_ahead):
                    for n in range(NS):
                        m = NS * g + n
                        if n % 2 == 0 and n:
                            add_pair(g, n // 2 - 1)
                        after(pool, s.S, m)
                        last = hb[:, n % 4, CH - 1:CH]
                        pool.tensor_tensor(state[:, n:n + 1], last, T.one[:], ALU.mult).then_inc(s.state, 1)
                        if prev and n == 6:
                            result(*prev, 1 - par)
                        parts_ahead(n)
                    add_pair(g, NS // 2 - 1)
                program(pool, POOL_AT, chunk, front_pool, result)

            @block.vector
            def _(dve):
                def statistics(g, b, c):
                    after(dve, s.add, g)
                    dve.bn_stats(G.stats[:, b, c, :], XV[:, b, bass.ds(c * ROWS, ROWS), :]).then_inc(s.st, 1)

                def gated(g, par):
                    after(dve, s.sum, 8 * g + NS // 2 - 1)
                    after(dve, s.sz, g)
                    dve.tensor_tensor(sz[:, par, :], pY[:], sz[:, par, :], ALU.mult).then_inc(s.y, 1)

                def chunk(g, b, c, par, prev, parts_ahead):
                    def product(n):
                        m = NS * g + n
                        after(dve, s.B, m)
                        if n == 0:
                            after(dve, s.dtx, g)
                        after(dve, s.HC, m, 4)
                        after(dve, s.state, m, 4)
                        dve.tensor_tensor(hb[:, n % 4, :], dtx[:, par, :], pB[:, n % 2, :], ALU.mult).then_inc(s.U, 1)

                    def weigh(n):
                        m = NS * g + n
                        after(dve, s.S, m)
                        after(dve, s.C, m)
                        after(dve, s.pair, 8 * g + n // 2, 2)
                        dve.tensor_tensor(hc[:, n % 4, :], hb[:, n % 4, :], pC[:, n % 2, :], ALU.mult).then_inc(s.HC, 1)
                    c_is_first = isinstance(c, int) and c == 0
                    product(0)
                    for n in range(NS):
                        m = NS * g + n
                        if n + 1 < NS:
                            product(n + 1)
                        after(dve, s.U, m)
                        after(dve, s.dA, m)
                        after(dve, s.state, m, NS)
                        dve.tensor_tensor_scan(hb[:, n % 4, :], dA[:, n % NDA, :], hb[:, n % 4, :],
                                               T.zero[:, 0:1] if c_is_first else state[:, n:n + 1],
                                               ALU.mult, ALU.add).then_inc(s.S, 1)
                        if n:
                            weigh(n - 1)
                        if prev and n == 3:
                            gated(g - 1, 1 - par)
                        if prev and n == 14:
                            statistics(*prev)
                        parts_ahead(n)
                    weigh(NS - 1)

                def finish(g, b, c, par):
                    gated(g, par)
                    statistics(g, b, c)
                program(dve, DVE_AT, chunk, front_dve, finish)
                after(dve, s.st, B * NCH - 1)


def layer3(nc, G, x3_dram, out):
    E = W + 1
    NT = CH // P
    NG = TAPS * NT
    RING = 9
    NM = 13
    NO = 3 * TAPS
    FIRST = 20
    NCLEAR = -(-E // RING)
    TAB_DMA = 8 * 16
    with ExitStack() as ctx:
        def sb(name, shape, dt=F32):
            return ctx.enter_context(nc.sbuf_tensor(name, shape, dt))

        def sem(name):
            return ctx.enter_context(nc.semaphore(name))

        def bank(name, shape):
            return ctx.enter_context(nc.psum_tensor(name, shape, F32))
        table = nc.dram_tensor("corner_table", (2, E, E, 4 * P), F32).ap()
        base = sb("d_base", [P, 2, NCH, NG])
        off_w = sb("d_off_w", [P, TAPS, NO])
        off_b = sb("d_off_b", [NO, 1])
        dcn_w = sb("d_dcn_w", [P, TAPS, P])
        vecs = sb("d_vecs", [P, 3])
        s_const, s_zero, s_border = sem("d_constants"), sem("d_zeros"), sem("d_border_zeroed")
        with ExitStack() as ctx2:
            def sb2(name, shape, dt=F32):
                return ctx2.enter_context(nc.sbuf_tensor(name, shape, dt))
            xn = sb2("d_xn", [P, HP, WP])
            xc = sb2("d_xc", [P, CH])
            om_s = sb2("d_om", [NO, CH])
            tT = sb2("d_tT", [P, NT, P])
            mask = sb2("d_mask", [P, NG])
            V, F, T1 = (sb2(f"d_{n}", [P, 2, NG]) for n in ("V", "F", "T1"))
            I = sb2("d_I", [P, 2, NG], mybir.dt.int32)
            WT = sb2("d_WT", [P, 2, 2, NG])
            J = sb2("d_J", [P, NG])
            tb = sb2("d_table_base", [P, 1])
            IDX = sb2("d_idx", [P, 2 * NCH, NG], U32)
            W4 = sb2("d_w4", [P, 2 * NCH, NG * 4])
            idx_now = sb2("d_idx_now", [P, NG], U32)
            w_now = sb2("d_w_now", [P, NG * 4])
            ring = sb2("d_ring", [P, RING, 4 * P])
            R = sb2("d_mix", [P, 3, NT, P])
            samp = sb2("d_samp", [P, 3, CH])
            ps_off = ctx2.enter_context(nc.psum_tensor("d_ps_off", [NO, CH], F32))
            ps_tab = ctx2.enter_context(nc.psum_tensor("d_ps_tab", [P, NT, P], F32))
            ps_om = ctx2.enter_context(nc.psum_tensor("d_ps_om", [P, NT, NO], F32))
            ps_s = [ctx2.enter_context(nc.psum_tensor(f"d_ps_s{i}", [P, NT, P], F32)) for i in range(3)]
            ps_out = ctx2.enter_context(nc.psum_tensor("d_ps_out", [P, CH], F32))
            s_offs = sem("d_offsets_out")
            s_omT = sem("d_offsets_turned")
            s_tabT = sem("d_table_turned")
            s_tT = sem("d_table_tile_out")
            s_tab = sem("d_table_stored")
            s_math = sem("d_index_steps")
            s_mix = sem("d_mix_steps")
            s_turn = sem("d_samples_turned")
            s_samp = sem("d_samples_out")
            s_dcn = sem("d_taps_summed")
            s_out = sem("d_output_kept")
            s_xn, s_xc, s_conv, s_mask = sem("d_xn_ready"), sem("d_xc_ready"), sem("d_offsets_summed"), sem("d_mask")
            s_wnow, s_inow, s_r0, s_st = sem("d_w_now"), sem("d_idx_now"), sem("d_corner0"), sem("d_stats")
            s_passed, s_passed_dve = sem("d_waits_passed"), sem("d_waits_passed_dve")
            s_clear = sem("d_second_table_cleared")
            s_land = [sem(f"d_landed{i}") for i in range(RING)]
            s_tb = sem("d_table_base_set")
            XV = G.X[:].rearrange("p b (h w) -> p b h w", h=H)

            def passes(eng, body, head=None):
                if head:
                    head(0, None)
                with eng.Fori(0, NCH) as c:
                    body(0, None, c)
                with eng.Fori(1, B) as p:
                    if head:
                        head(p, p - 1)
                    with eng.Fori(0, NCH) as c:
                        body(p, p - 1, c)
                if head:
                    head(None, B - 1)
                with eng.Fori(0, NCH) as c:
                    body(None, B - 1, c)

            def mixed(m):
                return 3 * (m - m % 2) + 4 + m % 2 + 1

            with nc.Block() as block:
                @block.sync
                def _(sp):
                    for dst, n in ((base[:].rearrange("p a c k -> p (a c k)"), "base"), (off_w[:], "off_w"),
                                   (off_b[:], "off_b"), (dcn_w[:], "dcn_w"), (vecs[:, 0:1], "dcn_b"),
                                   (vecs[:, 1:2], "gamma"), (vecs[:, 2:3], "beta")):
                        sp.dma_start(dst, G.d[n]).then_inc(s_const, 16)
                    for s in (s_offs, s_omT, s_tabT, s_tT, s_tab, s_math, s_mix, s_turn, s_samp, s_dcn, s_out):
                        sp.sem_inc(s, CREDIT)
                    sp.wait_ge(s_const, 16 * 7)

                @block.gpsimd
                def _(pool):
                    pool.memset(xn[:].rearrange("p h w -> p (h w)"), 0.0).then_inc(s_zero, 1)
                    pool.memset(tb[:], 0.0).then_inc(s_zero, 1)
                    pool.memset(ring[:].rearrange("p r e -> p (r e)"), 0.0).then_inc(s_zero, 1)
                    pool.wait_ge(s_zero, 3)

            with nc.Block() as block:
                @block.sync
                def _(sp):
                    for side in range(2):
                        sp.dma_start(table[0, side * (E - 1), :, 2 * side * P:2 * (side + 1) * P],
                                     ring[0:E, 0, 0:2 * P]).then_inc(s_border, 16)
                    sp.wait_ge(s_border, 32)
                    for slot in range(4):
                        sp.dma_start(table[0, :, slot % 2 * (E - 1), slot * P:(slot + 1) * P],
                                     ring[0:E, 0, 0:P]).then_inc(s_border, 16)
                    sp.wait_ge(s_border, 96)

                    def store(pT, pG, c):
                        if pT is None:
                            return
                        gT = NCH * pT + c
                        sp.wait_ge(s_tT, gT + (1 + CREDIT))
                        for yy in range(2):
                            for dy in range(2):
                                for dx in range(2):
                                    slot = 2 * dy + dx
                                    dst = table[pT % 2, bass.ds(ROWS * c + (yy + 1 - dy), NT, 2), 1 - dx:1 - dx + W,
                                                slot * P:(slot + 1) * P].rearrange("q x c -> x q c")
                                    sp.dma_start(dst, tT[yy * W:(yy + 1) * W, :, :]).then_inc(s_tab, 16)

                    def second_table(pT, pG):
                        if pT is not None and pG is not None:
                            sp.wait_ge(s_clear, 16 * NCLEAR)
                    passes(sp, store, second_table)
                    sp.wait_ge(s_tab, TAB_DMA * NCH * B + CREDIT)

                @block.gpsimd
                def _(pool):
                    flat = table.rearrange("a y x e -> (a y x) e")
                    for x0 in range(0, E, RING):
                        n = min(RING, E - x0)
                        pool.dma_start(table[1, :, x0:x0 + n, :], ring[0:E, 0:n, :]).then_inc(s_clear, 16)

                    def gather(pT, pG, c):
                        if pG is None:
                            return
                        gG = NCH * pG + c
                        pool.wait_ge(s_math, NM * gG + (NM + CREDIT))
                        for m in range(NG):
                            if m in (0, FIRST):
                                lo, hi = (0, FIRST) if m == 0 else (FIRST, NG)
                                apart(pool, s_passed)
                                pool.tensor_copy(idx_now[:, lo:hi], IDX[:, gG % (2 * NCH), lo:hi]).then_inc(s_inow, 1)
                                pool.wait_ge(s_inow, 2 * gG + (1 if m == 0 else 2))
                            pool.wait_ge(s_mix, 3 * NG * gG + (mixed(m + NG - RING) - 3 * NG + CREDIT))
                            apart(pool, s_passed)
                            pool.indirect_dma_start(
                                out=ring[:, m % RING, :], out_offset=None, in_=flat,
                                in_offset=bass.IndirectOffsetOnAxis(ap=idx_now[:, m:m + 1], axis=0),
                            ).then_inc(s_land[m % RING], 16)

                    def whole_table(pT, pG):
                        if pG is not None:
                            pool.wait_ge(s_clear, 16 * NCLEAR)
                            pool.wait_ge(s_tab, TAB_DMA * NCH * pG + (TAB_DMA * NCH + CREDIT))
                            apart(pool, s_passed)
                    passes(pool, gather, whole_table)

                @block.scalar
                def _(act):
                    def norm(pT, pG):
                        if pT is None:
                            return
                        act.activation(xn[:, PADH:PADH + H, PADW:PADW + W], XV[:, pT, :, :], ACT.Identity,
                                       bias=G.shift[:, bass.ds(pT, 1)], scale=G.rstd[:, bass.ds(pT, 1)]).then_inc(s_xn, 1)

                    def chunk(pT, pG, c):
                        doT, doG = pT is not None, pG is not None
                        if doT:
                            gT = NCH * pT + c
                        if doG:
                            gG = NCH * pG + c

                        def keep_samples(k):
                            act.wait_ge(s_turn, NG * gG + (NT * (k + 1) + CREDIT))
                            act.wait_ge(s_dcn, TAPS * gG + (k - 3 + 1 + CREDIT))
                            act.activation(samp[:, k % 3, :], ps_s[k % 3][:].rearrange("p t c -> p (t c)"),
                                           ACT.Copy).then_inc(s_samp, 1)
                        for k in range(TAPS):
                            if doG:
                                if k == 0:
                                    act.wait_ge(s_wnow, gG + 1)
                                for t in range(NT):
                                    m = NT * k + t
                                    act.wait_ge(s_land[m % RING], 64 * gG + 16 * (m // RING + 1))
                                    act.wait_ge(s_turn, NG * gG + (m - 3 * NT + 1 + CREDIT))
                                    act.activation(R[:, k % 3, t, :], ring[:, m % RING, 0:P], ACT.Copy,
                                                   scale=w_now[:, 4 * m:4 * m + 1]).then_inc(s_r0, 1)
                            if doT and k == 0:
                                act.wait_ge(s_tabT, NT * gT + CREDIT)
                                act.activation(xc[:], G.X[:, pT, bass.ds(CH * c, CH)], ACT.Identity,
                                               bias=G.shift[:, bass.ds(pT, 1)],
                                               scale=G.rstd[:, bass.ds(pT, 1)]).then_inc(s_xc, 1)
                            if doG and k >= 1:
                                keep_samples(k - 1)
                            if doT and k == 2:
                                act.wait_ge(s_tabT, NT * gT + (NT + CREDIT))
                                act.wait_ge(s_tab, TAB_DMA * gT + CREDIT)
                                act.activation(tT[:], ps_tab[:], ACT.Copy).then_inc(s_tT, 1)
                            if doT and k == 5:
                                act.wait_ge(s_conv, gT + 1)
                                act.wait_ge(s_omT, NT * gT + CREDIT)
                                act.activation(om_s[:], ps_off[:], ACT.Identity, bias=off_b[:, 0:1]).then_inc(s_offs, 1)
                            if doT and k == 7:
                                act.wait_ge(s_omT, NT * gT + (NT + CREDIT))
                                act.wait_ge(s_math, NM * gT + CREDIT)
                                act.activation(mask[:].rearrange("p (k t) -> p k t", t=NT),
                                               ps_om[:, :, 2 * TAPS:].rearrange("p t k -> p k t"),
                                               ACT.Sigmoid).then_inc(s_mask, 1)
                        if doG:
                            keep_samples(TAPS - 1)
                            act.wait_ge(s_dcn, TAPS * gG + (TAPS + CREDIT))
                            act.activation(G.X[:, pG, bass.ds(CH * c, CH)], ps_out[:], ACT.Identity,
                                           bias=vecs[:, 0:1]).then_inc(s_out, 1)
                    passes(act, chunk, norm)

                @block.tensor
                def _(pe):
                    def chunk(pT, pG, c):
                        doT, doG = pT is not None, pG is not None
                        if doT:
                            gT = NCH * pT + c
                        if doG:
                            gG = NCH * pG + c

                        def contract(k):
                            pe.wait_ge(s_samp, TAPS * gG + (k + 1 + CREDIT))
                            if k == 0:
                                pe.wait_ge(s_out, gG + CREDIT)
                            pe.matmul(ps_out[:], dcn_w[:, k, :], samp[:, k % 3, :], start=(k == 0),
                                      stop=(k == TAPS - 1)).then_inc(s_dcn, 1)
                        for k in range(TAPS):
                            if doG:
                                pe.wait_ge(s_samp, TAPS * gG + (k - 3 + 1 + CREDIT))
                                for t in range(NT):
                                    pe.wait_ge(s_mix, 3 * NG * gG + (mixed(NT * k + t) + CREDIT))
                                    pe.matmul(ps_s[k % 3][:, t, :], R[:, k % 3, t, :], G.ident, start=True,
                                              stop=True).then_inc(s_turn, 1)
                                if k >= 1:
                                    contract(k - 1)
                            if doT:
                                if k == 0:
                                    pe.wait_ge(s_xn, pT + 1)
                                    pe.wait_ge(s_offs, gT + CREDIT)
                                for tap in range(2 * k, min(2 * k + 2, TAPS)):
                                    ki, kj = tap // 3, tap % 3
                                    mm = pe.matmul(ps_off[:], off_w[:, tap, :],
                                                   xn[:, bass.ds(ROWS * c + (PADH - 1 + ki), ROWS), PADW - 1 + kj:PADW - 1 + kj + W],
                                                   start=(tap == 0), stop=(tap == TAPS - 1))
                                    if tap == TAPS - 1:
                                        mm.then_inc(s_conv, 1)
                                if k == 1:
                                    pe.wait_ge(s_xc, gT + 1)
                                    pe.wait_ge(s_tT, gT + CREDIT)
                                    for t in range(NT):
                                        pe.matmul(ps_tab[:, t, :], xc[:, t * P:(t + 1) * P], G.ident, start=True,
                                                  stop=True).then_inc(s_tabT, 1)
                                if k == 6:
                                    pe.wait_ge(s_offs, gT + (1 + CREDIT))
                                    pe.wait_ge(s_math, NM * gT + CREDIT)
                                    for t in range(NT):
                                        pe.matmul(ps_om[:, t, :], om_s[:, t * P:(t + 1) * P], G.ident[0:NO, 0:NO],
                                                  start=True, stop=True).then_inc(s_omT, 1)
                        if doG:
                            contract(TAPS - 1)
                    passes(pe, chunk)

                @block.vector
                def _(dve):
                    def next_table(pT, pG):
                        if pT is not None and pG is not None:
                            dve.wait_ge(s_math, NM * NCH * pT + CREDIT)
                            dve.tensor_scalar(tb[:], tb[:], -1.0, float(E * E), ALU.mult, ALU.add).then_inc(s_tb, 1)
                            dve.wait_ge(s_tb, pT)
                            apart(dve, s_passed_dve)

                    def indices(pT, gT, c):
                        step = 0

                        def do(make):
                            nonlocal step
                            dve.wait_ge(s_math, NM * gT + (step + CREDIT))
                            make().then_inc(s_math, 1)
                            step += 1
                        slot = gT % (2 * NCH)
                        dve.wait_ge(s_mask, gT + 1)
                        do(lambda: dve.tensor_tensor(V[:].rearrange("p a (k t) -> p a k t", t=NT),
                                                     ps_om[:, :, 0:2 * TAPS].rearrange("p t (k a) -> p a k t", a=2),
                                                     base[:, :, c, :].rearrange("p a (k t) -> p a k t", t=NT), ALU.add))
                        do(lambda: dve.tensor_scalar(V[:], V[:], 0.0, float(H + 1), ALU.max, ALU.min))
                        do(lambda: dve.tensor_copy(I[:], V[:]))
                        do(lambda: dve.tensor_copy(F[:], I[:]))
                        do(lambda: dve.tensor_tensor(T1[:], F[:], V[:], ALU.is_gt))
                        do(lambda: dve.tensor_tensor(F[:], F[:], T1[:], ALU.subtract))
                        do(lambda: dve.tensor_scalar(F[:], F[:], float(H), None, ALU.min))
                        do(lambda: dve.tensor_tensor(WT[:, :, 1, :], V[:], F[:], ALU.subtract))
                        do(lambda: dve.tensor_scalar(WT[:, :, 0, :], WT[:, :, 1, :], -1.0, 1.0, ALU.mult, ALU.add))
                        do(lambda: dve.scalar_tensor_tensor(J[:], F[:, 0, :], float(E), F[:, 1, :], ALU.mult, ALU.add))
                        do(lambda: dve.tensor_scalar(IDX[:, slot, :], J[:], tb[:, 0:1], None, ALU.add))
                        do(lambda: dve.tensor_tensor(WT[:, 0, :, :], WT[:, 0, :, :],
                                                     mask[:].unsqueeze(1).to_broadcast([P, 2, NG]), ALU.mult))
                        do(lambda: dve.tensor_tensor(
                            W4[:, slot, :].rearrange("p (n y x) -> p n y x", y=2, x=2),
                            WT[:, 0, :, :].rearrange("p y n -> p n y").unsqueeze(3).to_broadcast([P, NG, 2, 2]),
                            WT[:, 1, :, :].rearrange("p x n -> p n x").unsqueeze(2).to_broadcast([P, NG, 2, 2]),
                            ALU.mult))

                    def chunk(pT, pG, c):
                        doT, doG = pT is not None, pG is not None
                        if doT:
                            gT = NCH * pT + c
                        if doG:
                            gG = NCH * pG + c
                            dve.wait_ge(s_math, NM * gG + (NM + CREDIT))
                            dve.wait_ge(s_mix, 3 * NG * gG + CREDIT)
                            dve.tensor_copy(w_now[:], W4[:, gG % (2 * NCH), :]).then_inc(s_wnow, 1)
                            dve.wait_ge(s_wnow, gG + 1)
                        for k in range(TAPS):
                            if doG:
                                for t in range(0, NT, 2):
                                    first = 3 * (NT * k + t)
                                    for corner in range(1, 4):
                                        for j in range(2):
                                            m = NT * k + t + j
                                            if corner == 1:
                                                dve.wait_ge(s_r0, NG * gG + (m + 1))
                                            else:
                                                dve.wait_ge(s_mix, 3 * NG * gG + (first + 2 * (corner - 2) + j + 1 + CREDIT))
                                            dve.scalar_tensor_tensor(
                                                R[:, k % 3, t + j, :], ring[:, m % RING, corner * P:(corner + 1) * P],
                                                w_now[:, 4 * m + corner:4 * m + corner + 1], R[:, k % 3, t + j, :],
                                                ALU.mult, ALU.add).then_inc(s_mix, 1)
                            if doT and k == 7:
                                indices(pT, gT, c)
                        if doG:
                            dve.wait_ge(s_out, gG + (1 + CREDIT))
                            dve.bn_stats(G.stats[:, pG, c, :], G.X[:, pG, bass.ds(CH * c, CH)]).then_inc(s_st, 1)
                    passes(dve, chunk, next_table)
                    dve.wait_ge(s_st, B * NCH)

        HB = HW // 2
        mv = sb("b_mv", [P, 2])
        std = sb("b_std", [P, 1])
        scale, shift = sb("b_scale", [P, 1]), sb("b_shift", [P, 1])
        x3 = sb("b_x3", [P, 4, HB])
        z = sb("b_z", [P, 2, HB])
        s_step, s_std, s_z, s_y = (sem(n) for n in ("b_step", "b_std_done", "b_z", "b_y"))
        s_x3 = [sem(f"b_x3_landed{i}") for i in range(4)]
        s_sum, s_stored = sem("b_sum"), sem("b_stored")
        with nc.Block() as block:
            @block.vector
            def _(dve):
                dve.bn_aggr(mv[:], G.stats[:].rearrange("p b c s -> p (b c s)")).then_inc(s_step, 1)
                dve.wait_ge(s_std, 1)
                dve.reciprocal(scale[:], std[:]).then_inc(s_step, 1)
                dve.wait_ge(s_step, 2)
                dve.tensor_tensor(scale[:], scale[:], vecs[:, 1:2], ALU.mult).then_inc(s_step, 1)
                dve.wait_ge(s_step, 3)
                dve.tensor_tensor(mv[:, 1:2], mv[:, 0:1], scale[:], ALU.mult).then_inc(s_step, 1)
                dve.wait_ge(s_step, 4)
                dve.tensor_tensor(shift[:], vecs[:, 2:3], mv[:, 1:2], ALU.subtract).then_inc(s_step, 1)
                for n in range(2 * B):
                    b, h = n // 2, n % 2
                    dve.wait_ge(s_z, n + 1)
                    x = G.X[:, b, h * HB:(h + 1) * HB]
                    dve.scalar_tensor_tensor(x, z[:, n % 2, :], 0.1, z[:, n % 2, :], ALU.mult, ALU.max).then_inc(s_y, 1)
                    dve.wait_ge(s_y, n + 1)
                    dve.wait_ge(s_x3[n % 4], 16 * (n // 4 + 1))
                    dve.tensor_tensor(x, x, x3[:, n % 4, :], ALU.add).then_inc(s_sum, 1)

            @block.scalar
            def _(act):
                act.wait_ge(s_step, 1)
                act.activation(std[:], mv[:, 1:2], ACT.Sqrt, bias=G.eps5[:, 0:1]).then_inc(s_std, 1)
                act.wait_ge(s_step, 5)
                for n in range(2 * B):
                    b, h = n // 2, n % 2
                    if n >= 2:
                        act.wait_ge(s_y, n - 1)
                    act.activation(z[:, n % 2, :], G.X[:, b, h * HB:(h + 1) * HB], ACT.Identity,
                                   bias=shift[:, 0:1], scale=scale[:, 0:1]).then_inc(s_z, 1)

            @block.gpsimd
            def _(pool):
                for n in range(2 * B):
                    b, h = n // 2, n % 2
                    if n >= 4:
                        pool.wait_ge(s_sum, n - 3)
                    pool.dma_start(x3[:, n % 4, :], x3_dram[b][:, h * HB:(h + 1) * HB]).then_inc(s_x3[n % 4], 16)

            @block.sync
            def _(sp):
                for n in range(2 * B):
                    b, h = n // 2, n % 2
                    sp.wait_ge(s_sum, n + 1)
                    sp.dma_start(out[b][:, h * HB:(h + 1) * HB], G.X[:, b, h * HB:(h + 1) * HB]).then_inc(s_stored, 16)
                sp.wait_ge(s_stored, 16 * 2 * B)


def build_program(nc, d, out):
    class G:
        pass
    G.d = d
    x3 = nc.dram_tensor("x3_scratch", (B, P, HW), F32).ap()
    with ExitStack() as ctx:
        def sb(name, shape, dt=F32):
            return ctx.enter_context(nc.sbuf_tensor(name, shape, dt))
        G.X = sb("X", [P, B, HW])
        G.stats = sb("stats", [P, B, NCH, 6])
        G.small = sb("small", [P, 4 * P + 32])
        G.ident = G.small[:, 0:P]
        G.group_mean = G.small[:, P:2 * P]
        G.mean64 = G.small[:, 2 * P:3 * P]
        G.centre = G.small[:, 3 * P:4 * P]
        G.pick = G.small[:, 4 * P:4 * P + 32]
        G.eps5 = sb("eps5", [P, 1])
        G.rstd = sb("rstd", [P, B])
        G.shift = sb("shift", [P, B])
        load_image_and_statistics(nc, G, d["x"])
        for n, stage in (("L0", lambda: layer0(nc, G)), ("L1", lambda: layer1(nc, G)),
                         ("L2", lambda: layer2(nc, G, x3)), ("L3", lambda: layer3(nc, G, x3, out))):
            G.tag = n
            group_norm_scales(nc, ctx, G)
            stage()


def lay_out(i):
    def c(a):
        return np.ascontiguousarray(a)
    small, base = host_constants()
    o = {"x": c(i["x"].reshape(B, P, HW)), "small": small, "base": base}
    o["conv_w"] = c(i["L0_conv_conv_w"].transpose(1, 2, 3, 0).reshape(HALF, TAPS, HALF))
    o["conv_b"] = c(i["L0_conv_conv_b"].reshape(HALF, 1))
    o["expand_wT"] = c(i["L0_conv_expand_w"].T)
    o["concat_w"] = c(i["L0_conv_concat_w"])
    o["concat_b"] = c(i["L0_conv_concat_b"].reshape(HALF, 1))
    o["ln_g"] = c(i["L0_conv_ln_g"].reshape(HALF, 1))
    o["ln_b"] = c(i["L0_conv_ln_b"].reshape(HALF, 1))
    o["in_w"] = c(i["L0_conv_in_w"])
    o["in_b"] = c(i["L0_conv_in_b"].reshape(2, P).T)
    o["conv1d_w"] = c(i["L0_conv_conv1d_w"].T)
    o["conv1d_b"] = c(i["L0_conv_conv1d_b"].reshape(P, 1))
    o["xproj_w"] = c(i["L0_conv_xproj_w"])
    o["xproj_dtT"] = c(i["L0_conv_xproj_w"][:, :4].T)
    o["dt_w"] = c(i["L0_conv_dt_w"])
    o["dt_b"] = c(i["L0_conv_dt_b"].reshape(P, 1))
    o["A_log"] = c(i["L0_conv_A_log"])
    o["D_ssm"] = c(i["L0_conv_D_ssm"].reshape(P, 1))
    o["out_w"] = c(i["L0_conv_out_w"])
    o["out_b"] = c(i["L0_conv_out_b"].reshape(HALF, 1))
    for n in ("down", "up", "right", "left"):
        o[f"w_{n}"] = c(i[f"L1_conv_w_{n}"].transpose(1, 2, 0).reshape(P, TAPS * P))
    o["l2_w1"] = c(i["L2_conv_w1"][..., 0].transpose(1, 2, 0))
    o["l2_w3"] = c(i["L2_conv_w3"][:, 0, :, 0].T.reshape(1, 3 * P))
    o["l2_w4"] = c(i["L2_conv_w4"][:, :, 0, :])
    o["off_w"] = c(i["L3_conv_offset_w"].transpose(1, 2, 3, 0).reshape(P, TAPS, 3 * TAPS))
    o["off_b"] = c(i["L3_conv_offset_b"].reshape(3 * TAPS, 1))
    o["dcn_w"] = c(i["L3_conv_dcn_w"].transpose(1, 2, 3, 0).reshape(P, TAPS, P))
    for n in ("dcn_b", "gamma", "beta"):
        o[n] = c(i[f"L3_conv_{n}"].reshape(P, 1))
    return o


def kernel(**inputs):
    import concourse.bacc as _bacc
    from concourse.bass_utils import run_bass_kernel_spmd as _run

    nc = _bacc.Bacc("TRN2", target_bir_lowering=False, num_devices=1, dynamic_dma_scratch_size=4096)
    arrays = lay_out({k: np.asarray(v) for k, v in inputs.items()})
    d = {k: nc.dram_tensor(f"in_{k}", a.shape, mybir.dt.from_np(a.dtype), kind="ExternalInput").ap()
         for k, a in arrays.items()}
    out = nc.dram_tensor("out_dram", (B, P, HW), F32, kind="ExternalOutput").ap()
    build_program(nc, d, out)
    r = _run(nc, [{f"in_{k}": a for k, a in arrays.items()}], core_ids=[0])
    return r.results[0]["out_dram"].reshape(B, P, H, W)
```

```python
from contextlib import ExitStack

import concourse.bass as bass
import numpy as np
from concourse import mybir

F32 = mybir.dt.float32
F32R = mybir.dt.float32r
U32 = mybir.dt.uint32
ALU = mybir.AluOpType
ACT = mybir.ActivationFunctionType
AX_X = mybir.AxisListType.X

P = 128
B, H, W = 8, 64, 64
HW = H * W
CH = 512
NCH = HW // CH
ROWS = CH // W
HALF = 64
NS = 16
PADH, PADW = 3, 2
HP, WP = H + 2 * PADH, W + 2 * PADW
TAPS = 9
CREDIT = 32


def after(eng, sem, k, lag=0):
    eng.wait_ge(sem, k + (1 + CREDIT - lag))


def apart(eng, passed):
    eng.sem_inc(passed, 1)


def host_constants():
    ident = np.eye(P, dtype=np.float32)
    group_mean = np.kron(np.eye(P // 4), np.full((4, 4), 0.25)).astype(np.float32)
    mean64 = np.zeros((P, P), np.float32)
    mean64[:HALF, :] = 1.0 / HALF
    centre = np.zeros((P, P), np.float32)
    centre[:HALF, :HALF] = np.eye(HALF) - 1.0 / HALF
    pick = np.zeros((P, 32), np.float32)
    for k in range(64):
        pick[k, k % 32] = 1.0
    small = np.concatenate([ident, group_mean, mean64, centre, pick], axis=1)
    p = np.arange(P)
    base = np.zeros((P, 2, NCH, TAPS, 4), np.float32)
    for t in range(HW // P):
        for k in range(TAPS):
            base[:, 0, t // 4, k, t % 4] = 2 * t + p // W + k // 3
            base[:, 1, t // 4, k, t % 4] = p % W + k % 3
    return small, base.reshape(P, -1)


def group_norm_scales(nc, ctx_outer, G):
    with ExitStack() as ctx:
        def sem(name):
            return ctx.enter_context(nc.semaphore(f"{name}_{G.tag}"))
        tag = G.tag
        mv = ctx.enter_context(nc.sbuf_tensor(f"gn_mv{tag}", [P, B, 2], F32))
        moments = ctx.enter_context(nc.sbuf_tensor(f"gn_moments{tag}", [P, 2, B], F32))
        mean = ctx.enter_context(nc.sbuf_tensor(f"gn_mean{tag}", [P, 2, B], F32))
        var = ctx.enter_context(nc.sbuf_tensor(f"gn_var{tag}", [P, B], F32))
        ps = ctx.enter_context(nc.psum_tensor(f"gn_ps{tag}", [P, 2, B], F32))
        s_step, s_ps, s_std = sem("gn_step"), sem("gn_group_moments"), sem("gn_std")
        with nc.Block() as block:
            @block.vector
            def _(dve):
                for b in range(B):
                    nc.vector.bn_aggr(mv[:, b, :], G.stats[:, b, :, :].rearrange("p c s -> p (c s)")).then_inc(s_step, 1)
                dve.wait_ge(s_step, B)
                nc.vector.tensor_copy(moments[:, 0, :], mv[:, :, 0]).then_inc(s_step, 1)
                nc.vector.tensor_tensor(var[:], mv[:, :, 0], mv[:, :, 0], ALU.mult).then_inc(s_step, 1)
                dve.wait_ge(s_step, B + 2)
                nc.vector.tensor_tensor(moments[:, 1, :], mv[:, :, 1], var[:], ALU.add).then_inc(s_step, 1)
                dve.wait_ge(s_ps, 1)
                nc.vector.tensor_copy(mean[:], ps[:]).then_inc(s_step, 1)
                dve.wait_ge(s_step, B + 4)
                nc.vector.tensor_tensor(var[:], mean[:, 0, :], mean[:, 0, :], ALU.mult).then_inc(s_step, 1)
                dve.wait_ge(s_step, B + 5)
                nc.vector.tensor_tensor(mean[:, 1, :], mean[:, 1, :], var[:], ALU.subtract).then_inc(s_step, 1)
                dve.wait_ge(s_std, 1)
                nc.vector.reciprocal(G.rstd[:], mv[:, :, 0]).then_inc(s_step, 1)
                dve.wait_ge(s_step, B + 7)
                nc.vector.scalar_tensor_tensor(G.shift[:], mean[:, 0, :], -1.0, G.rstd[:], ALU.mult, ALU.mult).then_inc(s_step, 1)
                dve.wait_ge(s_step, B + 8)

            @block.tensor
            def _(pe):
                pe.wait_ge(s_step, B + 3)
                nc.tensor.matmul(ps[:].rearrange("p a b -> p (a b)"), G.group_mean, moments[:].rearrange("p a b -> p (a b)"),
                                 start=True, stop=True).then_inc(s_ps, 1)

            @block.scalar
            def _(act):
                act.wait_ge(s_step, B + 6)
                nc.scalar.activation(mv[:, :, 0], mean[:, 1, :], ACT.Sqrt, bias=G.eps5[:, 0:1]).then_inc(s_std, 1)


def load_image_and_statistics(nc, G, x_dram):
    with ExitStack() as ctx:
        s_x = [ctx.enter_context(nc.semaphore(f"x_landed{b}")) for b in range(B)]
        s_c = ctx.enter_context(nc.semaphore("constants_landed"))
        s_st = ctx.enter_context(nc.semaphore("load_stats_done"))
        with nc.Block() as block:
            @block.sync
            def _(sp):
                sp.dma_start(G.small[:], G.d["small"]).then_inc(s_c, 16)
                for b in range(B):
                    sp.dma_start(G.X[:, b, :], x_dram[b]).then_inc(s_x[b], 16)
                sp.wait_ge(s_c, 16)

            @block.vector
            def _(dve):
                nc.vector.memset(G.eps5[:], 1e-5).then_inc(s_st, 1)
                for b in range(B):
                    dve.wait_ge(s_x[b], 16)
                    for c in range(NCH):
                        nc.vector.bn_stats(G.stats[:, b, c, :], G.X[:, b, c * CH:(c + 1) * CH]).then_inc(s_st, 1)
                dve.wait_ge(s_st, 1 + B * NCH)


def layer1(nc, G, x1_dram):
    NG, NI, PAD, LINES = 2, 4, TAPS // 2, H - 1
    NB = 3
    ON_POOL = (1, 4, 6)
    with ExitStack() as ctx:
        def sb(name, shape, dt=F32):
            return ctx.enter_context(nc.sbuf_tensor(name, shape, dt))

        def sem(name):
            return ctx.enter_context(nc.semaphore(name))
        raw = sb("prop_raw", [P, TAPS * P])
        w_hi = sb("prop_w_hi", [P, 2, TAPS * P], F32R)
        w_lo = sb("prop_w_lo", [P, 2, TAPS * P], F32R)
        hi = [sb(f"prop_hi{s}", [P, NI, W + 2 * PAD], F32R) for s in range(NG)]
        lo = [sb(f"prop_lo{s}", [P, NI, W + 2 * PAD], F32R) for s in range(NG)]
        zero = sb("prop_zero", [P, NI, PAD])
        x1 = sb("prop_x1", [P, NB, HW])
        ps = [ctx.enter_context(nc.psum_tensor(f"prop_ps{s}", [P, NI, W], F32)) for s in range(NG)]
        s_zero, s_edge, s_norm = sem("p_zero"), sem("p_edges_zero"), sem("p_S_normed")
        s_raw, s_whi, s_wlo = sem("p_raw_landed"), sem("p_w_hi"), sem("p_w_lo")
        s_conv = [sem(f"p_conv{s}") for s in range(NG)]
        s_new = [sem(f"p_new{s}") for s in range(NG)]
        s_hi = [sem(f"p_hi{s}") for s in range(NG)]
        s_lo = [sem(f"p_lo{s}") for s in range(NG)]
        s_x1 = [sem(f"p_x1_landed{i}") for i in range(NB)]
        s_add = [sem("p_added_dve"), sem("p_added_pool")]
        s_stat = sem("p_stats")
        XV = G.X[:].rearrange("p b (h w) -> p b h w", h=H)
        names = ["w_down", "w_up", "w_right", "w_left"]

        def line(d, s, t):
            idx = t if d % 2 == 0 else t * -1 + (H - 1)
            if d < 2:
                return XV[:, NI * s:NI * s + NI, idx, :]
            return XV[:, NI * s:NI * s + NI, :, idx]

        def adder(b):
            p = b in ON_POOL
            return int(p), sum((i in ON_POOL) == p for i in range(b + 1))

        with nc.Block() as block:
            @block.sync
            def _(sp):
                sp.dma_start(raw[:], G.d[names[0]]).then_inc(s_raw, 16)
                for b in range(NB):
                    sp.dma_start(x1[:, b, :], x1_dram[:, b * HW:(b + 1) * HW]).then_inc(s_x1[b], 16)
                for d in range(1, 4):
                    sp.wait_ge(s_wlo, d)
                    sp.dma_start(raw[:], G.d[names[d]]).then_inc(s_raw, 16)
                for b in range(NB, B):
                    who, n = adder(b - NB)
                    sp.wait_ge(s_add[who], n)
                    sp.dma_start(x1[:, b % NB, :], x1_dram[:, b * HW:(b + 1) * HW]).then_inc(s_x1[b % NB], 16)

            @block.gpsimd
            def _(pool):
                pool.memset(zero[:].rearrange("p a b -> p (a b)"), 0.0).then_inc(s_zero, 1)
                for d in range(4):
                    pool.wait_ge(s_whi, d + 1)
                    pool.tensor_tensor(w_lo[:, d % 2, :], raw[:], w_hi[:, d % 2, :].bitcast(F32), ALU.subtract).then_inc(s_wlo, 1)
                for b in ON_POOL:
                    pool.wait_ge(s_new[b // NI], 4 * LINES)
                    pool.wait_ge(s_hi[b // NI], 4 * H)
                    pool.wait_ge(s_lo[b // NI], 4 * H)
                    pool.wait_ge(s_x1[b % NB], 16 * (b // NB + 1))
                    pool.tensor_tensor(G.X[:, b, :], G.X[:, b, :], x1[:, b % NB, :], ALU.add).then_inc(s_add[1], 1)

            @block.scalar
            def _(act):
                act.wait_ge(s_zero, 1)
                for buf in hi + lo:
                    for side in (0, PAD + W):
                        act.activation(buf[:, :, side:side + PAD], zero[:], ACT.Copy).then_inc(s_edge, 1)

                def split(d):
                    if d >= 2:
                        for s in range(NG):
                            act.wait_ge(s_conv[s], LINES * (d - 1))
                    act.wait_ge(s_raw, 16 * (d + 1))
                    act.activation(w_hi[:, d % 2, :], raw[:], ACT.Copy).then_inc(s_whi, 1)
                split(0)
                for b in (0, 1, 4, 5):
                    act.activation(G.X[:, b, :], G.X[:, b, :], ACT.Identity, bias=G.shift[:, b:b + 1],
                                   scale=G.rstd[:, b:b + 1]).then_inc(s_norm, 1)

                def round_line(d, t, s):
                    act.activation(hi[s][:, :, PAD:PAD + W], line(d, s, t), ACT.Copy).then_inc(s_hi[s], 1)
                for d in range(4):
                    for s in range(NG):
                        if d == 0:
                            act.wait_ge(s_norm, 8)
                        else:
                            act.wait_ge(s_new[s], LINES * d)
                            act.wait_ge(s_lo[s], H * d)
                        round_line(d, 0, s)
                    if d + 1 < 4:
                        split(d + 1)
                    with act.Fori(1, H) as t:
                        for s in range(NG):
                            act.wait_ge(s_new[s], t + LINES * d)
                            round_line(d, t, s)

            @block.tensor
            def _(pe):
                pe.wait_ge(s_edge, 8)
                for d in range(4):
                    pe.wait_ge(s_wlo, d + 1)
                    with pe.Fori(1, H) as t:
                        for s in range(NG):
                            for n, (wt, part, ready) in enumerate(((w_hi, hi[s], s_hi[s]), (w_lo, hi[s], None),
                                                                   (w_hi, lo[s], s_lo[s]))):
                                if ready:
                                    pe.wait_ge(ready, t + H * d)
                                for k in range(TAPS):
                                    mm = pe.matmul(ps[s][:], wt[:, d % 2, k * P:(k + 1) * P], part[:, :, k:k + W],
                                                   start=(n == 0 and k == 0), stop=(n == 2 and k == TAPS - 1))
                            mm.then_inc(s_conv[s], 1)

            @block.vector
            def _(dve):
                for b in (2, 3, 6, 7):
                    dve.tensor_scalar(G.X[:, b, :], G.X[:, b, :], G.rstd[:, b:b + 1], G.shift[:, b:b + 1],
                                      ALU.mult, ALU.add).then_inc(s_norm, 1)

                def rest_of_line(d, t, s):
                    dve.wait_ge(s_hi[s], t + (1 + H * d))
                    dve.tensor_tensor(lo[s][:, :, PAD:PAD + W], line(d, s, t), hi[s][:, :, PAD:PAD + W].bitcast(F32),
                                      ALU.subtract).then_inc(s_lo[s], 1)
                for d in range(4):
                    for s in range(NG):
                        rest_of_line(d, 0, s)
                    with dve.Fori(1, H) as t:
                        for s in range(NG):
                            dve.wait_ge(s_conv[s], t + LINES * d)
                            dve.scalar_tensor_tensor(line(d, s, t), ps[s][:], 0.0, line(d, s, t), ALU.max,
                                                     ALU.add).then_inc(s_new[s], 1)
                            rest_of_line(d, t, s)
                for s in range(NG):
                    dve.wait_ge(s_lo[s], 4 * H)
                for b in range(B):
                    who, n = adder(b)
                    if not who:
                        dve.wait_ge(s_x1[b % NB], 16 * (b // NB + 1))
                        dve.tensor_tensor(G.X[:, b, :], G.X[:, b, :], x1[:, b % NB, :], ALU.add).then_inc(s_add[0], 1)
                    dve.wait_ge(s_add[who], n)
                    for c in range(NCH):
                        dve.bn_stats(G.stats[:, b, c, :], G.X[:, b, c * CH:(c + 1) * CH]).then_inc(s_stat, 1)
                dve.wait_ge(s_stat, B * NCH)


def layer2(nc, G, x3_dram):
    K1, K3, GT = 5, 3, 3
    K7 = K1 + K3 - 1
    with ExitStack() as ctx:
        def sb(name, shape, dt=F32):
            return ctx.enter_context(nc.sbuf_tensor(name, shape, dt))

        def sem(name):
            return ctx.enter_context(nc.semaphore(name))
        w1 = sb("l2_w1", [P, K1, P])
        w3 = sb("l2_w3", [P, K3, P])
        w7 = sb("l2_w7", [P, K7, P])
        edge = sb("l2_edge", [P, 4, P])
        tmp = sb("l2_tmp", [P, P])
        w4g = sb("l2_w4g", [P, GT, 8])
        w4 = sb("l2_w4", [P, GT, P])
        xn = [sb(f"l2_xn{i}", [P, HP, WP]) for i in range(2)]
        gate = sb("l2_gate", [P, 2, CH])
        prod = sb("l2_prod", [P, 2, CH])
        ps3 = ctx.enter_context(nc.psum_tensor("l2_ps3", [P, 2, CH], F32))
        ps4 = ctx.enter_context(nc.psum_tensor("l2_ps4", [P, 2, CH], F32))
        s_ld, s_w, s_xn = sem("c_weights_landed"), sem("c_weights_made"), sem("c_xn_ready")
        s_t3, s_t4, s_gate, s_prod = sem("c_conv_done"), sem("c_gate_summed"), sem("c_gate_copied"), sem("c_product")
        s_x, s_st, s_out = sem("c_x_updated"), sem("c_stats"), sem("c_x_stored")
        XV = G.X[:].rearrange("p b (h w) -> p b h w", h=H)

        with nc.Block() as block:
            @block.sync
            def _(sp):
                sp.dma_start(w1[:], G.d["l2_w1"]).then_inc(s_ld, 16)
                sp.dma_start(w3[:].rearrange("p a o -> p (a o)"), G.d["l2_w3"].to_broadcast([P, K3 * P])).then_inc(s_ld, 16)
                sp.dma_start(w4g[:], G.d["l2_w4"]).then_inc(s_ld, 16)
                with sp.Fori(0, B) as b:
                    sp.wait_ge(s_x, b * NCH + NCH)
                    sp.dma_start(x3_dram[b], G.X[:, b, :]).then_inc(s_out, 16)
                sp.wait_ge(s_out, 16 * B)

            @block.gpsimd
            def _(pool):
                for i in range(2):
                    pool.memset(xn[i][:].rearrange("p a b -> p (a b)"), 0.0).then_inc(s_w, 1)
                pool.wait_ge(s_ld, 48)
                n = 2

                def done(ins):
                    nonlocal n
                    n += 1
                    ins.then_inc(s_w, 1)
                    pool.wait_ge(s_w, n)
                for j in range(K7):
                    first = True
                    for a in range(K3):
                        if 0 <= j - a < K1:
                            dst = w7[:, j, :] if first else tmp[:]
                            done(pool.tensor_tensor(dst, w1[:, j - a, :], w3[:, a, :], ALU.mult))
                            if not first:
                                done(pool.tensor_tensor(w7[:, j, :], w7[:, j, :], tmp[:], ALU.add))
                            first = False
                for e, (a, b1) in enumerate([(0, 3), (0, 4), (2, 0), (2, 1)]):
                    done(pool.tensor_tensor(tmp[:], w1[:, b1, :], w3[:, a, :], ALU.mult))
                    done(pool.tensor_scalar(edge[:, e, :], tmp[:], -1.0, None, ALU.mult))
                for k in range(GT):
                    done(pool.tensor_copy(w4[:, k, :].rearrange("p (r g) -> p r g", g=8),
                                          w4g[:, k:k + 1, :].to_broadcast([P, P // 8, 8])))
                pool.sem_inc(s_w, 100)
                with pool.Fori(0, B) as b:
                    for c in range(NCH):
                        g = b * NCH + c
                        pool.wait_ge(s_prod, g + 1)
                        xc = G.X[:, b, c * CH:(c + 1) * CH]
                        pool.tensor_tensor(xc, xc, prod[:, c % 2, :], ALU.add).then_inc(s_x, 1)

            @block.scalar
            def _(act):
                act.wait_ge(s_w, 100)

                def norm(b):
                    bb = b % 2
                    act.activation(xn[bb][:, PADH:PADH + H, PADW:PADW + W], XV[:, b, :, :], ACT.Identity,
                                   bias=G.shift[:, b:b + 1], scale=G.rstd[:, b:b + 1]).then_inc(s_xn, 1)
                norm(0)
                for b in range(B):
                    if b + 1 < B:
                        if b:
                            act.wait_ge(s_t3, b * NCH)
                        norm(b + 1)
                    for c in range(NCH):
                        g = b * NCH + c
                        act.wait_ge(s_t4, g + 1)
                        if g >= 2:
                            act.wait_ge(s_prod, g - 1)
                        act.activation(gate[:, c % 2, :], ps4[:, c % 2, :], ACT.Copy).then_inc(s_gate, 1)

            @block.tensor
            def _(pe):
                pe.wait_ge(s_w, 100)
                for b in range(B):
                    pe.wait_ge(s_xn, b + 1)
                    x = xn[b % 2]
                    for c in range(NCH):
                        g = b * NCH + c
                        if g >= 2:
                            pe.wait_ge(s_prod, g - 1)
                        o3 = ps3[:, c % 2, :].rearrange("p (h w) -> p h w", w=W)
                        o4 = ps4[:, c % 2, :].rearrange("p (h w) -> p h w", w=W)
                        r = c * ROWS
                        for k in range(GT):
                            mm = pe.matmul(o4, w4[:, k, :], x[:, PADH + r:PADH + r + ROWS, 2 * k:2 * k + W],
                                           start=(k == 0), stop=(k == GT - 1))
                        mm.then_inc(s_t4, 1)
                        for j in range(K7):
                            if j == K7 - 1 and c == 0:
                                for e, row in ((0, 0), (1, 1)):
                                    pe.matmul(o3[:, 0, :], edge[:, e, :], x[:, PADH + row, PADW:PADW + W],
                                              start=False, stop=False, skip_group_check=True)
                            if j == K7 - 1 and c == NCH - 1:
                                for e, row in ((2, H - 2), (3, H - 1)):
                                    pe.matmul(o3[:, ROWS - 1, :], edge[:, e, :], x[:, PADH + row, PADW:PADW + W],
                                              start=False, stop=False, skip_group_check=True)
                            mm = pe.matmul(o3, w7[:, j, :], x[:, r + j:r + j + ROWS, PADW:PADW + W],
                                           start=(j == 0), stop=(j == K7 - 1), skip_group_check=True)
                        mm.then_inc(s_t3, 1)

            @block.vector
            def _(dve):
                for b in range(B):
                    for c in range(NCH):
                        g = b * NCH + c
                        dve.wait_ge(s_t3, g + 1)
                        dve.wait_ge(s_gate, g + 1)
                        if g >= 2:
                            dve.wait_ge(s_x, g - 1)
                        dve.tensor_tensor(prod[:, c % 2, :], ps3[:, c % 2, :], gate[:, c % 2, :], ALU.mult).then_inc(s_prod, 1)
                        if g >= 1:
                            bb, cc = (g - 1) // NCH, (g - 1) % NCH
                            dve.wait_ge(s_x, g)
                            dve.bn_stats(G.stats[:, bb, cc, :], G.X[:, bb, cc * CH:(cc + 1) * CH]).then_inc(s_st, 1)
                dve.wait_ge(s_x, B * NCH)
                dve.bn_stats(G.stats[:, B - 1, NCH - 1, :], G.X[:, B - 1, (NCH - 1) * CH:]).then_inc(s_st, 1)
                dve.wait_ge(s_st, B * NCH)


def layer0_weights(nc, G, T):
    with ExitStack() as ctx:
        def sb(name, shape, dt=F32):
            return ctx.enter_context(nc.sbuf_tensor(name, shape, dt))
        expand = sb("w_expand", [P, HALF])
        concat = sb("w_concat", [P, HALF])
        folded = sb("w_folded", [P, P])
        in_raw = sb("w_in_raw", [P, 2 * P])
        cols = sb("w_cols", [P, 16])
        xproj = sb("w_xproj", [P, 36])
        xdt = sb("w_xdt", [4, P])
        dtw = sb("w_dtw", [4, P])
        ps = ctx.enter_context(nc.psum_tensor("w_ps", [P, 8, P], F32))
        s_zero, s_ld, s_mm, s_v = [ctx.enter_context(nc.semaphore(f"w0_{n}")) for n in ("zero", "landed", "products", "made")]
        concat_b, ln_g, ln_b, out_b, d_ssm = (cols[:, k:k + 1] for k in range(5))
        c1w = cols[:, 5:8]
        with nc.Block() as block:
            @block.gpsimd
            def _(pool):
                for t in (T.conv, folded, in_raw, cols, T.bc, T.out, T.fin_b, T.dt_b):
                    flat = t[:] if len(t.shape) == 2 else t[:].rearrange("p a b -> p (a b)")
                    pool.memset(flat, 0.0).then_inc(s_zero, 1)
                pool.memset(T.one[:], 1.0).then_inc(s_zero, 1)
                pool.memset(T.zero[:], 0.0).then_inc(s_zero, 1)

            @block.sync
            def _(sp):
                sp.wait_ge(s_zero, 10)
                loads = [(expand[:], "expand_wT"), (concat[:], "concat_w"), (in_raw[0:HALF, :], "in_w"),
                         (concat_b[0:HALF, :], "concat_b"), (ln_g[0:HALF, :], "ln_g"), (ln_b[0:HALF, :], "ln_b"),
                         (out_b[0:HALF, :], "out_b"), (d_ssm, "D_ssm"), (c1w, "conv1d_w"), (T.conv1d_b[:], "conv1d_b"),
                         (xproj[:], "xproj_w"), (xdt[:], "xproj_dtT"), (dtw[:], "dt_w"), (T.dt_b[:], "dt_b"),
                         (T.A[:], "A_log"), (T.out[:, 0:HALF], "out_w"), (T.in_b[:], "in_b"),
                         (T.conv[HALF:P, :, HALF:P], "conv_w"), (T.fin_b[HALF:P, :], "conv_b"),
                         (T.fin_b[0:HALF, :], "concat_b")]
                for dst, name in loads:
                    sp.dma_start(dst, G.d[name]).then_inc(s_ld, 16)
                sp.wait_ge(s_ld, 16 * len(loads))
                sp.sem_inc(s_ld, 1000)

            @block.tensor
            def _(pe):
                pe.wait_ge(s_ld, 1000)
                pe.matmul(ps[0:HALF, 0, 0:HALF], concat[:], expand[:], start=True, stop=True).then_inc(s_mm, 1)
                pe.matmul(ps[0:HALF, 4, 0:HALF], expand[:], concat[:], start=True, stop=True).then_inc(s_mm, 1)
                pe.wait_ge(s_v, 2)
                pe.matmul(ps[:, 0, :], folded[:], G.centre, start=True, stop=True).then_inc(s_mm, 1)
                pe.matmul(ps[:, 4, 0:1], G.centre, concat_b, start=True, stop=True).then_inc(s_mm, 1)
                pe.wait_ge(s_v, 4)
                pe.matmul(ps[:, 0, :], xdt[:], dtw[:], start=True, stop=True).then_inc(s_mm, 1)
                for h in range(2):
                    pe.matmul(ps[:, 4, h:h + 1], in_raw[:, h * P:(h + 1) * P], ln_b, start=True, stop=True).then_inc(s_mm, 1)

            @block.scalar
            def _(act):
                act.wait_ge(s_ld, 1000)
                act.activation(T.A[:], T.A[:], ACT.Exp).then_inc(s_zero, 1)

            @block.vector
            def _(dve):
                dve.wait_ge(s_ld, 1000)
                dve.wait_ge(s_mm, 2)
                dve.tensor_copy(folded[0:HALF, 0:HALF], ps[0:HALF, 0, 0:HALF]).then_inc(s_v, 1)
                dve.tensor_copy(T.conv[0:HALF, TAPS // 2, 0:HALF], ps[0:HALF, 4, 0:HALF]).then_inc(s_v, 1)
                dve.wait_ge(s_mm, 4)
                dve.tensor_copy(T.centred[:], ps[:, 0, :]).then_inc(s_v, 1)
                dve.tensor_copy(T.centred_b[:], ps[:, 4, 0:1]).then_inc(s_v, 1)
                dve.wait_ge(s_mm, 7)
                dve.tensor_copy(T.dt[:], ps[:, 0, :]).then_inc(s_v, 1)
                dve.tensor_tensor(T.in_b[:], T.in_b[:], ps[:, 4, 0:2], ALU.add).then_inc(s_v, 1)
                dve.tensor_scalar(T.inw[:], in_raw[:], ln_g, None, ALU.mult).then_inc(s_v, 1)
                for k in range(3):
                    dve.tensor_scalar(T.conv1d[:, k, :], G.ident, c1w[:, k:k + 1], None, ALU.mult).then_inc(s_v, 1)
                dve.tensor_scalar(T.d_diag[:], G.ident, d_ssm, None, ALU.mult).then_inc(s_v, 1)
                for k in range(2):
                    dve.tensor_copy(T.bc[:, 32 * k:32 * k + 32], xproj[:, 4:36]).then_inc(s_v, 1)
                dve.tensor_copy(T.pick[:], G.pick).then_inc(s_v, 1)
                dve.tensor_tensor(T.fin_b[0:HALF, :], T.fin_b[0:HALF, :], out_b[0:HALF, :], ALU.add).then_inc(s_v, 1)
                dve.wait_ge(s_zero, 11)
                dve.tensor_scalar(T.A[:], T.A[:], -1.0, None, ALU.mult).then_inc(s_v, 1)
                dve.wait_ge(s_v, 16)


def layer0(nc, G, x1_dram):
    NDA = 8
    LEAD = 3
    with ExitStack() as ctx:
        def sb(name, shape, dt=F32):
            return ctx.enter_context(nc.sbuf_tensor(name, shape, dt))

        class T:
            pass
        T.conv = sb("m_conv", [P, TAPS, P])
        T.centred, T.dt, T.bc, T.out, T.d_diag = (sb(f"m_{n}", [P, P]) for n in ("centred", "dt", "bc", "out", "d"))
        T.inw = sb("m_inw", [P, 2 * P])
        T.conv1d = sb("m_conv1d", [P, 3, P])
        T.pick = sb("m_pick", [P, 32], F32R)
        T.A = sb("m_A", [P, NS])
        T.in_b = sb("m_in_b", [P, 2])
        T.centred_b, T.conv1d_b, T.dt_b, T.fin_b, T.one = (sb(f"m_{n}", [P, 1]) for n in ("cb", "c1b", "dtb", "finb", "one"))
        T.zero = sb("m_zero", [P, W + 2])
        layer0_weights(nc, G, T)

        xn = sb("m_xn", [P, 2, ROWS + 2, W + 2])
        xnc = sb("m_xnc", [P, CH])
        tc = sb("m_tc", [P, CH])
        sq = sb("m_sq", [P, CH])
        arg = sb("m_arg", [P, CH])
        ea = sb("m_ea", [P, CH])
        ln = sb("m_ln", [P, CH])
        rest = sb("m_rest", [P, CH])
        fin = sb("m_fin", [P, CH])
        xs = sb("m_xs", [P, 2 + CH])
        xc = sb("m_xc", [P, CH])
        dt = sb("m_dtv", [P, 2, CH])
        dtx = sb("m_dtx", [P, 2, CH])
        sz = sb("m_sz", [P, 2, CH])
        bcs = sb("m_bcs", [P, 2, CH], F32R)
        dA = sb("m_dA", [P, NDA, CH])
        hb = sb("m_hb", [P, 4, CH])
        hc = sb("m_hc", [P, 4, CH])
        hs = sb("m_hs", [P, 2, CH])
        state = sb("m_state", [P, NS])
        pf = [ctx.enter_context(nc.psum_tensor(f"m_pf{i}", [P, CH], F32)) for i in range(2)]
        pB = ctx.enter_context(nc.psum_tensor("m_pB", [P, 2, CH], F32))
        pC = ctx.enter_context(nc.psum_tensor("m_pC", [P, 2, CH], F32))
        pY = ctx.enter_context(nc.psum_tensor("m_pY", [P, CH], F32))
        pO = ctx.enter_context(nc.psum_tensor("m_pO", [P, CH], F32))
        XV = G.X[:].rearrange("p b (h w) -> p b h w", h=H)

        class s:
            pass
        credited = []

        def sem(name):
            q = ctx.enter_context(nc.semaphore("m_" + name))
            credited.append(q)
            return q
        s.p1, s.tc, s.sq, s.var, s.lnv, s.rstd, s.u = (sem(n) for n in ("p1", "tc", "sq", "var", "lnv", "rstd", "u"))
        s.halo, s.xs, s.z, s.xse, s.sz, s.cv, s.xc = (sem(n) for n in ("halo", "xs", "z", "xse", "sz", "cv", "xc"))
        s.dtp, s.bc, s.xb, s.abs, s.e, s.ln, s.bhi, s.blo = (sem(n) for n in ("dtp", "bc", "xb", "abs", "e", "ln", "bhi", "blo"))
        s.r1, s.r2, s.r3, s.dt, s.dtx = (sem(n) for n in ("rest1", "rest2", "rest3", "dt", "dtx"))
        s.dterm, s.y, s.out, s.fin, s.add, s.st = (sem(n) for n in ("dterm", "y", "out", "fin", "add", "stats"))
        s.B, s.C, s.dA, s.U, s.S, s.HC, s.state = (sem(n) for n in ("B", "C", "dA", "U", "S", "HC", "state"))
        s.pair, s.sum = sem("pair"), sem("sum")
        s.norm, s.xn, s.edge = sem("norm"), sem("xn"), sem("edge")
        s.border = sem("border")
        s.stored = ctx.enter_context(nc.semaphore("m_stored"))

        PE_AT = {1: ["scan input"], 2: ["gate input"], 3: ["convolve"], 6: ["centre"], 7: ["project dt"],
                 8: ["project B, C"], 9: ["variance"]}
        ACT_AT = {2: ["scan input"], 4: ["norm"], 5: ["silu"], 6: ["pad"], 7: ["centre"], 8: ["dt argument"],
                  9: ["round B, C"], 10: ["log", "deviation"]}
        POOL_AT = {0: ["halo"], 11: ["softplus"], 13: ["normalise"], 14: ["dt * x"]}
        DVE_AT = {10: ["rest of B, C", "softplus"], 13: ["dt"]}
        TWO_AHEAD = ("norm", "centre", "variance", "deviation", "normalise")
        CONV_AT = {7: 1, 9: 1, 10: 1, 11: 2, 12: 1, 13: 1, 14: 1, 15: 1}
        SUM_AT = {5: 0, 6: 1, 8: 2, 10: 3, 12: 4, 14: 5}
        LATE_SUM_AT = {0: 6, 2: 7}

        def front_pe(g, b, c, par, what):
            pe = nc.tensor
            if what == "centre":
                after(pe, s.norm, g)
                after(pe, s.xc, g, 1)
                pe.matmul(pf[0][:], T.centred[:], xnc[:], start=True, stop=True).then_inc(s.p1, 1)
            if what == "variance":
                after(pe, s.sq, g)
                after(pe, s.xb, g, 1)
                pe.matmul(pf[1][:], G.mean64, sq[:], start=True, stop=True).then_inc(s.var, 1)
            if what == "scan input":
                after(pe, s.u, g)
                after(pe, s.blo, g, 1)
                pe.matmul(pf[0][:], T.inw[:, 0:P], tc[:], start=True, stop=True).then_inc(s.xs, 1)
            if what == "gate input":
                after(pe, s.lnv, g)
                pe.matmul(pf[1][:], T.inw[:, P:2 * P], tc[:], start=True, stop=True).then_inc(s.z, 1)
            if what == "convolve":
                after(pe, s.xse, g)
                for j in range(3):
                    mm = pe.matmul(pf[0][:], T.conv1d[:, j, :], xs[:, j:j + CH], start=(j == 0), stop=(j == 2))
                mm.then_inc(s.cv, 1)
            if what == "project dt":
                after(pe, s.sz, g)
                after(pe, s.xc, g)
                pe.matmul(pf[1][:], T.dt[:], xc[:], start=True, stop=True).then_inc(s.dtp, 1)
            if what == "project B, C":
                after(pe, s.sq, g + 1)
                pe.matmul(pf[0][:], T.bc[:], xc[:], start=True, stop=True).then_inc(s.bc, 1)

        def front_act(g, b, c, par, what):
            act = nc.scalar
            bias, scale = G.shift[:, bass.ds(b, 1)], G.rstd[:, bass.ds(b, 1)]
            if what == "norm":
                after(act, s.p1, g, 1)
                act.activation(xnc[:].rearrange("p (h w) -> p h w", w=W), XV[:, b, bass.ds(c * ROWS, ROWS), :],
                               ACT.Identity, bias=bias, scale=scale).then_inc(s.norm, 1)
            if what == "pad":
                after(act, s.out, g, 2)
                top = isinstance(c, int) and c == 0
                bottom = isinstance(c, int) and c == NCH - 1
                if top or bottom:
                    act.activation(xn[:, par, 0 if top else ROWS + 1, :], T.zero[:], ACT.Copy).then_inc(s.edge, 1)
                first = 0 if top else c * ROWS - 1
                n = ROWS + 2 - top - bottom
                act.activation(xn[:, par, int(top):int(top) + n, 1:1 + W], XV[:, b, bass.ds(first, n), :],
                               ACT.Identity, bias=bias, scale=scale).then_inc(s.xn, 1)
            if what == "centre":
                after(act, s.p1, g)
                after(act, s.z, g, 1)
                after(act, s.u, g, 1)
                act.activation(tc[:], pf[0][:], ACT.Identity, bias=T.centred_b[:, 0:1]).then_inc(s.tc, 1)
                act.activation(sq[:], pf[0][:], ACT.Square, bias=T.centred_b[:, 0:1]).then_inc(s.sq, 1)
            if what == "deviation":
                after(act, s.var, g)
                act.activation(sq[:], pf[1][:], ACT.Ln, bias=G.eps5[:, 0:1]).then_inc(s.lnv, 1)
                after(act, s.lnv, g)
                act.activation(sq[:], sq[:], ACT.Exp, scale=-0.5).then_inc(s.rstd, 1)
            if what == "scan input":
                after(act, s.xs, g)
                after(act, s.halo, g)
                act.activation(xs[:, 2:2 + CH], pf[0][:], ACT.Identity, bias=T.in_b[:, 0:1]).then_inc(s.xse, 1)
            if what == "silu":
                after(act, s.z, g)
                after(act, s.out, g, 2)
                act.activation(sz[:, par, :], pf[1][:], ACT.Silu, bias=T.in_b[:, 1:2]).then_inc(s.sz, 1)
                after(act, s.cv, g)
                after(act, s.dterm, g, 1)
                after(act, s.dtx, g, 1)
                act.activation(xc[:], pf[0][:], ACT.Silu, bias=T.conv1d_b[:, 0:1]).then_inc(s.xc, 1)
            if what == "dt argument":
                after(act, s.dtp, g)
                after(act, s.dt, g, 1)
                act.activation(arg[:], pf[1][:], ACT.Identity, bias=T.dt_b[:, 0:1]).then_inc(s.xb, 1)
                after(act, s.xb, g)
                after(act, s.r3, g, 1)
                act.activation(ea[:], arg[:], ACT.Abs).then_inc(s.abs, 1)
                after(act, s.abs, g)
                act.activation(ea[:], ea[:], ACT.Exp, scale=-1.0).then_inc(s.e, 1)
            if what == "round B, C":
                after(act, s.bc, g)
                after(act, s.C, 16 * g - 16, 1)
                act.activation(bcs[:, par, :], pf[0][:], ACT.Copy).then_inc(s.bhi, 1)
            if what == "log":
                after(act, s.e, g)
                after(act, s.r3, g, 1)
                act.activation(ln[:], ea[:], ACT.Ln, bias=T.one[:, 0:1]).then_inc(s.ln, 1)

        def front_pool(g, b, c, par, what):
            pool = nc.gpsimd
            if what == "normalise":
                after(pool, s.tc, g)
                after(pool, s.rstd, g)
                pool.tensor_tensor(tc[:], tc[:], sq[:], ALU.mult).then_inc(s.u, 1)
            if what == "halo":
                after(pool, s.cv, g, 1)
                after(pool, s.xse, g, 1)
                after(pool, s.halo, g, 1)
                if isinstance(c, int) and c == 0:
                    pool.tensor_tensor(xs[:, 0:2], T.zero[:, 0:2], T.zero[:, 0:2], ALU.add).then_inc(s.halo, 1)
                else:
                    pool.tensor_tensor(xs[:, 0:2], xs[:, CH:CH + 2], T.one[:].to_broadcast([P, 2]), ALU.mult).then_inc(s.halo, 1)
            if what == "softplus":
                after(pool, s.r1, g)
                pool.tensor_tensor(rest[:], ea[:], rest[:], ALU.subtract).then_inc(s.r2, 1)
                after(pool, s.r2, g)
                after(pool, s.ln, g)
                pool.tensor_tensor(rest[:], rest[:], ln[:], ALU.add).then_inc(s.r3, 1)
            if what == "dt * x":
                after(pool, s.dt, g)
                after(pool, s.xc, g)
                after(pool, s.U, 16 * g - 16, 1)
                pool.tensor_tensor(dtx[:, par, :], dt[:, par, :], xc[:], ALU.mult).then_inc(s.dtx, 1)

        def front_dve(g, b, c, par, what):
            dve = nc.vector
            if what == "rest of B, C":
                after(dve, s.bhi, g)
                dve.tensor_tensor(bcs[32:64, par, :], pf[0][32:64, :], bcs[32:64, par, :].bitcast(F32),
                                  ALU.subtract).then_inc(s.blo, 1)
            if what == "softplus":
                after(dve, s.e, g)
                after(dve, s.dt, g, 1)
                dve.tensor_scalar(rest[:], ea[:], 1.0, -1.0, ALU.add, ALU.add).then_inc(s.r1, 1)
            if what == "dt":
                after(dve, s.r3, g)
                after(dve, s.xb, g)
                after(dve, s.dA, 16 * g - 16, 1)
                dve.scalar_tensor_tensor(dt[:, par, :], arg[:], 0.0, rest[:], ALU.max, ALU.add).then_inc(s.dt, 1)

        def program(eng, at, chunk, front, finish, before=lambda: None):
            def parts(n, one_ahead, two_ahead):
                for what in at.get(n, ()):
                    where = two_ahead if what in TWO_AHEAD else one_ahead
                    if where:
                        front(*where, what)

            def image(b, last):
                def place(c):
                    if isinstance(c, int) and c >= NCH:
                        return b * NCH + c, (b + 1) % B, c - NCH
                    return b * NCH + c, b, c

                def one(c, par, last=True):
                    prev = place(c - 1) if last else None
                    if last and isinstance(c, int) and c == 0:
                        prev = (b * NCH - 1, b - 1, NCH - 1)
                    chunk(b * NCH + c, b, c, par, prev,
                          lambda n: parts(n, (*place(c + 1), 1 - par), (*place(c + 2), par)))
                one(0, 0, last)
                with eng.Fori(0, NCH // 2 - 2) as j:
                    one(2 * j + 1, 1)
                    one(2 * j + 2, 0)
                for c in range(NCH - 3, NCH):
                    one(c, c % 2)
            for n in range(NS):
                parts(n, None, (0, 0, 0, 0))
            for n in range(NS):
                parts(n, (0, 0, 0, 0), (1, 0, 1, 1))
            before()
            image(0, False)
            with eng.Fori(1, B) as b:
                image(b, True)
            finish(B * NCH - 1, B - 1, NCH - 1, 1)

        with nc.Block() as block:
            @block.sync
            def _(sp):
                for q in credited:
                    sp.sem_inc(q, CREDIT)
                XF = G.X[:].rearrange("p b f -> p (b f)")
                with sp.Fori(0, B * NCH) as g:
                    after(sp, s.add, g)
                    sp.dma_start(x1_dram[:, bass.ds(g * CH, CH)], XF[:, bass.ds(g * CH, CH)]).then_inc(s.stored, 16)
                sp.wait_ge(s.stored, 16 * B * NCH)

            @block.tensor
            def _(pe):
                def sum_pair(g, k):
                    after(pe, s.pair, 8 * g + k)
                    pe.matmul(pY[:], G.ident, hs[:, k % 2, :], start=False, stop=(k == NS // 2 - 1)).then_inc(s.sum, 1)

                def project_out(g, par):
                    after(pe, s.y, g)
                    pe.matmul(pO[:], T.out[:], sz[:, par, :], start=False, stop=True).then_inc(s.out, 1)

                def chunk(g, b, c, par, prev, parts_ahead):
                    def spread_B(n):
                        after(pe, s.U, NS * g + n, 2)
                        pe.matmul(pB[:, n % 2, :], T.pick[:, n:n + 1].to_broadcast([P, P]), bcs[:, par, :],
                                  start=True, stop=True).then_inc(s.B, 1)

                    def spread_C(n):
                        after(pe, s.HC, NS * g + n, 2)
                        pe.matmul(pC[:, n % 2, :], T.pick[:, NS + n:NS + n + 1].to_broadcast([P, P]), bcs[:, par, :],
                                  start=True, stop=True).then_inc(s.C, 1)
                    after(pe, s.blo, g)
                    spread_B(0)
                    spread_B(1)
                    tap = 0
                    for n in range(NS):
                        if n + 2 < NS:
                            spread_B(n + 2)
                        spread_C(n)
                        if prev and n in LATE_SUM_AT:
                            sum_pair(g - 1, LATE_SUM_AT[n])
                        if n == 4:
                            if prev:
                                project_out(g - 1, 1 - par)
                            after(pe, s.y, g, 1)
                            pe.matmul(pY[:], T.d_diag[:], xc[:], start=True, stop=False).then_inc(s.dterm, 1)
                        if n in SUM_AT:
                            sum_pair(g, SUM_AT[n])
                        for _ in range(CONV_AT.get(n, 0)):
                            if tap == 0:
                                after(pe, s.fin, g, 1)
                                after(pe, s.xn, g)
                            pe.matmul(pO[:].rearrange("p (h w) -> p h w", w=W), T.conv[:, tap, :],
                                      xn[:, par, tap // 3:tap // 3 + ROWS, tap % 3:tap % 3 + W],
                                      start=(tap == 0), stop=False)
                            tap += 1
                        parts_ahead(n)

                def finish(g, b, c, par):
                    for k in LATE_SUM_AT.values():
                        sum_pair(g, k)
                    project_out(g, par)
                program(pe, PE_AT, chunk, front_pe, finish)

            @block.scalar
            def _(act):
                after(act, s.border, 0)

                def result(g, b, c, par):
                    after(act, s.out, g)
                    after(act, s.add, g, 1)
                    act.activation(fin[:], pO[:], ACT.Relu, bias=T.fin_b[:, 0:1]).then_inc(s.fin, 1)

                def decay(g, n, par):
                    m = NS * g + n
                    after(act, s.dt, g)
                    after(act, s.S, m, NDA)
                    act.activation(dA[:, n % NDA, :], dt[:, par, :], ACT.Exp, scale=T.A[:, n:n + 1]).then_inc(s.dA, 1)

                def chunk(g, b, c, par, prev, parts_ahead):
                    for n in range(NS):
                        if n < NS - LEAD:
                            decay(g, n + LEAD, par)
                        else:
                            decay(g + 1, n + LEAD - NS, 1 - par)
                        if prev and n == 5:
                            result(*prev, 1 - par)
                        parts_ahead(n)
                program(act, ACT_AT, chunk, front_act, result, lambda: [decay(0, n, 0) for n in range(LEAD)])

            @block.gpsimd
            def _(pool):
                pool.memset(xn[:].rearrange("p a h w -> p (a h w)"), 0.0).then_inc(s.border, 1)

                def add_pair(g, k):
                    after(pool, s.HC, NS * g + 2 * k + 1)
                    after(pool, s.sum, 8 * g + k, 2)
                    pool.tensor_tensor(hs[:, k % 2, :], hc[:, (2 * k) % 4, :], hc[:, (2 * k + 1) % 4, :],
                                       ALU.add).then_inc(s.pair, 1)

                def result(g, b, c, par):
                    after(pool, s.fin, g)
                    xg = XV[:, b, bass.ds(c * ROWS, ROWS), :]
                    pool.tensor_tensor(xg, xg, fin[:].rearrange("p (h w) -> p h w", w=W), ALU.add).then_inc(s.add, 1)

                def chunk(g, b, c, par, prev, parts_ahead):
                    for n in range(NS):
                        m = NS * g + n
                        if n % 2 == 0 and n:
                            add_pair(g, n // 2 - 1)
                        after(pool, s.S, m)
                        last = hb[:, n % 4, CH - 1:CH]
                        pool.tensor_tensor(state[:, n:n + 1], last, T.one[:], ALU.mult).then_inc(s.state, 1)
                        if prev and n == 6:
                            result(*prev, 1 - par)
                        parts_ahead(n)
                    add_pair(g, NS // 2 - 1)
                program(pool, POOL_AT, chunk, front_pool, result)

            @block.vector
            def _(dve):
                def statistics(g, b, c):
                    after(dve, s.add, g)
                    dve.bn_stats(G.stats[:, b, c, :], XV[:, b, bass.ds(c * ROWS, ROWS), :]).then_inc(s.st, 1)

                def gated(g, par):
                    after(dve, s.sum, 8 * g + NS // 2 - 1)
                    after(dve, s.sz, g)
                    dve.tensor_tensor(sz[:, par, :], pY[:], sz[:, par, :], ALU.mult).then_inc(s.y, 1)

                def chunk(g, b, c, par, prev, parts_ahead):
                    def product(n):
                        m = NS * g + n
                        after(dve, s.B, m)
                        if n == 0:
                            after(dve, s.dtx, g)
                        after(dve, s.HC, m, 4)
                        after(dve, s.state, m, 4)
                        dve.tensor_tensor(hb[:, n % 4, :], dtx[:, par, :], pB[:, n % 2, :], ALU.mult).then_inc(s.U, 1)

                    def weigh(n):
                        m = NS * g + n
                        after(dve, s.S, m)
                        after(dve, s.C, m)
                        after(dve, s.pair, 8 * g + n // 2, 2)
                        dve.tensor_tensor(hc[:, n % 4, :], hb[:, n % 4, :], pC[:, n % 2, :], ALU.mult).then_inc(s.HC, 1)
                    c_is_first = isinstance(c, int) and c == 0
                    product(0)
                    for n in range(NS):
                        m = NS * g + n
                        if n + 1 < NS:
                            product(n + 1)
                        after(dve, s.U, m)
                        after(dve, s.dA, m)
                        after(dve, s.state, m, NS)
                        dve.tensor_tensor_scan(hb[:, n % 4, :], dA[:, n % NDA, :], hb[:, n % 4, :],
                                               T.zero[:, 0:1] if c_is_first else state[:, n:n + 1],
                                               ALU.mult, ALU.add).then_inc(s.S, 1)
                        if n:
                            weigh(n - 1)
                        if prev and n == 3:
                            gated(g - 1, 1 - par)
                        if prev and n == 14:
                            statistics(*prev)
                        parts_ahead(n)
                    weigh(NS - 1)

                def finish(g, b, c, par):
                    gated(g, par)
                    statistics(g, b, c)
                program(dve, DVE_AT, chunk, front_dve, finish)
                after(dve, s.st, B * NCH - 1)


def layer3(nc, G, x3_dram, out):
    E = W + 1
    NT = CH // P
    NG = TAPS * NT
    RING = 9
    NM = 13
    NO = 3 * TAPS
    FIRST = 20
    NCLEAR = -(-E // RING)
    TAB_DMA = 8 * 16
    with ExitStack() as ctx:
        def sb(name, shape, dt=F32):
            return ctx.enter_context(nc.sbuf_tensor(name, shape, dt))

        def sem(name):
            return ctx.enter_context(nc.semaphore(name))

        def bank(name, shape):
            return ctx.enter_context(nc.psum_tensor(name, shape, F32))
        table = nc.dram_tensor("corner_table", (2, E, E, 4 * P), F32).ap()
        base = sb("d_base", [P, 2, NCH, NG])
        off_w = sb("d_off_w", [P, TAPS, NO])
        off_b = sb("d_off_b", [NO, 1])
        dcn_w = sb("d_dcn_w", [P, TAPS, P])
        vecs = sb("d_vecs", [P, 3])
        s_const, s_zero, s_border = sem("d_constants"), sem("d_zeros"), sem("d_border_zeroed")
        with ExitStack() as ctx2:
            def sb2(name, shape, dt=F32):
                return ctx2.enter_context(nc.sbuf_tensor(name, shape, dt))
            xn = sb2("d_xn", [P, HP, WP])
            xc = sb2("d_xc", [P, CH])
            om_s = sb2("d_om", [NO, CH])
            tT = sb2("d_tT", [P, NT, P])
            mask = sb2("d_mask", [P, NG])
            V, F, T1 = (sb2(f"d_{n}", [P, 2, NG]) for n in ("V", "F", "T1"))
            I = sb2("d_I", [P, 2, NG], mybir.dt.int32)
            WT = sb2("d_WT", [P, 2, 2, NG])
            J = sb2("d_J", [P, NG])
            tb = sb2("d_table_base", [P, 1])
            IDX = sb2("d_idx", [P, 2 * NCH, NG], U32)
            W4 = sb2("d_w4", [P, 2 * NCH, NG * 4])
            idx_now = sb2("d_idx_now", [P, NG], U32)
            w_now = sb2("d_w_now", [P, 2, NG * 4])
            ring = sb2("d_ring", [P, RING, 4 * P])
            R = sb2("d_mix", [P, 3, NT, P])
            samp = sb2("d_samp", [P, 3, CH])
            ps_off = ctx2.enter_context(nc.psum_tensor("d_ps_off", [NO, CH], F32))
            ps_tab = ctx2.enter_context(nc.psum_tensor("d_ps_tab", [P, NT, P], F32))
            ps_om = ctx2.enter_context(nc.psum_tensor("d_ps_om", [P, NT, NO], F32))
            ps_s = [ctx2.enter_context(nc.psum_tensor(f"d_ps_s{i}", [P, NT, P], F32)) for i in range(3)]
            ps_out = ctx2.enter_context(nc.psum_tensor("d_ps_out", [P, 2, CH], F32))
            s_offs = sem("d_offsets_out")
            s_omT = sem("d_offsets_turned")
            s_tabT = sem("d_table_turned")
            s_tT = sem("d_table_tile_out")
            s_tab = sem("d_table_stored")
            s_math = sem("d_index_steps")
            s_mix = sem("d_mix_steps")
            s_turn = sem("d_samples_turned")
            s_samp = sem("d_samples_out")
            s_dcn = sem("d_taps_summed")
            s_out = sem("d_output_kept")
            s_xn, s_xc, s_conv, s_mask = sem("d_xn_ready"), sem("d_xc_ready"), sem("d_offsets_summed"), sem("d_mask")
            s_wnow, s_inow, s_r0, s_st = sem("d_w_now"), sem("d_idx_now"), sem("d_corner0"), sem("d_stats")
            s_passed, s_passed_dve = sem("d_waits_passed"), sem("d_waits_passed_dve")
            s_clear = sem("d_second_table_cleared")
            s_land = [sem(f"d_landed{i}") for i in range(RING)]
            s_tb = sem("d_table_base_set")
            XV = G.X[:].rearrange("p b (h w) -> p b h w", h=H)
            XF = G.X[:].rearrange("p b f -> p (b f)")
            SF = G.stats[:].rearrange("p b c s -> p (b c) s")

            def passes(eng, body, head=lambda pT, pG: None, before=lambda: None, end=lambda: None):
                def chunks(pT, pG, first=False):
                    head(pT, pG)
                    if first:
                        before()
                        body(pT, pG, 0, 0, False)
                        body(pT, pG, 1, 1, True)
                    with eng.Fori(int(first), NCH // 2) as j:
                        for i in range(2):
                            body(pT, pG, 2 * j + i, i, True)
                chunks(0, None)
                chunks(1, 0, True)
                with eng.Fori(2, B) as p:
                    chunks(p, p - 1)
                chunks(None, B - 1)
                end()

            def mixed(m):
                return 3 * (m - m % 2) + 4 + m % 2 + 1

            with nc.Block() as block:
                @block.sync
                def _(sp):
                    for dst, n in ((base[:].rearrange("p a c k -> p (a c k)"), "base"), (off_w[:], "off_w"),
                                   (off_b[:], "off_b"), (dcn_w[:], "dcn_w"), (vecs[:, 0:1], "dcn_b"),
                                   (vecs[:, 1:2], "gamma"), (vecs[:, 2:3], "beta")):
                        sp.dma_start(dst, G.d[n]).then_inc(s_const, 16)
                    for s in (s_offs, s_omT, s_tabT, s_tT, s_tab, s_math, s_mix, s_turn, s_samp, s_dcn, s_out):
                        sp.sem_inc(s, CREDIT)
                    sp.wait_ge(s_const, 16 * 7)

                @block.gpsimd
                def _(pool):
                    pool.memset(xn[:].rearrange("p h w -> p (h w)"), 0.0).then_inc(s_zero, 1)
                    pool.memset(tb[:], 0.0).then_inc(s_zero, 1)
                    pool.memset(ring[:].rearrange("p r e -> p (r e)"), 0.0).then_inc(s_zero, 1)
                    pool.wait_ge(s_zero, 3)

            with nc.Block() as block:
                @block.sync
                def _(sp):
                    for side in range(2):
                        sp.dma_start(table[0, side * (E - 1), :, 2 * side * P:2 * (side + 1) * P],
                                     ring[0:E, 0, 0:2 * P]).then_inc(s_border, 16)
                    sp.wait_ge(s_border, 32)
                    for slot in range(4):
                        sp.dma_start(table[0, :, slot % 2 * (E - 1), slot * P:(slot + 1) * P],
                                     ring[0:E, 0, 0:P]).then_inc(s_border, 16)
                    sp.wait_ge(s_border, 96)

                    def store(pT, pG, c, par, prev):
                        if pT is None:
                            return
                        gT = NCH * pT + c
                        sp.wait_ge(s_tT, gT + (1 + CREDIT))
                        for yy in range(2):
                            for dy in range(2):
                                for dx in range(2):
                                    slot = 2 * dy + dx
                                    dst = table[pT % 2, bass.ds(ROWS * c + (yy + 1 - dy), NT, 2), 1 - dx:1 - dx + W,
                                                slot * P:(slot + 1) * P].rearrange("q x c -> x q c")
                                    sp.dma_start(dst, tT[yy * W:(yy + 1) * W, :, :]).then_inc(s_tab, 16)

                    def second_table(pT, pG):
                        if isinstance(pG, int) and pG == 0:
                            sp.wait_ge(s_clear, 16 * NCLEAR)
                    passes(sp, store, second_table)
                    sp.wait_ge(s_tab, TAB_DMA * NCH * B + CREDIT)

                @block.gpsimd
                def _(pool):
                    flat = table.rearrange("a y x e -> (a y x) e")
                    for x0 in range(0, E, RING):
                        n = min(RING, E - x0)
                        pool.dma_start(table[1, :, x0:x0 + n, :], ring[0:E, 0:n, :]).then_inc(s_clear, 16)

                    def gather(pT, pG, c, par, prev):
                        if pG is None:
                            return
                        gG = NCH * pG + c
                        pool.wait_ge(s_math, NM * gG + (NM + CREDIT))
                        for m in range(NG):
                            if m in (0, FIRST):
                                lo, hi = (0, FIRST) if m == 0 else (FIRST, NG)
                                apart(pool, s_passed)
                                pool.tensor_copy(idx_now[:, lo:hi], IDX[:, gG % (2 * NCH), lo:hi]).then_inc(s_inow, 1)
                                pool.wait_ge(s_inow, 2 * gG + (1 if m == 0 else 2))
                            pool.wait_ge(s_mix, 3 * NG * gG + (mixed(m + NG - RING) - 3 * NG + CREDIT))
                            apart(pool, s_passed)
                            pool.indirect_dma_start(
                                out=ring[:, m % RING, :], out_offset=None, in_=flat,
                                in_offset=bass.IndirectOffsetOnAxis(ap=idx_now[:, m:m + 1], axis=0),
                            ).then_inc(s_land[m % RING], 16)

                    def whole_table(pT, pG):
                        if pG is not None:
                            pool.wait_ge(s_clear, 16 * NCLEAR)
                            pool.wait_ge(s_tab, TAB_DMA * NCH * pG + (TAB_DMA * NCH + CREDIT))
                            apart(pool, s_passed)
                    passes(pool, gather, whole_table)

                @block.scalar
                def _(act):
                    def norm(pT, pG):
                        if pT is None:
                            return
                        act.activation(xn[:, PADH:PADH + H, PADW:PADW + W], XV[:, pT, :, :], ACT.Identity,
                                       bias=G.shift[:, bass.ds(pT, 1)], scale=G.rstd[:, bass.ds(pT, 1)]).then_inc(s_xn, 1)

                    def keep_samples(gG, k):
                        act.wait_ge(s_turn, NG * gG + (NT * (k + 1) + CREDIT))
                        act.wait_ge(s_dcn, TAPS * gG + (k - 3 + 1 + CREDIT))
                        act.activation(samp[:, k % 3, :], ps_s[k % 3][:].rearrange("p t c -> p (t c)"),
                                       ACT.Copy).then_inc(s_samp, 1)

                    def keep_output(gG, par):
                        act.wait_ge(s_dcn, TAPS * gG + (TAPS + CREDIT))
                        act.activation(XF[:, bass.ds(CH * gG, CH)], ps_out[:, par, :], ACT.Identity,
                                       bias=vecs[:, 0:1]).then_inc(s_out, 1)

                    def chunk(pT, pG, c, par, prev):
                        doT, doG = pT is not None, pG is not None
                        if doT:
                            gT = NCH * pT + c
                        if doG:
                            gG = NCH * pG + c
                        for k in range(TAPS):
                            if doG:
                                if k == 0:
                                    act.wait_ge(s_wnow, gG + 1)
                                for t in range(NT):
                                    m = NT * k + t
                                    act.wait_ge(s_land[m % RING], 64 * gG + 16 * (m // RING + 1))
                                    act.wait_ge(s_turn, NG * gG + (m - 3 * NT + 1 + CREDIT))
                                    act.activation(R[:, k % 3, t, :], ring[:, m % RING, 0:P], ACT.Copy,
                                                   scale=w_now[:, par, 4 * m:4 * m + 1]).then_inc(s_r0, 1)
                            if doT and k == 0:
                                act.wait_ge(s_tabT, NT * gT + CREDIT)
                                act.activation(xc[:], G.X[:, pT, bass.ds(CH * c, CH)], ACT.Identity,
                                               bias=G.shift[:, bass.ds(pT, 1)],
                                               scale=G.rstd[:, bass.ds(pT, 1)]).then_inc(s_xc, 1)
                            if doG and k >= 1:
                                keep_samples(gG, k - 1)
                            if prev and k == 0 and doG:
                                keep_samples(gG - 1, TAPS - 1)
                            if prev and k == 1 and doG:
                                keep_output(gG - 1, 1 - par)
                            if doT and k == 3:
                                act.wait_ge(s_tabT, NT * gT + (NT + CREDIT))
                                act.wait_ge(s_tab, TAB_DMA * gT + CREDIT)
                                act.activation(tT[:], ps_tab[:], ACT.Copy).then_inc(s_tT, 1)
                            if doT and k == 5:
                                act.wait_ge(s_conv, gT + 1)
                                act.wait_ge(s_omT, NT * gT + CREDIT)
                                act.activation(om_s[:], ps_off[:], ACT.Identity, bias=off_b[:, 0:1]).then_inc(s_offs, 1)
                            if doT and k == 7:
                                act.wait_ge(s_omT, NT * gT + (NT + CREDIT))
                                act.wait_ge(s_math, NM * gT + CREDIT)
                                act.activation(mask[:].rearrange("p (k t) -> p k t", t=NT),
                                               ps_om[:, :, 2 * TAPS:].rearrange("p t k -> p k t"),
                                               ACT.Sigmoid).then_inc(s_mask, 1)

                    def end():
                        keep_samples(B * NCH - 1, TAPS - 1)
                        keep_output(B * NCH - 1, 1)
                    passes(act, chunk, norm, end=end)

                @block.tensor
                def _(pe):
                    def contract(gG, k, par):
                        pe.wait_ge(s_samp, TAPS * gG + (k + 1 + CREDIT))
                        if k == 0:
                            pe.wait_ge(s_out, gG + (CREDIT - 1))
                        pe.matmul(ps_out[:, par, :], dcn_w[:, k, :], samp[:, k % 3, :], start=(k == 0),
                                  stop=(k == TAPS - 1)).then_inc(s_dcn, 1)

                    def chunk(pT, pG, c, par, prev):
                        doT, doG = pT is not None, pG is not None
                        if doT:
                            gT = NCH * pT + c
                        if doG:
                            gG = NCH * pG + c

                        for k in range(TAPS):
                            if doG:
                                pe.wait_ge(s_samp, TAPS * gG + (k - 3 + 1 + CREDIT))
                                for t in range(NT):
                                    pe.wait_ge(s_mix, 3 * NG * gG + (mixed(NT * k + t) + CREDIT))
                                    pe.matmul(ps_s[k % 3][:, t, :], R[:, k % 3, t, :], G.ident, start=True,
                                              stop=True).then_inc(s_turn, 1)
                                if k >= 1:
                                    contract(gG, k - 1, par)
                                elif prev:
                                    contract(gG - 1, TAPS - 1, 1 - par)
                            if doT:
                                if k == 0:
                                    pe.wait_ge(s_xn, pT + 1)
                                    pe.wait_ge(s_offs, gT + CREDIT)
                                for tap in range(2 * k, min(2 * k + 2, TAPS)):
                                    ki, kj = tap // 3, tap % 3
                                    mm = pe.matmul(ps_off[:], off_w[:, tap, :],
                                                   xn[:, bass.ds(ROWS * c + (PADH - 1 + ki), ROWS), PADW - 1 + kj:PADW - 1 + kj + W],
                                                   start=(tap == 0), stop=(tap == TAPS - 1))
                                    if tap == TAPS - 1:
                                        mm.then_inc(s_conv, 1)
                                if k == 1:
                                    pe.wait_ge(s_xc, gT + 1)
                                    pe.wait_ge(s_tT, gT + CREDIT)
                                    for t in range(NT):
                                        pe.matmul(ps_tab[:, t, :], xc[:, t * P:(t + 1) * P], G.ident, start=True,
                                                  stop=True).then_inc(s_tabT, 1)
                                if k == 6:
                                    pe.wait_ge(s_offs, gT + (1 + CREDIT))
                                    pe.wait_ge(s_math, NM * gT + CREDIT)
                                    for t in range(NT):
                                        pe.matmul(ps_om[:, t, :], om_s[:, t * P:(t + 1) * P], G.ident[0:NO, 0:NO],
                                                  start=True, stop=True).then_inc(s_omT, 1)
                    passes(pe, chunk, end=lambda: contract(B * NCH - 1, TAPS - 1, 1))

                @block.vector
                def _(dve):
                    def next_table(pT, pG):
                        if pT is not None and pG is not None:
                            dve.wait_ge(s_math, NM * NCH * pT + CREDIT)
                            dve.tensor_scalar(tb[:], tb[:], -1.0, float(E * E), ALU.mult, ALU.add).then_inc(s_tb, 1)
                            dve.wait_ge(s_tb, pT)
                            apart(dve, s_passed_dve)

                    def indices(pT, gT, c):
                        step = 0

                        def do(make):
                            nonlocal step
                            dve.wait_ge(s_math, NM * gT + (step + CREDIT))
                            make().then_inc(s_math, 1)
                            step += 1
                        slot = gT % (2 * NCH)
                        dve.wait_ge(s_mask, gT + 1)
                        do(lambda: dve.tensor_tensor(V[:].rearrange("p a (k t) -> p a k t", t=NT),
                                                     ps_om[:, :, 0:2 * TAPS].rearrange("p t (k a) -> p a k t", a=2),
                                                     base[:, :, c, :].rearrange("p a (k t) -> p a k t", t=NT), ALU.add))
                        do(lambda: dve.tensor_scalar(V[:], V[:], 0.0, float(H + 1), ALU.max, ALU.min))
                        do(lambda: dve.tensor_copy(I[:], V[:]))
                        do(lambda: dve.tensor_copy(F[:], I[:]))
                        do(lambda: dve.tensor_tensor(T1[:], F[:], V[:], ALU.is_gt))
                        do(lambda: dve.tensor_tensor(F[:], F[:], T1[:], ALU.subtract))
                        do(lambda: dve.tensor_scalar(F[:], F[:], float(H), None, ALU.min))
                        do(lambda: dve.tensor_tensor(WT[:, :, 1, :], V[:], F[:], ALU.subtract))
                        do(lambda: dve.tensor_scalar(WT[:, :, 0, :], WT[:, :, 1, :], -1.0, 1.0, ALU.mult, ALU.add))
                        do(lambda: dve.scalar_tensor_tensor(J[:], F[:, 0, :], float(E), F[:, 1, :], ALU.mult, ALU.add))
                        do(lambda: dve.tensor_scalar(IDX[:, slot, :], J[:], tb[:, 0:1], None, ALU.add))
                        do(lambda: dve.tensor_tensor(WT[:, 0, :, :], WT[:, 0, :, :],
                                                     mask[:].unsqueeze(1).to_broadcast([P, 2, NG]), ALU.mult))
                        do(lambda: dve.tensor_tensor(
                            W4[:, slot, :].rearrange("p (n y x) -> p n y x", y=2, x=2),
                            WT[:, 0, :, :].rearrange("p y n -> p n y").unsqueeze(3).to_broadcast([P, NG, 2, 2]),
                            WT[:, 1, :, :].rearrange("p x n -> p n x").unsqueeze(2).to_broadcast([P, NG, 2, 2]),
                            ALU.mult))

                    def weights(gG, par, last_pass=False):
                        if last_pass:
                            dve.wait_ge(s_math, NM * NCH * B + CREDIT)
                        else:
                            dve.wait_ge(s_math, NM * gG + (NM + CREDIT))
                        if not isinstance(gG, int) or gG >= 2:
                            dve.wait_ge(s_mix, 3 * NG * gG + (CREDIT - 3 * NG))
                        dve.tensor_copy(w_now[:, par, :], W4[:, gG % (2 * NCH), :]).then_inc(s_wnow, 1)

                    def statistics(gG):
                        dve.wait_ge(s_out, gG + (1 + CREDIT))
                        dve.bn_stats(SF[:, gG, :], XF[:, bass.ds(CH * gG, CH)]).then_inc(s_st, 1)

                    def chunk(pT, pG, c, par, prev):
                        doT, doG = pT is not None, pG is not None
                        if doT:
                            gT = NCH * pT + c
                        if doG:
                            gG = NCH * pG + c
                            dve.wait_ge(s_wnow, gG + 1)
                        for k in range(TAPS):
                            if doG:
                                for t in range(0, NT, 2):
                                    first = 3 * (NT * k + t)
                                    for corner in range(1, 4):
                                        for j in range(2):
                                            m = NT * k + t + j
                                            if corner == 1:
                                                dve.wait_ge(s_r0, NG * gG + (m + 1))
                                            else:
                                                dve.wait_ge(s_mix, 3 * NG * gG + (first + 2 * (corner - 2) + j + 1 + CREDIT))
                                            dve.scalar_tensor_tensor(
                                                R[:, k % 3, t + j, :], ring[:, m % RING, corner * P:(corner + 1) * P],
                                                w_now[:, par, 4 * m + corner:4 * m + corner + 1], R[:, k % 3, t + j, :],
                                                ALU.mult, ALU.add).then_inc(s_mix, 1)
                            if doG and prev and k == 3:
                                statistics(gG - 1)
                            if doG and k == 5:
                                weights(gG + 1, 1 - par, not doT)
                            if doT and k == 8:
                                indices(pT, gT, c)
                    passes(dve, chunk, next_table, lambda: weights(0, 0), lambda: statistics(B * NCH - 1))
                    dve.wait_ge(s_st, B * NCH)

        HB = HW // 2
        mv = sb("b_mv", [P, 2])
        std = sb("b_std", [P, 1])
        scale, shift = sb("b_scale", [P, 1]), sb("b_shift", [P, 1])
        x3 = sb("b_x3", [P, 4, HB])
        z = sb("b_z", [P, 2, HB])
        s_step, s_std, s_z, s_y = (sem(n) for n in ("b_step", "b_std_done", "b_z", "b_y"))
        s_x3 = [sem(f"b_x3_landed{i}") for i in range(4)]
        s_sum, s_stored = sem("b_sum"), sem("b_stored")
        with nc.Block() as block:
            @block.vector
            def _(dve):
                dve.bn_aggr(mv[:], G.stats[:].rearrange("p b c s -> p (b c s)")).then_inc(s_step, 1)
                dve.wait_ge(s_std, 1)
                dve.reciprocal(scale[:], std[:]).then_inc(s_step, 1)
                dve.wait_ge(s_step, 2)
                dve.tensor_tensor(scale[:], scale[:], vecs[:, 1:2], ALU.mult).then_inc(s_step, 1)
                dve.wait_ge(s_step, 3)
                dve.tensor_tensor(mv[:, 1:2], mv[:, 0:1], scale[:], ALU.mult).then_inc(s_step, 1)
                dve.wait_ge(s_step, 4)
                dve.tensor_tensor(shift[:], vecs[:, 2:3], mv[:, 1:2], ALU.subtract).then_inc(s_step, 1)
                for n in range(2 * B):
                    b, h = n // 2, n % 2
                    dve.wait_ge(s_z, n + 1)
                    x = G.X[:, b, h * HB:(h + 1) * HB]
                    dve.scalar_tensor_tensor(x, z[:, n % 2, :], 0.1, z[:, n % 2, :], ALU.mult, ALU.max).then_inc(s_y, 1)
                    dve.wait_ge(s_y, n + 1)
                    dve.wait_ge(s_x3[n % 4], 16 * (n // 4 + 1))
                    dve.tensor_tensor(x, x, x3[:, n % 4, :], ALU.add).then_inc(s_sum, 1)

            @block.scalar
            def _(act):
                act.wait_ge(s_step, 1)
                act.activation(std[:], mv[:, 1:2], ACT.Sqrt, bias=G.eps5[:, 0:1]).then_inc(s_std, 1)
                act.wait_ge(s_step, 5)
                for n in range(2 * B):
                    b, h = n // 2, n % 2
                    if n >= 2:
                        act.wait_ge(s_y, n - 1)
                    act.activation(z[:, n % 2, :], G.X[:, b, h * HB:(h + 1) * HB], ACT.Identity,
                                   bias=shift[:, 0:1], scale=scale[:, 0:1]).then_inc(s_z, 1)

            @block.gpsimd
            def _(pool):
                for n in range(2 * B):
                    b, h = n // 2, n % 2
                    if n >= 4:
                        pool.wait_ge(s_sum, n - 3)
                    pool.dma_start(x3[:, n % 4, :], x3_dram[b][:, h * HB:(h + 1) * HB]).then_inc(s_x3[n % 4], 16)

            @block.sync
            def _(sp):
                for n in range(2 * B):
                    b, h = n // 2, n % 2
                    sp.wait_ge(s_sum, n + 1)
                    sp.dma_start(out[b][:, h * HB:(h + 1) * HB], G.X[:, b, h * HB:(h + 1) * HB]).then_inc(s_stored, 16)
                sp.wait_ge(s_stored, 16 * 2 * B)


def build_program(nc, d, out):
    class G:
        pass
    G.d = d
    x1 = nc.dram_tensor("x1_scratch", (P, B * HW), F32).ap()
    x3 = nc.dram_tensor("x3_scratch", (B, P, HW), F32).ap()
    with ExitStack() as ctx:
        def sb(name, shape, dt=F32):
            return ctx.enter_context(nc.sbuf_tensor(name, shape, dt))
        G.X = sb("X", [P, B, HW])
        G.stats = sb("stats", [P, B, NCH, 6])
        G.small = sb("small", [P, 4 * P + 32])
        G.ident = G.small[:, 0:P]
        G.group_mean = G.small[:, P:2 * P]
        G.mean64 = G.small[:, 2 * P:3 * P]
        G.centre = G.small[:, 3 * P:4 * P]
        G.pick = G.small[:, 4 * P:4 * P + 32]
        G.eps5 = sb("eps5", [P, 1])
        G.rstd = sb("rstd", [P, B])
        G.shift = sb("shift", [P, B])
        load_image_and_statistics(nc, G, d["x"])
        for n, stage in (("L0", lambda: layer0(nc, G, x1)), ("L1", lambda: layer1(nc, G, x1)),
                         ("L2", lambda: layer2(nc, G, x3)), ("L3", lambda: layer3(nc, G, x3, out))):
            G.tag = n
            group_norm_scales(nc, ctx, G)
            stage()


def lay_out(i):
    def c(a):
        return np.ascontiguousarray(a)
    small, base = host_constants()
    o = {"x": c(i["x"].reshape(B, P, HW)), "small": small, "base": base}
    o["conv_w"] = c(i["L0_conv_conv_w"].transpose(1, 2, 3, 0).reshape(HALF, TAPS, HALF))
    o["conv_b"] = c(i["L0_conv_conv_b"].reshape(HALF, 1))
    o["expand_wT"] = c(i["L0_conv_expand_w"].T)
    o["concat_w"] = c(i["L0_conv_concat_w"])
    o["concat_b"] = c(i["L0_conv_concat_b"].reshape(HALF, 1))
    o["ln_g"] = c(i["L0_conv_ln_g"].reshape(HALF, 1))
    o["ln_b"] = c(i["L0_conv_ln_b"].reshape(HALF, 1))
    o["in_w"] = c(i["L0_conv_in_w"])
    o["in_b"] = c(i["L0_conv_in_b"].reshape(2, P).T)
    o["conv1d_w"] = c(i["L0_conv_conv1d_w"].T)
    o["conv1d_b"] = c(i["L0_conv_conv1d_b"].reshape(P, 1))
    o["xproj_w"] = c(i["L0_conv_xproj_w"])
    o["xproj_dtT"] = c(i["L0_conv_xproj_w"][:, :4].T)
    o["dt_w"] = c(i["L0_conv_dt_w"])
    o["dt_b"] = c(i["L0_conv_dt_b"].reshape(P, 1))
    o["A_log"] = c(i["L0_conv_A_log"])
    o["D_ssm"] = c(i["L0_conv_D_ssm"].reshape(P, 1))
    o["out_w"] = c(i["L0_conv_out_w"])
    o["out_b"] = c(i["L0_conv_out_b"].reshape(HALF, 1))
    for n in ("down", "up", "right", "left"):
        o[f"w_{n}"] = c(i[f"L1_conv_w_{n}"].transpose(1, 2, 0).reshape(P, TAPS * P))
    o["l2_w1"] = c(i["L2_conv_w1"][..., 0].transpose(1, 2, 0))
    o["l2_w3"] = c(i["L2_conv_w3"][:, 0, :, 0].T.reshape(1, 3 * P))
    o["l2_w4"] = c(i["L2_conv_w4"][:, :, 0, :])
    o["off_w"] = c(i["L3_conv_offset_w"].transpose(1, 2, 3, 0).reshape(P, TAPS, 3 * TAPS))
    o["off_b"] = c(i["L3_conv_offset_b"].reshape(3 * TAPS, 1))
    o["dcn_w"] = c(i["L3_conv_dcn_w"].transpose(1, 2, 3, 0).reshape(P, TAPS, P))
    for n in ("dcn_b", "gamma", "beta"):
        o[n] = c(i[f"L3_conv_{n}"].reshape(P, 1))
    return o


def kernel(**inputs):
    import concourse.bacc as _bacc
    from concourse.bass_utils import run_bass_kernel_spmd as _run

    nc = _bacc.Bacc("TRN2", target_bir_lowering=False, num_devices=1, dynamic_dma_scratch_size=4096)
    arrays = lay_out({k: np.asarray(v) for k, v in inputs.items()})
    d = {k: nc.dram_tensor(f"in_{k}", a.shape, mybir.dt.from_np(a.dtype), kind="ExternalInput").ap()
         for k, a in arrays.items()}
    out = nc.dram_tensor("out_dram", (B, P, HW), F32, kind="ExternalOutput").ap()
    build_program(nc, d, out)
    r = _run(nc, [{f"in_{k}": a for k, a in arrays.items()}], core_ids=[0])
    return r.results[0]["out_dram"].reshape(B, P, H, W)
```

```python
from contextlib import ExitStack

import concourse.bass as bass
import numpy as np
from concourse import mybir

F32 = mybir.dt.float32
F32R = mybir.dt.float32r
U32 = mybir.dt.uint32
ALU = mybir.AluOpType
ACT = mybir.ActivationFunctionType
AX_X = mybir.AxisListType.X

P = 128
B, H, W = 8, 64, 64
HW = H * W
CH = 512
NCH = HW // CH
ROWS = CH // W
HALF = 64
NS = 16
PADH, PADW = 3, 2
HP, WP = H + 2 * PADH, W + 2 * PADW
TAPS = 9
K1, K3, GT = 5, 3, 3
K7 = K1 + K3 - 1
CREDIT = 32


def after(eng, sem, k, lag=0):
    eng.wait_ge(sem, k + (1 + CREDIT - lag))


def apart(eng, passed):
    eng.sem_inc(passed, 1)


def host_constants():
    ident = np.eye(P, dtype=np.float32)
    group_mean = np.kron(np.eye(P // 4), np.full((4, 4), 0.25)).astype(np.float32)
    mean64 = np.zeros((P, P), np.float32)
    mean64[:HALF, :] = 1.0 / HALF
    centre = np.zeros((P, P), np.float32)
    centre[:HALF, :HALF] = np.eye(HALF) - 1.0 / HALF
    pick = np.zeros((P, 32), np.float32)
    for k in range(64):
        pick[k, k % 32] = 1.0
    small = np.concatenate([ident, group_mean, mean64, centre, pick], axis=1)
    p = np.arange(P)
    base = np.zeros((P, 2, NCH, TAPS, 4), np.float32)
    for t in range(HW // P):
        for k in range(TAPS):
            base[:, 0, t // 4, k, t % 4] = 2 * t + p // W + k // 3
            base[:, 1, t // 4, k, t % 4] = p % W + k % 3
    return small, base.reshape(P, -1)


def group_norm_scales(nc, ctx_outer, G):
    with ExitStack() as ctx:
        def sem(name):
            return ctx.enter_context(nc.semaphore(f"{name}_{G.tag}"))
        tag = G.tag
        mv = ctx.enter_context(nc.sbuf_tensor(f"gn_mv{tag}", [P, B, 2], F32))
        moments = ctx.enter_context(nc.sbuf_tensor(f"gn_moments{tag}", [P, 2, B], F32))
        mean = ctx.enter_context(nc.sbuf_tensor(f"gn_mean{tag}", [P, 2, B], F32))
        var = ctx.enter_context(nc.sbuf_tensor(f"gn_var{tag}", [P, B], F32))
        ps = ctx.enter_context(nc.psum_tensor(f"gn_ps{tag}", [P, 2, B], F32))
        s_step, s_ps, s_std = sem("gn_step"), sem("gn_group_moments"), sem("gn_std")
        with nc.Block() as block:
            @block.vector
            def _(dve):
                for b in range(B):
                    nc.vector.bn_aggr(mv[:, b, :], G.stats[:, b, :, :].rearrange("p c s -> p (c s)")).then_inc(s_step, 1)
                dve.wait_ge(s_step, B)
                nc.vector.tensor_copy(moments[:, 0, :], mv[:, :, 0]).then_inc(s_step, 1)
                nc.vector.tensor_tensor(var[:], mv[:, :, 0], mv[:, :, 0], ALU.mult).then_inc(s_step, 1)
                dve.wait_ge(s_step, B + 2)
                nc.vector.tensor_tensor(moments[:, 1, :], mv[:, :, 1], var[:], ALU.add).then_inc(s_step, 1)
                dve.wait_ge(s_ps, 1)
                nc.vector.tensor_copy(mean[:], ps[:]).then_inc(s_step, 1)
                dve.wait_ge(s_step, B + 4)
                nc.vector.tensor_tensor(var[:], mean[:, 0, :], mean[:, 0, :], ALU.mult).then_inc(s_step, 1)
                dve.wait_ge(s_step, B + 5)
                nc.vector.tensor_tensor(mean[:, 1, :], mean[:, 1, :], var[:], ALU.subtract).then_inc(s_step, 1)
                dve.wait_ge(s_std, 1)
                nc.vector.reciprocal(G.rstd[:], mv[:, :, 0]).then_inc(s_step, 1)
                dve.wait_ge(s_step, B + 7)
                nc.vector.scalar_tensor_tensor(G.shift[:], mean[:, 0, :], -1.0, G.rstd[:], ALU.mult, ALU.mult).then_inc(s_step, 1)
                dve.wait_ge(s_step, B + 8)

            @block.tensor
            def _(pe):
                pe.wait_ge(s_step, B + 3)
                nc.tensor.matmul(ps[:].rearrange("p a b -> p (a b)"), G.group_mean, moments[:].rearrange("p a b -> p (a b)"),
                                 start=True, stop=True).then_inc(s_ps, 1)

            @block.scalar
            def _(act):
                act.wait_ge(s_step, B + 6)
                nc.scalar.activation(mv[:, :, 0], mean[:, 1, :], ACT.Sqrt, bias=G.eps5[:, 0:1]).then_inc(s_std, 1)


def load_image_and_statistics(nc, G, x_dram):
    with ExitStack() as ctx:
        s_x = [ctx.enter_context(nc.semaphore(f"x_landed{b}")) for b in range(B)]
        s_c = ctx.enter_context(nc.semaphore("constants_landed"))
        s_st = ctx.enter_context(nc.semaphore("load_stats_done"))
        with nc.Block() as block:
            @block.sync
            def _(sp):
                sp.dma_start(G.small[:], G.d["small"]).then_inc(s_c, 16)
                for b in range(B):
                    sp.dma_start(G.X[:, b, :], x_dram[b]).then_inc(s_x[b], 16)
                sp.wait_ge(s_c, 16)

            @block.vector
            def _(dve):
                nc.vector.memset(G.eps5[:], 1e-5).then_inc(s_st, 1)
                for b in range(B):
                    dve.wait_ge(s_x[b], 16)
                    for c in range(NCH):
                        nc.vector.bn_stats(G.stats[:, b, c, :], G.X[:, b, c * CH:(c + 1) * CH]).then_inc(s_st, 1)
                dve.wait_ge(s_st, 1 + B * NCH)


def layer1(nc, G, outer, x1_dram):
    NG, NI, PAD, LINES = 2, 4, TAPS // 2, H - 1
    NB = 3
    ON_POOL = (1, 2, 4, 5, 7)
    with ExitStack() as ctx:
        def sb(name, shape, dt=F32):
            return ctx.enter_context(nc.sbuf_tensor(name, shape, dt))

        def sem(name):
            return ctx.enter_context(nc.semaphore(name))
        weights2 = Layer2Weights(nc, G, outer, ctx)
        raw = sb("prop_raw", [P, TAPS * P])
        w_hi = sb("prop_w_hi", [P, 2, TAPS * P], F32R)
        w_lo = sb("prop_w_lo", [P, 2, TAPS * P], F32R)
        hi = [sb(f"prop_hi{s}", [P, NI, W + 2 * PAD], F32R) for s in range(NG)]
        lo = [sb(f"prop_lo{s}", [P, NI, W + 2 * PAD], F32R) for s in range(NG)]
        zero = sb("prop_zero", [P, NI, PAD])
        x1 = sb("prop_x1", [P, NB, HW])
        ps = [ctx.enter_context(nc.psum_tensor(f"prop_ps{s}", [P, NI, W], F32)) for s in range(NG)]
        s_zero, s_edge = sem("p_zero"), sem("p_edges_zero")
        s_norm = [sem(f"p_S_normed{s}") for s in range(NG)]
        s_raw, s_whi, s_wlo = sem("p_raw_landed"), sem("p_w_hi"), sem("p_w_lo")
        s_conv = [sem(f"p_conv{s}") for s in range(NG)]
        s_new = [sem(f"p_new{s}") for s in range(NG)]
        s_hi = [sem(f"p_hi{s}") for s in range(NG)]
        s_lo = [sem(f"p_lo{s}") for s in range(NG)]
        s_x1 = [sem(f"p_x1_landed{i}") for i in range(NB)]
        s_add = [sem("p_added_dve"), sem("p_added_pool")]
        s_stat = sem("p_stats")
        XV = G.X[:].rearrange("p b (h w) -> p b h w", h=H)
        names = ["w_down", "w_up", "w_right", "w_left"]

        def line(d, s, t):
            idx = t if d % 2 == 0 else t * -1 + (H - 1)
            if d < 2:
                return XV[:, NI * s:NI * s + NI, idx, :]
            return XV[:, NI * s:NI * s + NI, :, idx]

        def adder(b):
            p = b in ON_POOL
            return int(p), sum((i in ON_POOL) == p for i in range(b + 1))

        with nc.Block() as block:
            @block.sync
            def _(sp):
                sp.dma_start(raw[:], G.d[names[0]]).then_inc(s_raw, 16)
                for b in range(NB):
                    sp.dma_start(x1[:, b, :], x1_dram[:, b * HW:(b + 1) * HW]).then_inc(s_x1[b], 16)
                weights2.load(sp)
                for d in range(1, 4):
                    sp.wait_ge(s_wlo, d)
                    sp.dma_start(raw[:], G.d[names[d]]).then_inc(s_raw, 16)
                for b in range(NB, B):
                    who, n = adder(b - NB)
                    sp.wait_ge(s_add[who], n)
                    sp.dma_start(x1[:, b % NB, :], x1_dram[:, b * HW:(b + 1) * HW]).then_inc(s_x1[b % NB], 16)

            @block.gpsimd
            def _(pool):
                pool.memset(zero[:].rearrange("p a b -> p (a b)"), 0.0).then_inc(s_zero, 1)
                for d in range(4):
                    pool.wait_ge(s_whi, d + 1)
                    pool.tensor_tensor(w_lo[:, d % 2, :], raw[:], w_hi[:, d % 2, :].bitcast(F32), ALU.subtract).then_inc(s_wlo, 1)
                weights2.make(pool)
                for b in ON_POOL:
                    pool.wait_ge(s_new[b // NI], 4 * LINES)
                    pool.wait_ge(s_hi[b // NI], 4 * H)
                    pool.wait_ge(s_lo[b // NI], 4 * H)
                    pool.wait_ge(s_x1[b % NB], 16 * (b // NB + 1))
                    pool.tensor_tensor(G.X[:, b, :], G.X[:, b, :], x1[:, b % NB, :], ALU.add).then_inc(s_add[1], 1)

            @block.scalar
            def _(act):
                act.wait_ge(s_zero, 1)
                for buf in hi + lo:
                    for side in (0, PAD + W):
                        act.activation(buf[:, :, side:side + PAD], zero[:], ACT.Copy).then_inc(s_edge, 1)

                def split(d):
                    if d >= 2:
                        for s in range(NG):
                            act.wait_ge(s_conv[s], LINES * (d - 1))
                    act.wait_ge(s_raw, 16 * (d + 1))
                    act.activation(w_hi[:, d % 2, :], raw[:], ACT.Copy).then_inc(s_whi, 1)
                split(0)

                def round_line(d, t, s):
                    act.activation(hi[s][:, :, PAD:PAD + W], line(d, s, t), ACT.Copy).then_inc(s_hi[s], 1)
                for d in range(4):
                    for s in range(NG):
                        if d == 0:
                            for b in (NI * s, NI * s + 1):
                                act.activation(G.X[:, b, :], G.X[:, b, :], ACT.Identity, bias=G.shift[:, b:b + 1],
                                               scale=G.rstd[:, b:b + 1]).then_inc(s_norm[s], 1)
                            act.wait_ge(s_norm[s], NI)
                        else:
                            act.wait_ge(s_new[s], LINES * d)
                            act.wait_ge(s_lo[s], H * d)
                        round_line(d, 0, s)
                    if d + 1 < 4:
                        split(d + 1)
                    with act.Fori(1, H) as t:
                        for s in range(NG):
                            act.wait_ge(s_new[s], t + LINES * d)
                            round_line(d, t, s)

            @block.tensor
            def _(pe):
                pe.wait_ge(s_edge, 8)
                for d in range(4):
                    pe.wait_ge(s_wlo, d + 1)
                    with pe.Fori(1, H) as t:
                        for s in range(NG):
                            for n, (wt, part, ready) in enumerate(((w_hi, hi[s], s_hi[s]), (w_lo, hi[s], None),
                                                                   (w_hi, lo[s], s_lo[s]))):
                                if ready:
                                    pe.wait_ge(ready, t + H * d)
                                for k in range(TAPS):
                                    mm = pe.matmul(ps[s][:], wt[:, d % 2, k * P:(k + 1) * P], part[:, :, k:k + W],
                                                   start=(n == 0 and k == 0), stop=(n == 2 and k == TAPS - 1))
                            mm.then_inc(s_conv[s], 1)

            @block.vector
            def _(dve):
                def rest_of_line(d, t, s):
                    dve.wait_ge(s_hi[s], t + (1 + H * d))
                    dve.tensor_tensor(lo[s][:, :, PAD:PAD + W], line(d, s, t), hi[s][:, :, PAD:PAD + W].bitcast(F32),
                                      ALU.subtract).then_inc(s_lo[s], 1)
                for d in range(4):
                    for s in range(NG):
                        if d == 0:
                            for b in (NI * s + 2, NI * s + 3):
                                dve.tensor_scalar(G.X[:, b, :], G.X[:, b, :], G.rstd[:, b:b + 1], G.shift[:, b:b + 1],
                                                  ALU.mult, ALU.add).then_inc(s_norm[s], 1)
                        rest_of_line(d, 0, s)
                    with dve.Fori(1, H) as t:
                        for s in range(NG):
                            dve.wait_ge(s_conv[s], t + LINES * d)
                            dve.scalar_tensor_tensor(line(d, s, t), ps[s][:], 0.0, line(d, s, t), ALU.max,
                                                     ALU.add).then_inc(s_new[s], 1)
                            rest_of_line(d, t, s)
                for s in range(NG):
                    dve.wait_ge(s_lo[s], 4 * H)
                for b in range(B):
                    who, n = adder(b)
                    if not who:
                        dve.wait_ge(s_x1[b % NB], 16 * (b // NB + 1))
                        dve.tensor_tensor(G.X[:, b, :], G.X[:, b, :], x1[:, b % NB, :], ALU.add).then_inc(s_add[0], 1)
                    dve.wait_ge(s_add[who], n)
                    for c in range(NCH):
                        dve.bn_stats(G.stats[:, b, c, :], G.X[:, b, c * CH:(c + 1) * CH]).then_inc(s_stat, 1)
                dve.wait_ge(s_stat, B * NCH)


class Layer2Weights:
    def __init__(self, nc, G, outer, ctx):
        def sb(where, name, shape):
            return where.enter_context(nc.sbuf_tensor(name, shape, F32))
        self.G = G
        G.w7, G.edge, G.w4 = sb(outer, "l2_w7", [P, K7, P]), sb(outer, "l2_edge", [P, 4, P]), sb(outer, "l2_w4", [P, GT, P])
        self.w1, self.w3 = sb(ctx, "l2_w1", [P, K1, P]), sb(ctx, "l2_w3", [P, K3, P])
        self.w4g, self.tmp = sb(ctx, "l2_w4g", [P, GT, 8]), sb(ctx, "l2_tmp", [P, P])
        self.landed = ctx.enter_context(nc.semaphore("c_weights_landed"))
        self.made = ctx.enter_context(nc.semaphore("c_weights_made"))

    def load(self, sp):
        d = self.G.d
        sp.dma_start(self.w1[:], d["l2_w1"]).then_inc(self.landed, 16)
        sp.dma_start(self.w3[:].rearrange("p a o -> p (a o)"), d["l2_w3"].to_broadcast([P, K3 * P])).then_inc(self.landed, 16)
        sp.dma_start(self.w4g[:], d["l2_w4"]).then_inc(self.landed, 16)

    def make(self, pool):
        w7, edge, w4, w1, w3, tmp = self.G.w7, self.G.edge, self.G.w4, self.w1, self.w3, self.tmp
        pool.wait_ge(self.landed, 48)
        n = 0

        def done(ins):
            nonlocal n
            n += 1
            ins.then_inc(self.made, 1)
            pool.wait_ge(self.made, n)
        for j in range(K7):
            first = True
            for a in range(K3):
                if 0 <= j - a < K1:
                    dst = w7[:, j, :] if first else tmp[:]
                    done(pool.tensor_tensor(dst, w1[:, j - a, :], w3[:, a, :], ALU.mult))
                    if not first:
                        done(pool.tensor_tensor(w7[:, j, :], w7[:, j, :], tmp[:], ALU.add))
                    first = False
        for e, (a, b1) in enumerate([(0, 3), (0, 4), (2, 0), (2, 1)]):
            done(pool.tensor_tensor(tmp[:], w1[:, b1, :], w3[:, a, :], ALU.mult))
            done(pool.tensor_scalar(edge[:, e, :], tmp[:], -1.0, None, ALU.mult))
        for k in range(GT):
            done(pool.tensor_copy(w4[:, k, :].rearrange("p (r g) -> p r g", g=8),
                                  self.w4g[:, k:k + 1, :].to_broadcast([P, P // 8, 8])))


def layer0_weights(nc, G, T):
    with ExitStack() as ctx:
        def sb(name, shape, dt=F32):
            return ctx.enter_context(nc.sbuf_tensor(name, shape, dt))
        expand = sb("w_expand", [P, HALF])
        concat = sb("w_concat", [P, HALF])
        folded = sb("w_folded", [P, P])
        in_raw = sb("w_in_raw", [P, 2 * P])
        cols = sb("w_cols", [P, 16])
        xproj = sb("w_xproj", [P, 36])
        xdt = sb("w_xdt", [4, P])
        dtw = sb("w_dtw", [4, P])
        ps = ctx.enter_context(nc.psum_tensor("w_ps", [P, 8, P], F32))
        s_zero, s_ld, s_mm, s_v = [ctx.enter_context(nc.semaphore(f"w0_{n}")) for n in ("zero", "landed", "products", "made")]
        concat_b, ln_g, ln_b, out_b, d_ssm = (cols[:, k:k + 1] for k in range(5))
        c1w = cols[:, 5:8]
        with nc.Block() as block:
            @block.gpsimd
            def _(pool):
                for t in (T.conv, folded, in_raw, cols, T.bc, T.out, T.fin_b, T.dt_b):
                    flat = t[:] if len(t.shape) == 2 else t[:].rearrange("p a b -> p (a b)")
                    pool.memset(flat, 0.0).then_inc(s_zero, 1)
                pool.memset(T.one[:], 1.0).then_inc(s_zero, 1)
                pool.memset(T.zero[:], 0.0).then_inc(s_zero, 1)

            @block.sync
            def _(sp):
                sp.wait_ge(s_zero, 10)
                loads = [(expand[:], "expand_wT"), (concat[:], "concat_w"), (in_raw[0:HALF, :], "in_w"),
                         (concat_b[0:HALF, :], "concat_b"), (ln_g[0:HALF, :], "ln_g"), (ln_b[0:HALF, :], "ln_b"),
                         (out_b[0:HALF, :], "out_b"), (d_ssm, "D_ssm"), (c1w, "conv1d_w"), (T.conv1d_b[:], "conv1d_b"),
                         (xproj[:], "xproj_w"), (xdt[:], "xproj_dtT"), (dtw[:], "dt_w"), (T.dt_b[:], "dt_b"),
                         (T.A[:], "A_log"), (T.out[:, 0:HALF], "out_w"), (T.in_b[:], "in_b"),
                         (T.conv[HALF:P, :, HALF:P], "conv_w"), (T.fin_b[HALF:P, :], "conv_b"),
                         (T.fin_b[0:HALF, :], "concat_b")]
                for dst, name in loads:
                    sp.dma_start(dst, G.d[name]).then_inc(s_ld, 16)
                sp.wait_ge(s_ld, 16 * len(loads))
                sp.sem_inc(s_ld, 1000)

            @block.tensor
            def _(pe):
                pe.wait_ge(s_ld, 1000)
                pe.matmul(ps[0:HALF, 0, 0:HALF], concat[:], expand[:], start=True, stop=True).then_inc(s_mm, 1)
                pe.matmul(ps[0:HALF, 4, 0:HALF], expand[:], concat[:], start=True, stop=True).then_inc(s_mm, 1)
                pe.wait_ge(s_v, 2)
                pe.matmul(ps[:, 0, :], folded[:], G.centre, start=True, stop=True).then_inc(s_mm, 1)
                pe.matmul(ps[:, 4, 0:1], G.centre, concat_b, start=True, stop=True).then_inc(s_mm, 1)
                pe.wait_ge(s_v, 4)
                pe.matmul(ps[:, 0, :], xdt[:], dtw[:], start=True, stop=True).then_inc(s_mm, 1)
                for h in range(2):
                    pe.matmul(ps[:, 4, h:h + 1], in_raw[:, h * P:(h + 1) * P], ln_b, start=True, stop=True).then_inc(s_mm, 1)

            @block.scalar
            def _(act):
                act.wait_ge(s_ld, 1000)
                act.activation(T.A[:], T.A[:], ACT.Exp).then_inc(s_zero, 1)

            @block.vector
            def _(dve):
                dve.wait_ge(s_ld, 1000)
                dve.wait_ge(s_mm, 2)
                dve.tensor_copy(folded[0:HALF, 0:HALF], ps[0:HALF, 0, 0:HALF]).then_inc(s_v, 1)
                dve.tensor_copy(T.conv[0:HALF, TAPS // 2, 0:HALF], ps[0:HALF, 4, 0:HALF]).then_inc(s_v, 1)
                dve.wait_ge(s_mm, 4)
                dve.tensor_copy(T.centred[:], ps[:, 0, :]).then_inc(s_v, 1)
                dve.tensor_copy(T.centred_b[:], ps[:, 4, 0:1]).then_inc(s_v, 1)
                dve.wait_ge(s_mm, 7)
                dve.tensor_copy(T.dt[:], ps[:, 0, :]).then_inc(s_v, 1)
                dve.tensor_tensor(T.in_b[:], T.in_b[:], ps[:, 4, 0:2], ALU.add).then_inc(s_v, 1)
                dve.tensor_scalar(T.inw[:], in_raw[:], ln_g, None, ALU.mult).then_inc(s_v, 1)
                for k in range(3):
                    dve.tensor_scalar(T.conv1d[:, k, :], G.ident, c1w[:, k:k + 1], None, ALU.mult).then_inc(s_v, 1)
                dve.tensor_scalar(T.d_diag[:], G.ident, d_ssm, None, ALU.mult).then_inc(s_v, 1)
                for k in range(2):
                    dve.tensor_copy(T.bc[:, 32 * k:32 * k + 32], xproj[:, 4:36]).then_inc(s_v, 1)
                dve.tensor_copy(T.pick[:], G.pick).then_inc(s_v, 1)
                dve.tensor_tensor(T.fin_b[0:HALF, :], T.fin_b[0:HALF, :], out_b[0:HALF, :], ALU.add).then_inc(s_v, 1)
                dve.wait_ge(s_zero, 11)
                dve.tensor_scalar(T.A[:], T.A[:], -1.0, None, ALU.mult).then_inc(s_v, 1)
                dve.wait_ge(s_v, 16)


def layer0(nc, G, x1_dram):
    NDA = 8
    LEAD = 3
    with ExitStack() as ctx:
        def sb(name, shape, dt=F32):
            return ctx.enter_context(nc.sbuf_tensor(name, shape, dt))

        class T:
            pass
        T.conv = sb("m_conv", [P, TAPS, P])
        T.centred, T.dt, T.bc, T.out, T.d_diag = (sb(f"m_{n}", [P, P]) for n in ("centred", "dt", "bc", "out", "d"))
        T.inw = sb("m_inw", [P, 2 * P])
        T.conv1d = sb("m_conv1d", [P, 3, P])
        T.pick = sb("m_pick", [P, 32], F32R)
        T.A = sb("m_A", [P, NS])
        T.in_b = sb("m_in_b", [P, 2])
        T.centred_b, T.conv1d_b, T.dt_b, T.fin_b, T.one = (sb(f"m_{n}", [P, 1]) for n in ("cb", "c1b", "dtb", "finb", "one"))
        T.zero = sb("m_zero", [P, W + 2])
        layer0_weights(nc, G, T)

        xn = sb("m_xn", [P, 2, ROWS + 2, W + 2])
        xnc = sb("m_xnc", [P, CH])
        tc = sb("m_tc", [P, CH])
        sq = sb("m_sq", [P, CH])
        arg = sb("m_arg", [P, CH])
        ea = sb("m_ea", [P, CH])
        ln = sb("m_ln", [P, CH])
        rest = sb("m_rest", [P, CH])
        fin = sb("m_fin", [P, CH])
        xs = sb("m_xs", [P, 2 + CH])
        xc = sb("m_xc", [P, CH])
        dt = sb("m_dtv", [P, 2, CH])
        dtx = sb("m_dtx", [P, 2, CH])
        sz = sb("m_sz", [P, 2, CH])
        bcs = sb("m_bcs", [P, 2, CH], F32R)
        dA = sb("m_dA", [P, NDA, CH])
        hb = sb("m_hb", [P, 4, CH])
        hc = sb("m_hc", [P, 4, CH])
        hs = sb("m_hs", [P, 2, CH])
        state = sb("m_state", [P, NS])
        pf = [ctx.enter_context(nc.psum_tensor(f"m_pf{i}", [P, CH], F32)) for i in range(2)]
        pB = ctx.enter_context(nc.psum_tensor("m_pB", [P, 2, CH], F32))
        pC = ctx.enter_context(nc.psum_tensor("m_pC", [P, 2, CH], F32))
        pY = ctx.enter_context(nc.psum_tensor("m_pY", [P, CH], F32))
        pO = ctx.enter_context(nc.psum_tensor("m_pO", [P, CH], F32))
        XV = G.X[:].rearrange("p b (h w) -> p b h w", h=H)

        class s:
            pass
        credited = []

        def sem(name):
            q = ctx.enter_context(nc.semaphore("m_" + name))
            credited.append(q)
            return q
        s.p1, s.tc, s.sq, s.var, s.lnv, s.rstd, s.u = (sem(n) for n in ("p1", "tc", "sq", "var", "lnv", "rstd", "u"))
        s.halo, s.xs, s.z, s.xse, s.sz, s.cv, s.xc = (sem(n) for n in ("halo", "xs", "z", "xse", "sz", "cv", "xc"))
        s.dtp, s.bc, s.xb, s.abs, s.e, s.ln, s.bhi, s.blo = (sem(n) for n in ("dtp", "bc", "xb", "abs", "e", "ln", "bhi", "blo"))
        s.r1, s.r2, s.r3, s.dt, s.dtx = (sem(n) for n in ("rest1", "rest2", "rest3", "dt", "dtx"))
        s.dterm, s.y, s.out, s.fin, s.add, s.st = (sem(n) for n in ("dterm", "y", "out", "fin", "add", "stats"))
        s.B, s.C, s.dA, s.U, s.S, s.HC, s.state = (sem(n) for n in ("B", "C", "dA", "U", "S", "HC", "state"))
        s.pair, s.sum = sem("pair"), sem("sum")
        s.norm, s.xn, s.edge = sem("norm"), sem("xn"), sem("edge")
        s.border = sem("border")
        s.stored = ctx.enter_context(nc.semaphore("m_stored"))

        PE_AT = {1: ["scan input"], 2: ["gate input"], 3: ["convolve"], 6: ["centre"], 7: ["project dt"],
                 8: ["project B, C"], 9: ["variance"]}
        ACT_AT = {2: ["scan input"], 3: ["norm"], 5: ["silu"], 6: ["pad"], 7: ["centre"], 8: ["dt argument"],
                  9: ["round B, C"], 10: ["log", "deviation"]}
        POOL_AT = {0: ["halo"], 11: ["softplus"], 12: ["dt"], 13: ["normalise"], 14: ["dt * x"]}
        DVE_AT = {10: ["rest of B, C", "softplus"]}
        TWO_AHEAD = ("norm", "centre", "variance", "deviation", "normalise")
        CONV_AT = {7: 1, 9: 1, 10: 1, 11: 2, 12: 1, 13: 1, 14: 1, 15: 1}
        SUM_AT = {5: 0, 6: 1, 8: 2, 10: 3, 12: 4, 14: 5}
        LATE_SUM_AT = {0: 6, 2: 7}

        def front_pe(g, b, c, par, what):
            pe = nc.tensor
            if what == "centre":
                after(pe, s.norm, g)
                after(pe, s.xc, g, 1)
                pe.matmul(pf[0][:], T.centred[:], xnc[:], start=True, stop=True).then_inc(s.p1, 1)
            if what == "variance":
                after(pe, s.sq, g)
                after(pe, s.xb, g, 1)
                pe.matmul(pf[1][:], G.mean64, sq[:], start=True, stop=True).then_inc(s.var, 1)
            if what == "scan input":
                after(pe, s.u, g)
                after(pe, s.blo, g, 1)
                pe.matmul(pf[0][:], T.inw[:, 0:P], tc[:], start=True, stop=True).then_inc(s.xs, 1)
            if what == "gate input":
                after(pe, s.lnv, g)
                pe.matmul(pf[1][:], T.inw[:, P:2 * P], tc[:], start=True, stop=True).then_inc(s.z, 1)
            if what == "convolve":
                after(pe, s.xse, g)
                for j in range(3):
                    mm = pe.matmul(pf[0][:], T.conv1d[:, j, :], xs[:, j:j + CH], start=(j == 0), stop=(j == 2))
                mm.then_inc(s.cv, 1)
            if what == "project dt":
                after(pe, s.sz, g)
                after(pe, s.xc, g)
                pe.matmul(pf[1][:], T.dt[:], xc[:], start=True, stop=True).then_inc(s.dtp, 1)
            if what == "project B, C":
                after(pe, s.sq, g + 1)
                pe.matmul(pf[0][:], T.bc[:], xc[:], start=True, stop=True).then_inc(s.bc, 1)

        def front_act(g, b, c, par, what):
            act = nc.scalar
            bias, scale = G.shift[:, bass.ds(b, 1)], G.rstd[:, bass.ds(b, 1)]
            if what == "norm":
                after(act, s.p1, g, 1)
                act.activation(xnc[:].rearrange("p (h w) -> p h w", w=W), XV[:, b, bass.ds(c * ROWS, ROWS), :],
                               ACT.Identity, bias=bias, scale=scale).then_inc(s.norm, 1)
            if what == "pad":
                after(act, s.out, g, 2)
                top = isinstance(c, int) and c == 0
                bottom = isinstance(c, int) and c == NCH - 1
                if top or bottom:
                    act.activation(xn[:, par, 0 if top else ROWS + 1, :], T.zero[:], ACT.Copy).then_inc(s.edge, 1)
                first = 0 if top else c * ROWS - 1
                n = ROWS + 2 - top - bottom
                act.activation(xn[:, par, int(top):int(top) + n, 1:1 + W], XV[:, b, bass.ds(first, n), :],
                               ACT.Identity, bias=bias, scale=scale).then_inc(s.xn, 1)
            if what == "centre":
                after(act, s.p1, g)
                after(act, s.z, g, 1)
                after(act, s.u, g, 1)
                act.activation(tc[:], pf[0][:], ACT.Identity, bias=T.centred_b[:, 0:1]).then_inc(s.tc, 1)
                act.activation(sq[:], pf[0][:], ACT.Square, bias=T.centred_b[:, 0:1]).then_inc(s.sq, 1)
            if what == "deviation":
                after(act, s.var, g)
                act.activation(sq[:], pf[1][:], ACT.Ln, bias=G.eps5[:, 0:1]).then_inc(s.lnv, 1)
                after(act, s.lnv, g)
                act.activation(sq[:], sq[:], ACT.Exp, scale=-0.5).then_inc(s.rstd, 1)
            if what == "scan input":
                after(act, s.xs, g)
                after(act, s.halo, g)
                act.activation(xs[:, 2:2 + CH], pf[0][:], ACT.Identity, bias=T.in_b[:, 0:1]).then_inc(s.xse, 1)
            if what == "silu":
                after(act, s.z, g)
                after(act, s.out, g, 2)
                act.activation(sz[:, par, :], pf[1][:], ACT.Silu, bias=T.in_b[:, 1:2]).then_inc(s.sz, 1)
                after(act, s.cv, g)
                after(act, s.dterm, g, 1)
                after(act, s.dtx, g, 1)
                act.activation(xc[:], pf[0][:], ACT.Silu, bias=T.conv1d_b[:, 0:1]).then_inc(s.xc, 1)
            if what == "dt argument":
                after(act, s.dtp, g)
                after(act, s.r3, g, 1)
                act.activation(ea[:], pf[1][:], ACT.Abs, bias=T.dt_b[:, 0:1]).then_inc(s.abs, 1)
                after(act, s.dt, g, 1)
                act.activation(arg[:], pf[1][:], ACT.Relu, bias=T.dt_b[:, 0:1]).then_inc(s.xb, 1)
                after(act, s.abs, g)
                act.activation(ea[:], ea[:], ACT.Exp, scale=-1.0).then_inc(s.e, 1)
            if what == "round B, C":
                after(act, s.bc, g)
                after(act, s.C, 16 * g - 16, 1)
                act.activation(bcs[:, par, :], pf[0][:], ACT.Copy).then_inc(s.bhi, 1)
            if what == "log":
                after(act, s.e, g)
                after(act, s.r3, g, 1)
                act.activation(ln[:], ea[:], ACT.Ln, bias=T.one[:, 0:1]).then_inc(s.ln, 1)

        def front_pool(g, b, c, par, what):
            pool = nc.gpsimd
            if what == "normalise":
                after(pool, s.tc, g)
                after(pool, s.rstd, g)
                pool.tensor_tensor(tc[:], tc[:], sq[:], ALU.mult).then_inc(s.u, 1)
            if what == "halo":
                after(pool, s.cv, g, 1)
                after(pool, s.xse, g, 1)
                after(pool, s.halo, g, 1)
                if isinstance(c, int) and c == 0:
                    pool.tensor_tensor(xs[:, 0:2], T.zero[:, 0:2], T.zero[:, 0:2], ALU.add).then_inc(s.halo, 1)
                else:
                    pool.tensor_tensor(xs[:, 0:2], xs[:, CH:CH + 2], T.one[:].to_broadcast([P, 2]), ALU.mult).then_inc(s.halo, 1)
            if what == "softplus":
                after(pool, s.r1, g)
                pool.tensor_tensor(rest[:], ea[:], rest[:], ALU.subtract).then_inc(s.r2, 1)
                after(pool, s.r2, g)
                after(pool, s.ln, g)
                pool.tensor_tensor(rest[:], rest[:], ln[:], ALU.add).then_inc(s.r3, 1)
            if what == "dt":
                after(pool, s.r3, g)
                after(pool, s.xb, g)
                after(pool, s.dA, 16 * g - 16, 1)
                pool.tensor_tensor(dt[:, par, :], arg[:], rest[:], ALU.add).then_inc(s.dt, 1)
            if what == "dt * x":
                after(pool, s.dt, g)
                after(pool, s.xc, g)
                after(pool, s.U, 16 * g - 16, 1)
                pool.tensor_tensor(dtx[:, par, :], dt[:, par, :], xc[:], ALU.mult).then_inc(s.dtx, 1)

        def front_dve(g, b, c, par, what):
            dve = nc.vector
            if what == "rest of B, C":
                after(dve, s.bhi, g)
                dve.tensor_tensor(bcs[32:64, par, :], pf[0][32:64, :], bcs[32:64, par, :].bitcast(F32),
                                  ALU.subtract).then_inc(s.blo, 1)
            if what == "softplus":
                after(dve, s.e, g)
                after(dve, s.dt, g, 1)
                dve.tensor_scalar(rest[:], ea[:], 1.0, -1.0, ALU.add, ALU.add).then_inc(s.r1, 1)

        def program(eng, at, chunk, front, finish, before=lambda: None):
            def parts(n, one_ahead, two_ahead):
                for what in at.get(n, ()):
                    where = two_ahead if what in TWO_AHEAD else one_ahead
                    if where:
                        front(*where, what)

            def image(b, last):
                def place(c):
                    if isinstance(c, int) and c >= NCH:
                        return b * NCH + c, (b + 1) % B, c - NCH
                    return b * NCH + c, b, c

                def one(c, par, last=True):
                    prev = place(c - 1) if last else None
                    if last and isinstance(c, int) and c == 0:
                        prev = (b * NCH - 1, b - 1, NCH - 1)
                    chunk(b * NCH + c, b, c, par, prev,
                          lambda n: parts(n, (*place(c + 1), 1 - par), (*place(c + 2), par)))
                one(0, 0, last)
                with eng.Fori(0, NCH // 2 - 2) as j:
                    one(2 * j + 1, 1)
                    one(2 * j + 2, 0)
                for c in range(NCH - 3, NCH):
                    one(c, c % 2)
            for n in range(NS):
                parts(n, None, (0, 0, 0, 0))
            for n in range(NS):
                parts(n, (0, 0, 0, 0), (1, 0, 1, 1))
            before()
            image(0, False)
            with eng.Fori(1, B) as b:
                image(b, True)
            finish(B * NCH - 1, B - 1, NCH - 1, 1)

        with nc.Block() as block:
            @block.sync
            def _(sp):
                for q in credited:
                    sp.sem_inc(q, CREDIT)
                XF = G.X[:].rearrange("p b f -> p (b f)")
                with sp.Fori(0, B * NCH) as g:
                    after(sp, s.add, g)
                    sp.dma_start(x1_dram[:, bass.ds(g * CH, CH)], XF[:, bass.ds(g * CH, CH)]).then_inc(s.stored, 16)
                sp.wait_ge(s.stored, 16 * B * NCH)

            @block.tensor
            def _(pe):
                def sum_pair(g, k):
                    after(pe, s.pair, 8 * g + k)
                    pe.matmul(pY[:], G.ident, hs[:, k % 2, :], start=False, stop=(k == NS // 2 - 1)).then_inc(s.sum, 1)

                def project_out(g, par):
                    after(pe, s.y, g)
                    pe.matmul(pO[:], T.out[:], sz[:, par, :], start=False, stop=True).then_inc(s.out, 1)

                def chunk(g, b, c, par, prev, parts_ahead):
                    def spread_B(n):
                        after(pe, s.U, NS * g + n, 2)
                        pe.matmul(pB[:, n % 2, :], T.pick[:, n:n + 1].to_broadcast([P, P]), bcs[:, par, :],
                                  start=True, stop=True).then_inc(s.B, 1)

                    def spread_C(n):
                        after(pe, s.HC, NS * g + n, 2)
                        pe.matmul(pC[:, n % 2, :], T.pick[:, NS + n:NS + n + 1].to_broadcast([P, P]), bcs[:, par, :],
                                  start=True, stop=True).then_inc(s.C, 1)
                    after(pe, s.blo, g)
                    spread_B(0)
                    spread_B(1)
                    tap = 0
                    for n in range(NS):
                        if n + 2 < NS:
                            spread_B(n + 2)
                        spread_C(n)
                        if prev and n in LATE_SUM_AT:
                            sum_pair(g - 1, LATE_SUM_AT[n])
                        if n == 4:
                            if prev:
                                project_out(g - 1, 1 - par)
                            after(pe, s.y, g, 1)
                            pe.matmul(pY[:], T.d_diag[:], xc[:], start=True, stop=False).then_inc(s.dterm, 1)
                        if n in SUM_AT:
                            sum_pair(g, SUM_AT[n])
                        for _ in range(CONV_AT.get(n, 0)):
                            if tap == 0:
                                after(pe, s.fin, g, 1)
                                after(pe, s.xn, g)
                            pe.matmul(pO[:].rearrange("p (h w) -> p h w", w=W), T.conv[:, tap, :],
                                      xn[:, par, tap // 3:tap // 3 + ROWS, tap % 3:tap % 3 + W],
                                      start=(tap == 0), stop=False)
                            tap += 1
                        parts_ahead(n)

                def finish(g, b, c, par):
                    for k in LATE_SUM_AT.values():
                        sum_pair(g, k)
                    project_out(g, par)
                program(pe, PE_AT, chunk, front_pe, finish)

            @block.scalar
            def _(act):
                after(act, s.border, 0)

                def result(g, b, c, par):
                    after(act, s.out, g)
                    after(act, s.add, g, 1)
                    act.activation(fin[:], pO[:], ACT.Relu, bias=T.fin_b[:, 0:1]).then_inc(s.fin, 1)

                def decay(g, n, par):
                    m = NS * g + n
                    after(act, s.dt, g)
                    after(act, s.S, m, NDA)
                    act.activation(dA[:, n % NDA, :], dt[:, par, :], ACT.Exp, scale=T.A[:, n:n + 1]).then_inc(s.dA, 1)

                def chunk(g, b, c, par, prev, parts_ahead):
                    for n in range(NS):
                        if n < NS - LEAD:
                            decay(g, n + LEAD, par)
                        else:
                            decay(g + 1, n + LEAD - NS, 1 - par)
                        if prev and n == 5:
                            result(*prev, 1 - par)
                        parts_ahead(n)
                program(act, ACT_AT, chunk, front_act, result, lambda: [decay(0, n, 0) for n in range(LEAD)])

            @block.gpsimd
            def _(pool):
                pool.memset(xn[:].rearrange("p a h w -> p (a h w)"), 0.0).then_inc(s.border, 1)

                def add_pair(g, k):
                    after(pool, s.HC, NS * g + 2 * k + 1)
                    after(pool, s.sum, 8 * g + k, 2)
                    pool.tensor_tensor(hs[:, k % 2, :], hc[:, (2 * k) % 4, :], hc[:, (2 * k + 1) % 4, :],
                                       ALU.add).then_inc(s.pair, 1)

                def result(g, b, c, par):
                    after(pool, s.fin, g)
                    xg = XV[:, b, bass.ds(c * ROWS, ROWS), :]
                    pool.tensor_tensor(xg, xg, fin[:].rearrange("p (h w) -> p h w", w=W), ALU.add).then_inc(s.add, 1)

                def chunk(g, b, c, par, prev, parts_ahead):
                    for n in range(NS):
                        m = NS * g + n
                        if n % 2 == 0 and n:
                            add_pair(g, n // 2 - 1)
                        after(pool, s.S, m)
                        last = hb[:, n % 4, CH - 1:CH]
                        pool.tensor_tensor(state[:, n:n + 1], last, T.one[:], ALU.mult).then_inc(s.state, 1)
                        if prev and n == 6:
                            result(*prev, 1 - par)
                        parts_ahead(n)
                    add_pair(g, NS // 2 - 1)
                program(pool, POOL_AT, chunk, front_pool, result)

            @block.vector
            def _(dve):
                def statistics(g, b, c):
                    after(dve, s.add, g)
                    dve.bn_stats(G.stats[:, b, c, :], XV[:, b, bass.ds(c * ROWS, ROWS), :]).then_inc(s.st, 1)

                def gated(g, par):
                    after(dve, s.sum, 8 * g + NS // 2 - 1)
                    after(dve, s.sz, g)
                    dve.tensor_tensor(sz[:, par, :], pY[:], sz[:, par, :], ALU.mult).then_inc(s.y, 1)

                def chunk(g, b, c, par, prev, parts_ahead):
                    def product(n):
                        m = NS * g + n
                        after(dve, s.B, m)
                        if n == 0:
                            after(dve, s.dtx, g)
                        after(dve, s.HC, m, 4)
                        after(dve, s.state, m, 4)
                        dve.tensor_tensor(hb[:, n % 4, :], dtx[:, par, :], pB[:, n % 2, :], ALU.mult).then_inc(s.U, 1)

                    def weigh(n):
                        m = NS * g + n
                        after(dve, s.S, m)
                        after(dve, s.C, m)
                        after(dve, s.pair, 8 * g + n // 2, 2)
                        dve.tensor_tensor(hc[:, n % 4, :], hb[:, n % 4, :], pC[:, n % 2, :], ALU.mult).then_inc(s.HC, 1)
                    c_is_first = isinstance(c, int) and c == 0
                    product(0)
                    for n in range(NS):
                        m = NS * g + n
                        if n + 1 < NS:
                            product(n + 1)
                        after(dve, s.U, m)
                        after(dve, s.dA, m)
                        after(dve, s.state, m, NS)
                        dve.tensor_tensor_scan(hb[:, n % 4, :], dA[:, n % NDA, :], hb[:, n % 4, :],
                                               T.zero[:, 0:1] if c_is_first else state[:, n:n + 1],
                                               ALU.mult, ALU.add).then_inc(s.S, 1)
                        if n:
                            weigh(n - 1)
                        if prev and n == 3:
                            gated(g - 1, 1 - par)
                        if prev and n == 14:
                            statistics(*prev)
                        parts_ahead(n)
                    weigh(NS - 1)

                def finish(g, b, c, par):
                    gated(g, par)
                    statistics(g, b, c)
                program(dve, DVE_AT, chunk, front_dve, finish)
                after(dve, s.st, B * NCH - 1)


def layers2_and_3(nc, G, x3_dram, out):
    E = W + 1
    NT = CH // P
    NG = TAPS * NT
    RING = 12
    GN = 11
    NM = 13
    NO = 3 * TAPS
    FIRST = 20
    NCLEAR = -(-E // RING)
    TAB_DMA = 8 * 16
    with ExitStack() as ctx:
        def sb(name, shape, dt=F32):
            return ctx.enter_context(nc.sbuf_tensor(name, shape, dt))

        def sem(name):
            return ctx.enter_context(nc.semaphore(name))

        def bank(name, shape):
            return ctx.enter_context(nc.psum_tensor(name, shape, F32))
        table = nc.dram_tensor("corner_table", (2, E, E, 4 * P), F32).ap()
        base = sb("d_base", [P, 2, NCH, NG])
        off_w = sb("d_off_w", [P, TAPS, NO])
        off_b = sb("d_off_b", [NO, 1])
        dcn_w = sb("d_dcn_w", [P, TAPS, P])
        vecs = sb("d_vecs", [P, 3])
        w7, edge, w4 = G.w7, G.edge, G.w4
        s_const, s_zero, s_border = sem("d_constants"), sem("d_zeros"), sem("d_border_zeroed")
        with ExitStack() as ctx2:
            def sb2(name, shape, dt=F32):
                return ctx2.enter_context(nc.sbuf_tensor(name, shape, dt))
            xn2 = sb2("l2_xn", [P, ROWS + 2 * PADH, WP])
            gate = sb2("l2_gate", [P, CH])
            prod = sb2("l2_prod", [P, CH])
            zero = sb2("d_zero", [P, PADH * WP])
            st3 = sb2("d_stats", [P, NCH * 6])
            mv3 = sb2("d_mv", [P, 2])
            mom, gm = sb2("d_moments", [P, 2]), sb2("d_group_moments", [P, 2])
            t3 = sb2("d_gn_tmp", [P, 2])
            norm3 = sb2("d_norm", [P, 2])
            xn = sb2("d_xn", [P, ROWS + 2, W + 2])
            xc = sb2("d_xc", [P, CH])
            om_s = sb2("d_om", [NO, CH])
            tT = sb2("d_tT", [P, NT, P])
            mask = sb2("d_mask", [P, NG])
            V, F, T1 = (sb2(f"d_{n}", [P, 2, NG]) for n in ("V", "F", "T1"))
            I = sb2("d_I", [P, 2, NG], mybir.dt.int32)
            WT = sb2("d_WT", [P, 2, 2, NG])
            J = sb2("d_J", [P, NG])
            tb = sb2("d_table_base", [P, 1])
            IDX = sb2("d_idx", [P, 2 * NCH, NG], U32)
            W4 = sb2("d_w4", [P, 2 * NCH, NG * 4])
            idx_now = sb2("d_idx_now", [P, NG], U32)
            w_now = sb2("d_w_now", [P, 2, NG * 4])
            ring = sb2("d_ring", [P, RING, 4 * P])
            R = sb2("d_mix", [P, 3, NT, P])
            samp = sb2("d_samp", [P, 3, CH])
            ps_off = ctx2.enter_context(nc.psum_tensor("d_ps_off", [P, CH], F32))
            ps_om = ps_off[:, 0:NT * NO].rearrange("p (t o) -> p t o", o=NO)
            ps3 = ctx2.enter_context(nc.psum_tensor("l2_ps_conv", [P, CH], F32))
            ps4 = ctx2.enter_context(nc.psum_tensor("l2_ps_gate", [P, CH], F32))
            ps_tab = ctx2.enter_context(nc.psum_tensor("d_ps_tab", [P, NT, P], F32))
            ps_s = [ctx2.enter_context(nc.psum_tensor(f"d_ps_s{i}", [P, NT, P], F32)) for i in range(3)]
            ps_out = ctx2.enter_context(nc.psum_tensor("d_ps_out", [P, CH], F32))
            s_offs = sem("d_offsets_out")
            s_omT = sem("d_offsets_turned")
            s_tabT = sem("d_table_turned")
            s_tT = sem("d_table_tile_out")
            s_tab = sem("d_table_stored")
            s_math = sem("d_index_steps")
            s_mix = sem("d_mix_steps")
            s_turn = sem("d_samples_turned")
            s_samp = sem("d_samples_out")
            s_dcn = sem("d_taps_summed")
            s_out = sem("d_output_kept")
            s_xn2, s_edge2, s_t4, s_gate = sem("c_xn_ready"), sem("c_edge_zero"), sem("c_gate_summed"), sem("c_gate_copied")
            s_t3, s_prod, s_x, s_st2 = sem("c_conv_done"), sem("c_product"), sem("c_x_updated"), sem("c_stats")
            s_gn, s_gm, s_sd = sem("d_gn_steps"), sem("d_gn_moments"), sem("d_gn_deviation")
            s_x3 = sem("c_x3_stored")
            s_edge3 = sem("d_edge_zero")
            s_xn, s_xc, s_conv, s_mask = sem("d_xn_ready"), sem("d_xc_ready"), sem("d_offsets_summed"), sem("d_mask")
            s_wnow, s_inow, s_r0, s_st = sem("d_w_now"), sem("d_idx_now"), sem("d_corner0"), sem("d_stats")
            s_passed, s_passed_dve, s_passed_act = (sem(f"d_waits_passed{n}") for n in ("", "_dve", "_act"))
            s_clear = sem("d_image_start_cleared")
            s_land = [sem(f"d_landed{i}") for i in range(RING)]
            s_tb = sem("d_table_base_set")
            XV = G.X[:].rearrange("p b (h w) -> p b h w", h=H)
            XF = G.X[:].rearrange("p b f -> p (b f)")
            SF = G.stats[:].rearrange("p b c s -> p (b c) s")
            SI = G.stats[:].rearrange("p b c s -> p b (c s)")

            def passes(eng, body, head=lambda pL, pT, pG: None, before=lambda: None, end=lambda: None):
                def chunks(pL, pT, pG, first=False):
                    head(pL, pT, pG)
                    if first:
                        before()
                    for c in (0, 1):
                        body(pL, pT, pG, c, c, c > 0 or not first)
                    with eng.Fori(1, NCH // 2 - 1) as j:
                        for i in range(2):
                            body(pL, pT, pG, 2 * j + i, i, True)
                    for c in (NCH - 2, NCH - 1):
                        body(pL, pT, pG, c, c % 2, True)
                chunks(0, None, None)
                chunks(1, 0, None)
                chunks(2, 1, 0, True)
                with eng.Fori(2, B - 1) as p:
                    chunks(p + 1, p, p - 1)
                chunks(None, B - 1, B - 2)
                chunks(None, None, B - 1)
                end()

            def at_edge(c, where):
                return isinstance(c, int) and c == where

            def mixed(m):
                return 3 * (m - m % 2) + 4 + m % 2 + 1

            with nc.Block() as block:
                @block.sync
                def _(sp):
                    for dst, n in ((base[:].rearrange("p a c k -> p (a c k)"), "base"), (off_w[:], "off_w"),
                                   (off_b[:], "off_b"), (dcn_w[:], "dcn_w"), (vecs[:, 0:1], "dcn_b"),
                                   (vecs[:, 1:2], "gamma"), (vecs[:, 2:3], "beta")):
                        sp.dma_start(dst, G.d[n]).then_inc(s_const, 16)
                    for s in (s_xn2, s_edge2, s_t4, s_gate, s_t3, s_prod, s_x, s_st2, s_gn, s_gm, s_sd, s_offs, s_omT, s_tabT, s_tT, s_tab, s_math, s_mix, s_turn, s_samp, s_dcn, s_out):
                        sp.sem_inc(s, CREDIT)
                    sp.wait_ge(s_const, 16 * 7)

                @block.gpsimd
                def _(pool):
                    pool.memset(xn[:].rearrange("p h w -> p (h w)"), 0.0).then_inc(s_zero, 1)
                    pool.memset(xn2[:].rearrange("p h w -> p (h w)"), 0.0).then_inc(s_zero, 1)
                    pool.memset(zero[:], 0.0).then_inc(s_zero, 1)
                    pool.memset(tb[:], 0.0).then_inc(s_zero, 1)
                    pool.memset(ring[:].rearrange("p r e -> p (r e)"), 0.0).then_inc(s_zero, 1)
                    pool.wait_ge(s_zero, 5)

            with nc.Block() as block:
                @block.sync
                def _(sp):
                    for side in range(2):
                        sp.dma_start(table[0, side * (E - 1), :, 2 * side * P:2 * (side + 1) * P],
                                     ring[0:E, 0, 0:2 * P]).then_inc(s_border, 16)
                    sp.wait_ge(s_border, 32)
                    for slot in range(4):
                        sp.dma_start(table[0, :, slot % 2 * (E - 1), slot * P:(slot + 1) * P],
                                     ring[0:E, 0, 0:P]).then_inc(s_border, 16)
                    sp.wait_ge(s_border, 96)

                    def store(pL, pT, pG, c, par, prev):
                        if pT is None:
                            return
                        gT = NCH * pT + c
                        sp.wait_ge(s_tT, gT + (1 + CREDIT))
                        for yy in range(2):
                            for dy in range(2):
                                for dx in range(2):
                                    slot = 2 * dy + dx
                                    dst = table[pT % 2, bass.ds(ROWS * c + (yy + 1 - dy), NT, 2), 1 - dx:1 - dx + W,
                                                slot * P:(slot + 1) * P].rearrange("q x c -> x q c")
                                    sp.dma_start(dst, tT[yy * W:(yy + 1) * W, :, :]).then_inc(s_tab, 16)

                    def image_start(pL, pT, pG):
                        if pT is not None:
                            after(sp, s_x, NCH * pT + (NCH - 1))
                            sp.dma_start(x3_dram[pT], G.X[:, pT, :]).then_inc(s_x3, 16)
                        if isinstance(pG, int) and pG == 0:
                            sp.wait_ge(s_clear, 16 * NCLEAR)
                    passes(sp, store, image_start)
                    sp.wait_ge(s_tab, TAB_DMA * NCH * B + CREDIT)
                    sp.wait_ge(s_x3, 16 * B)

                @block.gpsimd
                def _(pool):
                    flat = table.rearrange("a y x e -> (a y x) e")
                    for x0 in range(0, E, RING):
                        n = min(RING, E - x0)
                        pool.dma_start(table[1, :, x0:x0 + n, :], ring[0:E, 0:n, :]).then_inc(s_clear, 16)

                    def gather(pL, pT, pG, c, par, prev):
                        if pG is None:
                            return
                        gG = NCH * pG + c
                        pool.wait_ge(s_math, NM * gG + (NM + CREDIT))
                        for m in range(NG):
                            if m in (0, FIRST):
                                lo, hi = (0, FIRST) if m == 0 else (FIRST, NG)
                                apart(pool, s_passed)
                                pool.tensor_copy(idx_now[:, lo:hi], IDX[:, gG % (2 * NCH), lo:hi]).then_inc(s_inow, 1)
                                pool.wait_ge(s_inow, 2 * gG + (1 if m == 0 else 2))
                            pool.wait_ge(s_mix, 3 * NG * gG + (mixed(m + NG - RING) - 3 * NG + CREDIT))
                            apart(pool, s_passed)
                            pool.indirect_dma_start(
                                out=ring[:, m % RING, :], out_offset=None, in_=flat,
                                in_offset=bass.IndirectOffsetOnAxis(ap=idx_now[:, m:m + 1], axis=0),
                            ).then_inc(s_land[m % RING], 16)

                    def whole_table(pL, pT, pG):
                        if pG is not None:
                            pool.wait_ge(s_clear, 16 * NCLEAR)
                            pool.wait_ge(s_tab, TAB_DMA * NCH * pG + (TAB_DMA * NCH + CREDIT))
                            apart(pool, s_passed)
                    passes(pool, gather, whole_table)

                @block.scalar
                def _(act):
                    def image_start(pL, pT, pG):
                        if pT is not None:
                            after(act, s_gn, GN * pT + 8)
                            after(act, s_gn, GN * pT, 1)
                            act.activation(t3[:, 1:2], t3[:, 0:1], ACT.Sqrt, bias=G.eps5[:, 0:1]).then_inc(s_sd, 1)
                        if pG is not None:
                            act.wait_ge(s_x3, 16 * pG + 16)

                    def rows(dst, sem_ready, sem_edge, p, c, halo, scale, bias):
                        top, bottom = at_edge(c, 0), at_edge(c, NCH - 1)
                        if top or bottom:
                            r = 0 if top else halo + ROWS
                            act.activation(dst[:, r:r + halo, :], zero[:, 0:halo * dst.shape[2]].rearrange("p (h w) -> p h w", h=halo),
                                           ACT.Copy).then_inc(sem_edge, 1)
                        lo = halo if top else 0
                        n = ROWS + 2 * halo - (halo if top or bottom else 0)
                        side = (dst.shape[2] - W) // 2
                        act.activation(dst[:, lo:lo + n, side:side + W], XV[:, p, bass.ds(ROWS * c + (lo - halo), n), :],
                                       ACT.Identity, bias=bias, scale=scale).then_inc(sem_ready, 1)

                    def keep_samples(gG, k):
                        act.wait_ge(s_turn, NG * gG + (NT * (k + 1) + CREDIT))
                        act.wait_ge(s_dcn, TAPS * gG + (k - 3 + 1 + CREDIT))
                        act.activation(samp[:, k % 3, :], ps_s[k % 3][:].rearrange("p t c -> p (t c)"),
                                       ACT.Copy).then_inc(s_samp, 1)

                    def keep_output(gG, par):
                        act.wait_ge(s_dcn, TAPS * gG + (TAPS + CREDIT))
                        act.activation(XF[:, bass.ds(CH * gG, CH)], ps_out[:], ACT.Identity,
                                       bias=vecs[:, 0:1]).then_inc(s_out, 1)

                    def chunk(pL, pT, pG, c, par, prev):
                        doL, doT, doG = pL is not None, pT is not None, pG is not None
                        c_is_first = at_edge(c, 0)
                        if doL:
                            gL = NCH * pL + c
                        if doT:
                            gT = NCH * pT + c
                        if doG:
                            gG = NCH * pG + c
                        for k in range(TAPS):
                            if doG:
                                if k == 0:
                                    act.wait_ge(s_wnow, gG + 1)
                                for t in range(NT):
                                    m = NT * k + t
                                    act.wait_ge(s_land[m % RING], 16 * (NG // RING) * gG + 16 * (m // RING + 1))
                                    act.wait_ge(s_turn, NG * gG + (m - 3 * NT + 1 + CREDIT))
                                    act.activation(R[:, k % 3, t, :], ring[:, m % RING, 0:P], ACT.Copy,
                                                   scale=w_now[:, par, 4 * m:4 * m + 1]).then_inc(s_r0, 1)
                            if doT and k == 0:
                                if c_is_first:
                                    after(act, s_gn, GN * pT + (GN - 1))
                                rows(xn, s_xn, s_edge3, pT, c, 1, norm3[:, 0:1], norm3[:, 1:2])
                                act.wait_ge(s_tabT, NT * gT + CREDIT)
                                apart(act, s_passed_act)
                                act.activation(xc[:], G.X[:, pT, bass.ds(CH * c, CH)], ACT.Identity,
                                               bias=norm3[:, 1:2], scale=norm3[:, 0:1]).then_inc(s_xc, 1)
                            if doL and k == 2:
                                after(act, s_t3, gL, 1)
                                rows(xn2, s_xn2, s_edge2, pL, c, PADH, G.rstd[:, bass.ds(pL, 1)], G.shift[:, bass.ds(pL, 1)])
                            if doL and k == 7:
                                after(act, s_t4, gL)
                                after(act, s_prod, gL, 1)
                                act.activation(gate[:], ps4[:], ACT.Copy).then_inc(s_gate, 1)
                            if doG and k >= 1:
                                keep_samples(gG, k - 1)
                            if prev and k == 0 and doG:
                                keep_samples(gG - 1, TAPS - 1)
                            if prev and k == 1 and doG:
                                keep_output(gG - 1, 1 - par)
                            if doT and k == 3:
                                act.wait_ge(s_tabT, NT * gT + (NT + CREDIT))
                                act.wait_ge(s_tab, TAB_DMA * gT + CREDIT)
                                act.activation(tT[:], ps_tab[:], ACT.Copy).then_inc(s_tT, 1)
                            if doT and k == 6:
                                act.wait_ge(s_conv, gT + 1)
                                act.wait_ge(s_omT, NT * gT + CREDIT)
                                act.activation(om_s[:], ps_off[0:NO, :], ACT.Identity, bias=off_b[:, 0:1]).then_inc(s_offs, 1)
                            if doT and k == 8:
                                act.wait_ge(s_omT, NT * gT + (NT + CREDIT))
                                act.wait_ge(s_math, NM * gT + CREDIT)
                                act.activation(mask[:].rearrange("p (k t) -> p k t", t=NT),
                                               ps_om[:, :, 2 * TAPS:].rearrange("p t k -> p k t"),
                                               ACT.Sigmoid).then_inc(s_mask, 1)

                    def end():
                        keep_samples(B * NCH - 1, TAPS - 1)
                        keep_output(B * NCH - 1, 1)
                    passes(act, chunk, image_start, end=end)

                @block.tensor
                def _(pe):
                    def contract(gG, k):
                        pe.wait_ge(s_samp, TAPS * gG + (k + 1 + CREDIT))
                        if k == 0:
                            pe.wait_ge(s_out, gG + CREDIT)
                        pe.matmul(ps_out[:], dcn_w[:, k, :], samp[:, k % 3, :], start=(k == 0),
                                  stop=(k == TAPS - 1)).then_inc(s_dcn, 1)

                    def gate_taps(gL):
                        after(pe, s_xn2, gL)
                        after(pe, s_gate, gL, 1)
                        for k in range(GT):
                            mm = pe.matmul(ps4[:].rearrange("p (h w) -> p h w", w=W), w4[:, k, :],
                                           xn2[:, PADH:PADH + ROWS, 2 * k:2 * k + W], start=(k == 0), stop=(k == GT - 1))
                        mm.then_inc(s_t4, 1)

                    def column_taps(gL, c, taps):
                        o3 = ps3[:].rearrange("p (h w) -> p h w", w=W)
                        for j in taps:
                            if j == 0:
                                after(pe, s_prod, gL, 1)
                            if j == K7 - 1:
                                if at_edge(c, 0):
                                    for e in range(2):
                                        pe.matmul(o3[:, 0, :], edge[:, e, :], xn2[:, PADH + e, PADW:PADW + W],
                                                  start=False, stop=False, skip_group_check=True)
                                if at_edge(c, NCH - 1):
                                    for e in range(2):
                                        pe.matmul(o3[:, ROWS - 1, :], edge[:, 2 + e, :],
                                                  xn2[:, PADH + ROWS - 2 + e, PADW:PADW + W],
                                                  start=False, stop=False, skip_group_check=True)
                            mm = pe.matmul(o3, w7[:, j, :], xn2[:, j:j + ROWS, PADW:PADW + W],
                                           start=(j == 0), stop=(j == K7 - 1), skip_group_check=True)
                        if K7 - 1 in taps:
                            mm.then_inc(s_t3, 1)

                    def image_start(pL, pT, pG):
                        if pT is not None:
                            after(pe, s_gn, GN * pT + 4)
                            pe.matmul(ps3[:, 0:2], G.group_mean, mom[:], start=True, stop=True).then_inc(s_gm, 1)

                    def chunk(pL, pT, pG, c, par, prev):
                        doL, doT, doG = pL is not None, pT is not None, pG is not None
                        c_is_first = at_edge(c, 0)
                        if doL:
                            gL = NCH * pL + c
                        if doT:
                            gT = NCH * pT + c
                        if doG:
                            gG = NCH * pG + c

                        for k in range(TAPS):
                            if doG:
                                pe.wait_ge(s_samp, TAPS * gG + (k - 3 + 1 + CREDIT))
                                for t in range(NT):
                                    pe.wait_ge(s_mix, 3 * NG * gG + (mixed(NT * k + t) + CREDIT))
                                    pe.transpose(ps_s[k % 3][:, t, :], R[:, k % 3, t, :], G.ident).then_inc(s_turn, 1)
                                if k >= 1:
                                    contract(gG, k - 1)
                                elif prev:
                                    contract(gG - 1, TAPS - 1)
                            if doT:
                                if k == 1:
                                    pe.wait_ge(s_xn, gT + 1)
                                    pe.wait_ge(s_math, NM * gT + CREDIT)
                                for tap in range(max(2 * k - 2, 0), min(2 * k, TAPS)):
                                    ki, kj = tap // 3, tap % 3
                                    mm = pe.matmul(ps_off[0:NO, :], off_w[:, tap, :],
                                                   xn[:, ki:ki + ROWS, kj:kj + W],
                                                   start=(tap == 0), stop=(tap == TAPS - 1))
                                    if tap == TAPS - 1:
                                        mm.then_inc(s_conv, 1)
                                if k == 1:
                                    pe.wait_ge(s_xc, gT + 1)
                                    pe.wait_ge(s_tT, gT + CREDIT)
                                    for t in range(NT):
                                        pe.transpose(ps_tab[:, t, :], xc[:, t * P:(t + 1) * P], G.ident).then_inc(s_tabT, 1)
                                if k == 7:
                                    pe.wait_ge(s_offs, gT + (1 + CREDIT))
                                    for t in range(NT):
                                        pe.matmul(ps_om[:, t, :], om_s[:, t * P:(t + 1) * P], G.ident[0:NO, 0:NO],
                                                  start=True, stop=True).then_inc(s_omT, 1)
                            if doL and k == 4:
                                gate_taps(gL)
                            if doL and k >= 5:
                                column_taps(gL, c, {5: (0,), 6: (1, 2, 3), 7: (4,), 8: (5, 6)}[k])
                    passes(pe, chunk, image_start, end=lambda: contract(B * NCH - 1, TAPS - 1))

                @block.vector
                def _(dve):
                    def update(gL, next_rows):
                        after(dve, s_t3, gL)
                        after(dve, s_gate, gL)
                        after(dve, s_x, gL, 1)
                        dve.tensor_tensor(prod[:], ps3[:], gate[:], ALU.mult).then_inc(s_prod, 1)
                        after(dve, s_prod, gL)
                        if next_rows:
                            after(dve, s_xn2, gL + 1)
                        x = XF[:, bass.ds(CH * gL, CH)]
                        dve.tensor_tensor(x, x, prod[:], ALU.add).then_inc(s_x, 1)
                        after(dve, s_x, gL)
                        dve.bn_stats(SF[:, gL, :], x).then_inc(s_st2, 1)

                    def image_norm(p):
                        step = 0

                        def do(make, alone=False):
                            nonlocal step
                            after(dve, s_gn, GN * p + step, 1)
                            if alone:
                                apart(dve, s_passed_dve)
                            make().then_inc(s_gn, 1)
                            step += 1
                        after(dve, s_st2, NCH * p + (NCH - 1))
                        do(lambda: dve.tensor_scalar(st3[:], SI[:, p, :], 1.0, None, ALU.mult))
                        do(lambda: dve.bn_aggr(mv3[:], st3[:]), True)
                        do(lambda: dve.tensor_copy(mom[:, 0:1], mv3[:, 0:1]))
                        do(lambda: dve.tensor_tensor(t3[:, 0:1], mv3[:, 0:1], mv3[:, 0:1], ALU.mult))
                        do(lambda: dve.tensor_tensor(mom[:, 1:2], mv3[:, 1:2], t3[:, 0:1], ALU.add))
                        after(dve, s_gm, p)
                        do(lambda: dve.tensor_copy(gm[:], ps3[:, 0:2]))
                        do(lambda: dve.tensor_tensor(mv3[:, 0:1], gm[:, 0:1], gm[:, 0:1], ALU.mult))
                        do(lambda: dve.tensor_copy(mv3[:, 1:2], gm[:, 1:2]))
                        do(lambda: dve.tensor_tensor(t3[:, 0:1], mv3[:, 1:2], mv3[:, 0:1], ALU.subtract))
                        after(dve, s_sd, p)
                        do(lambda: dve.reciprocal(norm3[:, 0:1], t3[:, 1:2]))
                        do(lambda: dve.scalar_tensor_tensor(norm3[:, 1:2], gm[:, 0:1], -1.0, norm3[:, 0:1], ALU.mult, ALU.mult))

                    def image_start(pL, pT, pG):
                        if pT is not None:
                            update(NCH * pT + (NCH - 1), False)
                            image_norm(pT)
                        if pT is not None and pG is not None:
                            dve.wait_ge(s_math, NM * NCH * pT + CREDIT)
                            dve.tensor_scalar(tb[:], tb[:], -1.0, float(E * E), ALU.mult, ALU.add).then_inc(s_tb, 1)
                            dve.wait_ge(s_tb, pT)
                            apart(dve, s_passed_dve)

                    def indices(pT, gT, c):
                        step = 0

                        def do(make):
                            nonlocal step
                            dve.wait_ge(s_math, NM * gT + (step + CREDIT))
                            make().then_inc(s_math, 1)
                            step += 1
                        slot = gT % (2 * NCH)
                        dve.wait_ge(s_mask, gT + 1)
                        do(lambda: dve.tensor_tensor(V[:].rearrange("p a (k t) -> p a k t", t=NT),
                                                     ps_om[:, :, 0:2 * TAPS].rearrange("p t (k a) -> p a k t", a=2),
                                                     base[:, :, c, :].rearrange("p a (k t) -> p a k t", t=NT), ALU.add))
                        do(lambda: dve.tensor_scalar(V[:], V[:], 0.0, float(H + 1), ALU.max, ALU.min))
                        do(lambda: dve.tensor_copy(I[:], V[:]))
                        do(lambda: dve.tensor_copy(F[:], I[:]))
                        do(lambda: dve.tensor_tensor(T1[:], F[:], V[:], ALU.is_gt))
                        do(lambda: dve.tensor_tensor(F[:], F[:], T1[:], ALU.subtract))
                        do(lambda: dve.tensor_scalar(F[:], F[:], float(H), None, ALU.min))
                        do(lambda: dve.tensor_tensor(WT[:, :, 1, :], V[:], F[:], ALU.subtract))
                        do(lambda: dve.tensor_scalar(WT[:, :, 0, :], WT[:, :, 1, :], -1.0, 1.0, ALU.mult, ALU.add))
                        do(lambda: dve.scalar_tensor_tensor(J[:], F[:, 0, :], float(E), F[:, 1, :], ALU.mult, ALU.add))
                        do(lambda: dve.tensor_scalar(IDX[:, slot, :], J[:], tb[:, 0:1], None, ALU.add))
                        do(lambda: dve.tensor_tensor(WT[:, 0, :, :], WT[:, 0, :, :],
                                                     mask[:].unsqueeze(1).to_broadcast([P, 2, NG]), ALU.mult))
                        do(lambda: dve.tensor_tensor(
                            W4[:, slot, :].rearrange("p (n y x) -> p n y x", y=2, x=2),
                            WT[:, 0, :, :].rearrange("p y n -> p n y").unsqueeze(3).to_broadcast([P, NG, 2, 2]),
                            WT[:, 1, :, :].rearrange("p x n -> p n x").unsqueeze(2).to_broadcast([P, NG, 2, 2]),
                            ALU.mult))

                    def weights(gG, par, last_pass=False):
                        if last_pass:
                            dve.wait_ge(s_math, NM * NCH * B + CREDIT)
                        else:
                            dve.wait_ge(s_math, NM * gG + (NM + CREDIT))
                        if not isinstance(gG, int) or gG >= 2:
                            dve.wait_ge(s_mix, 3 * NG * gG + (CREDIT - 3 * NG))
                        dve.tensor_copy(w_now[:, par, :], W4[:, gG % (2 * NCH), :]).then_inc(s_wnow, 1)

                    def statistics(gG):
                        dve.wait_ge(s_out, gG + (1 + CREDIT))
                        dve.bn_stats(SF[:, gG, :], XF[:, bass.ds(CH * gG, CH)]).then_inc(s_st, 1)

                    def chunk(pL, pT, pG, c, par, prev):
                        doL, doT, doG = pL is not None, pT is not None, pG is not None
                        c_is_first = at_edge(c, 0)
                        if doL:
                            gL = NCH * pL + c
                        if doT:
                            gT = NCH * pT + c
                        if doG:
                            gG = NCH * pG + c
                            dve.wait_ge(s_wnow, gG + 1)
                        for k in range(TAPS):
                            if doG:
                                for t in range(0, NT, 2):
                                    first = 3 * (NT * k + t)
                                    for corner in range(1, 4):
                                        for j in range(2):
                                            m = NT * k + t + j
                                            if corner == 1:
                                                dve.wait_ge(s_r0, NG * gG + (m + 1))
                                            else:
                                                dve.wait_ge(s_mix, 3 * NG * gG + (first + 2 * (corner - 2) + j + 1 + CREDIT))
                                            dve.scalar_tensor_tensor(
                                                R[:, k % 3, t + j, :], ring[:, m % RING, corner * P:(corner + 1) * P],
                                                w_now[:, par, 4 * m + corner:4 * m + corner + 1], R[:, k % 3, t + j, :],
                                                ALU.mult, ALU.add).then_inc(s_mix, 1)
                            if doG and prev and k == 3:
                                statistics(gG - 1)
                            if doG and k == 5:
                                weights(gG + 1, 1 - par, not doT)
                            if doL and k == 3 and not c_is_first:
                                update(gL - 1, True)
                            if doT and k == 8:
                                indices(pT, gT, c)
                    passes(dve, chunk, image_start, lambda: weights(0, 0), lambda: statistics(B * NCH - 1))
                    dve.wait_ge(s_st, B * NCH)

        HB = HW // 2
        mv = sb("b_mv", [P, 2])
        std = sb("b_std", [P, 1])
        scale, shift = sb("b_scale", [P, 1]), sb("b_shift", [P, 1])
        x3 = sb("b_x3", [P, 4, HB])
        z = sb("b_z", [P, 2, HB])
        s_step, s_std, s_z, s_y = (sem(n) for n in ("b_step", "b_std_done", "b_z", "b_y"))
        s_x3 = [sem(f"b_x3_landed{i}") for i in range(4)]
        s_sum, s_stored = sem("b_sum"), sem("b_stored")
        with nc.Block() as block:
            @block.vector
            def _(dve):
                dve.bn_aggr(mv[:], G.stats[:].rearrange("p b c s -> p (b c s)")).then_inc(s_step, 1)
                dve.wait_ge(s_std, 1)
                dve.reciprocal(scale[:], std[:]).then_inc(s_step, 1)
                dve.wait_ge(s_step, 2)
                dve.tensor_tensor(scale[:], scale[:], vecs[:, 1:2], ALU.mult).then_inc(s_step, 1)
                dve.wait_ge(s_step, 3)
                dve.tensor_tensor(mv[:, 1:2], mv[:, 0:1], scale[:], ALU.mult).then_inc(s_step, 1)
                dve.wait_ge(s_step, 4)
                dve.tensor_tensor(shift[:], vecs[:, 2:3], mv[:, 1:2], ALU.subtract).then_inc(s_step, 1)
                for n in range(2 * B):
                    b, h = n // 2, n % 2
                    dve.wait_ge(s_z, n + 1)
                    x = G.X[:, b, h * HB:(h + 1) * HB]
                    dve.scalar_tensor_tensor(x, z[:, n % 2, :], 0.1, z[:, n % 2, :], ALU.mult, ALU.max).then_inc(s_y, 1)
                    dve.wait_ge(s_y, n + 1)
                    dve.wait_ge(s_x3[n % 4], 16 * (n // 4 + 1))
                    dve.tensor_tensor(x, x, x3[:, n % 4, :], ALU.add).then_inc(s_sum, 1)

            @block.scalar
            def _(act):
                act.wait_ge(s_step, 1)
                act.activation(std[:], mv[:, 1:2], ACT.Sqrt, bias=G.eps5[:, 0:1]).then_inc(s_std, 1)
                act.wait_ge(s_step, 5)
                for n in range(2 * B):
                    b, h = n // 2, n % 2
                    if n >= 2:
                        act.wait_ge(s_y, n - 1)
                    act.activation(z[:, n % 2, :], G.X[:, b, h * HB:(h + 1) * HB], ACT.Identity,
                                   bias=shift[:, 0:1], scale=scale[:, 0:1]).then_inc(s_z, 1)

            @block.gpsimd
            def _(pool):
                for n in range(2 * B):
                    b, h = n // 2, n % 2
                    if n >= 4:
                        pool.wait_ge(s_sum, n - 3)
                    pool.dma_start(x3[:, n % 4, :], x3_dram[b][:, h * HB:(h + 1) * HB]).then_inc(s_x3[n % 4], 16)

            @block.sync
            def _(sp):
                for n in range(2 * B):
                    b, h = n // 2, n % 2
                    sp.wait_ge(s_sum, n + 1)
                    sp.dma_start(out[b][:, h * HB:(h + 1) * HB], G.X[:, b, h * HB:(h + 1) * HB]).then_inc(s_stored, 16)
                sp.wait_ge(s_stored, 16 * 2 * B)


def build_program(nc, d, out):
    class G:
        pass
    G.d = d
    x1 = nc.dram_tensor("x1_scratch", (P, B * HW), F32).ap()
    x3 = nc.dram_tensor("x3_scratch", (B, P, HW), F32).ap()
    with ExitStack() as ctx:
        def sb(name, shape, dt=F32):
            return ctx.enter_context(nc.sbuf_tensor(name, shape, dt))
        G.X = sb("X", [P, B, HW])
        G.stats = sb("stats", [P, B, NCH, 6])
        G.small = sb("small", [P, 4 * P + 32])
        G.ident = G.small[:, 0:P]
        G.group_mean = G.small[:, P:2 * P]
        G.mean64 = G.small[:, 2 * P:3 * P]
        G.centre = G.small[:, 3 * P:4 * P]
        G.pick = G.small[:, 4 * P:4 * P + 32]
        G.eps5 = sb("eps5", [P, 1])
        G.rstd = sb("rstd", [P, B])
        G.shift = sb("shift", [P, B])
        load_image_and_statistics(nc, G, d["x"])
        for n, stage in (("L0", lambda: layer0(nc, G, x1)), ("L1", lambda: layer1(nc, G, ctx, x1)),
                         ("L2", lambda: layers2_and_3(nc, G, x3, out))):
            G.tag = n
            group_norm_scales(nc, ctx, G)
            stage()


def lay_out(i):
    def c(a):
        return np.ascontiguousarray(a)
    small, base = host_constants()
    o = {"x": c(i["x"].reshape(B, P, HW)), "small": small, "base": base}
    o["conv_w"] = c(i["L0_conv_conv_w"].transpose(1, 2, 3, 0).reshape(HALF, TAPS, HALF))
    o["conv_b"] = c(i["L0_conv_conv_b"].reshape(HALF, 1))
    o["expand_wT"] = c(i["L0_conv_expand_w"].T)
    o["concat_w"] = c(i["L0_conv_concat_w"])
    o["concat_b"] = c(i["L0_conv_concat_b"].reshape(HALF, 1))
    o["ln_g"] = c(i["L0_conv_ln_g"].reshape(HALF, 1))
    o["ln_b"] = c(i["L0_conv_ln_b"].reshape(HALF, 1))
    o["in_w"] = c(i["L0_conv_in_w"])
    o["in_b"] = c(i["L0_conv_in_b"].reshape(2, P).T)
    o["conv1d_w"] = c(i["L0_conv_conv1d_w"].T)
    o["conv1d_b"] = c(i["L0_conv_conv1d_b"].reshape(P, 1))
    o["xproj_w"] = c(i["L0_conv_xproj_w"])
    o["xproj_dtT"] = c(i["L0_conv_xproj_w"][:, :4].T)
    o["dt_w"] = c(i["L0_conv_dt_w"])
    o["dt_b"] = c(i["L0_conv_dt_b"].reshape(P, 1))
    o["A_log"] = c(i["L0_conv_A_log"])
    o["D_ssm"] = c(i["L0_conv_D_ssm"].reshape(P, 1))
    o["out_w"] = c(i["L0_conv_out_w"])
    o["out_b"] = c(i["L0_conv_out_b"].reshape(HALF, 1))
    for n in ("down", "up", "right", "left"):
        o[f"w_{n}"] = c(i[f"L1_conv_w_{n}"].transpose(1, 2, 0).reshape(P, TAPS * P))
    o["l2_w1"] = c(i["L2_conv_w1"][..., 0].transpose(1, 2, 0))
    o["l2_w3"] = c(i["L2_conv_w3"][:, 0, :, 0].T.reshape(1, 3 * P))
    o["l2_w4"] = c(i["L2_conv_w4"][:, :, 0, :])
    o["off_w"] = c(i["L3_conv_offset_w"].transpose(1, 2, 3, 0).reshape(P, TAPS, 3 * TAPS))
    o["off_b"] = c(i["L3_conv_offset_b"].reshape(3 * TAPS, 1))
    o["dcn_w"] = c(i["L3_conv_dcn_w"].transpose(1, 2, 3, 0).reshape(P, TAPS, P))
    for n in ("dcn_b", "gamma", "beta"):
        o[n] = c(i[f"L3_conv_{n}"].reshape(P, 1))
    return o


def kernel(**inputs):
    import concourse.bacc as _bacc
    from concourse.bass_utils import run_bass_kernel_spmd as _run

    nc = _bacc.Bacc("TRN2", target_bir_lowering=False, num_devices=1, dynamic_dma_scratch_size=4096)
    arrays = lay_out({k: np.asarray(v) for k, v in inputs.items()})
    d = {k: nc.dram_tensor(f"in_{k}", a.shape, mybir.dt.from_np(a.dtype), kind="ExternalInput").ap()
         for k, a in arrays.items()}
    out = nc.dram_tensor("out_dram", (B, P, HW), F32, kind="ExternalOutput").ap()
    build_program(nc, d, out)
    r = _run(nc, [{f"in_{k}": a for k, a in arrays.items()}], core_ids=[0])
    return r.results[0]["out_dram"].reshape(B, P, H, W)
```
